# Optimizing a Trainium2 kernel written in Bass

```python
import numpy as np
import jax
import jax.numpy as jnp

def _softmax(x, axis=-1):
    return jax.nn.softmax(x, axis=axis)

def _gelu(x):
    return jax.nn.gelu(x, approximate=True)

def _silu(x):
    return jax.nn.silu(x)

def _sigmoid(x):
    return jax.nn.sigmoid(x)

def _layernorm(x, axis=-1, eps=1e-05):
    m = jnp.mean(x, axis=axis, keepdims=True)
    v = jnp.var(x, axis=axis, keepdims=True)
    return (x - m) / jnp.sqrt(v + eps)

def _scatter_add(tgt, idx, src, axis=0):
    return tgt.at[idx].add(src)

def _segment_sum(src, seg, n):
    return jax.ops.segment_sum(src, seg, n)
kernel_name = 'mk_gnn_ffn_d2_gnn_r32_59a282'

def setup_inputs(seed: int=0):
    np.random.seed(seed)
    _w = jnp.asarray

    def _rec_inputs():
        import jax
        import jax.numpy as jnp
        _gk = jax.random.key(seed)
        x = -0.0003713 + 1 * jax.random.normal(jax.random.fold_in(_gk, 1), (3125, 256), jnp.float32)
        _s = jax.random.randint(jax.random.fold_in(_gk, 2), (25000,), 0, 3125, jnp.int32)
        _d = jax.random.randint(jax.random.fold_in(_gk, 3), (25000,), 0, 3125, jnp.int32)
        _loop = jnp.arange(3125, dtype=jnp.int32)
        src = jnp.concatenate([_s, _d, _loop])
        dst = jnp.concatenate([_d, _s, _loop])
        _o = jnp.argsort(dst, stable=True)
        src = src[_o]
        dst = dst[_o]
        return (x, src, dst)
    x, src, dst = _rec_inputs()

    def _L0_gnn_setup():
        import jax, jax.numpy as jnp
        import numpy as np
        N_NODES = 50000
        N_EDGES = 25000
        DIM = 256
        HEADS = 8
        DIM_OUT = 32
        key = jax.random.key(seed)
        ks = jax.random.split(key, 9)
        s = 1.0 / np.sqrt(DIM)
        inner = HEADS * DIM_OUT
        return {'x': jax.random.normal(ks[0], (N_NODES, DIM), dtype=jnp.float32), 'Wq': jax.random.uniform(ks[1], (DIM, inner), jnp.float32, -s, s), 'bq': jax.random.uniform(ks[2], (inner,), jnp.float32, -s, s), 'Wk': jax.random.uniform(ks[3], (DIM, inner), jnp.float32, -s, s), 'bk': jax.random.uniform(ks[4], (inner,), jnp.float32, -s, s), 'Wv': jax.random.uniform(ks[5], (DIM, inner), jnp.float32, -s, s), 'bv': jax.random.uniform(ks[6], (inner,), jnp.float32, -s, s), 'src': jax.random.randint(ks[7], (N_EDGES,), 0, N_NODES), 'dst': jax.random.randint(ks[8], (N_EDGES,), 0, N_NODES)}
    _L0_gnn_all = _L0_gnn_setup()
    _L0_gnn_in = {k: v for k, v in _L0_gnn_all.items() if k in ('Wq', 'bq', 'Wk', 'bk', 'Wv', 'bv')}
    del _L0_gnn_all

    def _L0_ffn_setup():
        import jax, jax.numpy as jnp
        import numpy as np
        DIM = 256
        H = 8
        D = 64
        G = 64
        INNER = H * D
        SCALE = D ** (-0.5)
        key = jax.random.key(seed)
        ks = jax.random.split(key, 12)
        B, N = (4, 512)
        x = jax.random.normal(ks[0], (B, N, DIM), dtype=jnp.float32)
        s = lambda fan_in: 1.0 / np.sqrt(fan_in)
        W_fx = jax.random.normal(ks[1], (DIM, INNER), dtype=jnp.float32) * s(DIM)
        b_fx = jnp.zeros((INNER,), dtype=jnp.float32)
        W_x = jax.random.normal(ks[2], (DIM, INNER), dtype=jnp.float32) * s(DIM)
        b_x = jnp.zeros((INNER,), dtype=jnp.float32)
        A = jax.random.normal(ks[3], (G, D), dtype=jnp.float32)
        Q, _ = jnp.linalg.qr(A.T)
        W_slice = Q[:, :G].astype(jnp.float32)
        b_slice = jnp.zeros((G,), dtype=jnp.float32)
        W_q = jax.random.normal(ks[4], (D, D), dtype=jnp.float32) * s(D)
        W_k = jax.random.normal(ks[5], (D, D), dtype=jnp.float32) * s(D)
        W_v = jax.random.normal(ks[6], (D, D), dtype=jnp.float32) * s(D)
        W_out = jax.random.normal(ks[7], (INNER, DIM), dtype=jnp.float32) * s(INNER)
        b_out = jnp.zeros((DIM,), dtype=jnp.float32)
        temperature = jnp.ones((1, H, 1, 1), dtype=jnp.float32) * 0.5
        return {'x': x, 'W_fx': W_fx, 'b_fx': b_fx, 'W_x': W_x, 'b_x': b_x, 'W_slice': W_slice, 'b_slice': b_slice, 'W_q': W_q, 'W_k': W_k, 'W_v': W_v, 'W_out': W_out, 'b_out': b_out, 'temperature': temperature}
    _L0_ffn_all = _L0_ffn_setup()
    _L0_ffn_in = {k: v for k, v in _L0_ffn_all.items() if k in ('W_fx', 'b_fx', 'W_x', 'b_x', 'W_slice', 'b_slice', 'W_q', 'W_k', 'W_v', 'W_out', 'b_out', 'temperature')}
    del _L0_ffn_all

    def _L1_gnn_setup():
        import jax, jax.numpy as jnp
        import numpy as np
        N, E, D, H, DK, DV, L, HUS = (625, 10000, 256, 8, 32, 32, 2, 1024)

        def _layer_norm(x, g, b, eps=1e-05):
            mu = jnp.mean(x, axis=-1, keepdims=True)
            var = jnp.mean((x - mu) ** 2, axis=-1, keepdims=True)
            return (x - mu) * jax.lax.rsqrt(var + eps) * g + b

        def _ga_layer(h, src, dst, Wq, Wk, Wv, Wo, g, b):
            n = h.shape[0]
            q = (h @ Wq).reshape(n, H, DK)
            k = (h @ Wk).reshape(n, H, DK)
            v = (h @ Wv).reshape(n, H, DV)
            e = jnp.sum(q[dst] * k[src], axis=-1) / np.sqrt(DK).astype(np.float32)
            m = jax.ops.segment_max(e, dst, num_segments=n)
            a = jnp.exp(e - m[dst])
            z = jax.ops.segment_sum(a, dst, num_segments=n)
            alpha = a / (z[dst] + 1e-09)
            msg = v[src] * alpha[:, :, None]
            agg = jax.ops.segment_sum(msg, dst, num_segments=n).reshape(n, H * DV)
            out = agg @ Wo
            return _layer_norm(out + h, g, b)
        key = jax.random.key(seed)
        ks = jax.random.split(key, 12)
        s = 0.02
        return {'h': jax.random.normal(ks[0], (N, D), jnp.float32), 'src': jax.random.randint(ks[1], (E,), 0, N, jnp.int32), 'dst': jax.random.randint(ks[2], (E,), 0, N, jnp.int32), 'Wq': jax.random.normal(ks[3], (L, D, H * DK), jnp.float32) * s, 'Wk': jax.random.normal(ks[4], (L, D, H * DK), jnp.float32) * s, 'Wv': jax.random.normal(ks[5], (L, D, H * DV), jnp.float32) * s, 'Wo': jax.random.normal(ks[6], (L, H * DV, D), jnp.float32) * s, 'ln_g': jnp.ones((L, D), jnp.float32), 'ln_b': jnp.zeros((L, D), jnp.float32), 'w1': jax.random.normal(ks[7], (D, HUS), jnp.float32) * s, 'b1': jnp.zeros((HUS,), jnp.float32), 'w2': jax.random.normal(ks[8], (HUS, D), jnp.float32) * s, 'b2': jnp.zeros((D,), jnp.float32)}
    _L1_gnn_all = _L1_gnn_setup()
    _L1_gnn_in = {k: v for k, v in _L1_gnn_all.items() if k in ('Wq', 'Wk', 'Wv', 'Wo', 'ln_g', 'ln_b', 'w1', 'b1', 'w2', 'b2')}
    del _L1_gnn_all

    def _L1_ffn_setup():
        import jax, jax.numpy as jnp
        import numpy as np
        B, N, D = (16, 128, 256)
        NUM_EXPERTS, TOP_K, HEADS = (4, 2, 4)
        N_EDGES = 32768
        LN_EPS = 1e-05

        def _layernorm(x, g, b):
            mu = x.mean(-1, keepdims=True)
            var = ((x - mu) ** 2).mean(-1, keepdims=True)
            return (x - mu) * jax.lax.rsqrt(var + LN_EPS) * g + b

        def _forward(x, edge_index, W_gat, att_src, att_dst, b_gat, ln_gamma, ln_beta, W1, b1, W2, b2):
            Bc, Nc, Dc = x.shape
            M = Bc * Nc
            x_flat = x.reshape(M, Dc)
            h = (x_flat @ W_gat).reshape(M, HEADS, NUM_EXPERTS)
            loops = jnp.arange(M, dtype=edge_index.dtype)
            src = jnp.concatenate([edge_index[0], loops])
            dst = jnp.concatenate([edge_index[1], loops])
            a_src = (h * att_src).sum(-1)
            a_dst = (h * att_dst).sum(-1)
            e = jax.nn.leaky_relu(a_src[src] + a_dst[dst], negative_slope=0.2)
            e_max = jax.ops.segment_max(e, dst, num_segments=M)
            ee = jnp.exp(e - e_max[dst])
            denom = jax.ops.segment_sum(ee, dst, num_segments=M)
            alpha = ee / (denom[dst] + 1e-16)
            msg = h[src] * alpha[:, :, None]
            agg = jax.ops.segment_sum(msg, dst, num_segments=M).reshape(M, HEADS * NUM_EXPERTS) + b_gat
            scores = _layernorm(agg, ln_gamma, ln_beta).reshape(M, HEADS, NUM_EXPERTS).mean(1)
            scores = scores.reshape(Bc, Nc, NUM_EXPERTS)
            topk_s, topk_i = jax.lax.top_k(scores, TOP_K)
            w = jax.nn.softmax(topk_s, axis=-1)
            out = jnp.zeros_like(x)
            for ei in range(NUM_EXPERTS):
                g = jnp.where(topk_i == ei, w, 0.0).sum(-1)
                hh = jax.nn.gelu(x @ W1[ei] + b1[ei], approximate=False)
                out = out + g[..., None] * (hh @ W2[ei] + b2[ei])
            return out
        key = jax.random.key(seed)
        ks = jax.random.split(key, 8)
        s = 0.05
        return {'x': jax.random.normal(ks[0], (B, N, D), jnp.float32), 'W_gat': jax.random.normal(ks[1], (D, HEADS * NUM_EXPERTS), jnp.float32) * s, 'att_src': jax.random.normal(ks[2], (HEADS, NUM_EXPERTS), jnp.float32) * s, 'att_dst': jax.random.normal(ks[3], (HEADS, NUM_EXPERTS), jnp.float32) * s, 'b_gat': jnp.zeros((HEADS * NUM_EXPERTS,), jnp.float32), 'ln_gamma': jnp.ones((HEADS * NUM_EXPERTS,), jnp.float32), 'ln_beta': jnp.zeros((HEADS * NUM_EXPERTS,), jnp.float32), 'W1': jax.random.normal(ks[4], (NUM_EXPERTS, D, 2 * D), jnp.float32) * s, 'b1': jnp.zeros((NUM_EXPERTS, 2 * D), jnp.float32), 'W2': jax.random.normal(ks[5], (NUM_EXPERTS, 2 * D, D), jnp.float32) * s, 'b2': jnp.zeros((NUM_EXPERTS, D), jnp.float32), 'edge_index': jax.random.randint(ks[6], (2, N_EDGES), 0, B * N, jnp.int32)}
    _L1_ffn_all = _L1_ffn_setup()
    _L1_ffn_in = {k: v for k, v in _L1_ffn_all.items() if k in ('W_gat', 'att_src', 'att_dst', 'b_gat', 'ln_gamma', 'ln_beta', 'W1', 'b1', 'W2', 'b2', 'edge_index')}
    del _L1_ffn_all
    return {'x': x, 'src': src, 'dst': dst, 'L0_gnn_Wq': _L0_gnn_in['Wq'], 'L0_gnn_bq': _L0_gnn_in['bq'], 'L0_gnn_Wk': _L0_gnn_in['Wk'], 'L0_gnn_bk': _L0_gnn_in['bk'], 'L0_gnn_Wv': _L0_gnn_in['Wv'], 'L0_gnn_bv': _L0_gnn_in['bv'], 'L0_ffn_W_fx': _L0_ffn_in['W_fx'], 'L0_ffn_b_fx': _L0_ffn_in['b_fx'], 'L0_ffn_W_x': _L0_ffn_in['W_x'], 'L0_ffn_b_x': _L0_ffn_in['b_x'], 'L0_ffn_W_slice': _L0_ffn_in['W_slice'], 'L0_ffn_b_slice': _L0_ffn_in['b_slice'], 'L0_ffn_W_q': _L0_ffn_in['W_q'], 'L0_ffn_W_k': _L0_ffn_in['W_k'], 'L0_ffn_W_v': _L0_ffn_in['W_v'], 'L0_ffn_W_out': _L0_ffn_in['W_out'], 'L0_ffn_b_out': _L0_ffn_in['b_out'], 'L0_ffn_temperature': _L0_ffn_in['temperature'], 'L1_gnn_Wq': _L1_gnn_in['Wq'], 'L1_gnn_Wk': _L1_gnn_in['Wk'], 'L1_gnn_Wv': _L1_gnn_in['Wv'], 'L1_gnn_Wo': _L1_gnn_in['Wo'], 'L1_gnn_ln_g': _L1_gnn_in['ln_g'], 'L1_gnn_ln_b': _L1_gnn_in['ln_b'], 'L1_gnn_w1': _L1_gnn_in['w1'], 'L1_gnn_b1': _L1_gnn_in['b1'], 'L1_gnn_w2': _L1_gnn_in['w2'], 'L1_gnn_b2': _L1_gnn_in['b2'], 'L1_ffn_W_gat': _L1_ffn_in['W_gat'], 'L1_ffn_att_src': _L1_ffn_in['att_src'], 'L1_ffn_att_dst': _L1_ffn_in['att_dst'], 'L1_ffn_b_gat': _L1_ffn_in['b_gat'], 'L1_ffn_ln_gamma': _L1_ffn_in['ln_gamma'], 'L1_ffn_ln_beta': _L1_ffn_in['ln_beta'], 'L1_ffn_W1': _L1_ffn_in['W1'], 'L1_ffn_b1': _L1_ffn_in['b1'], 'L1_ffn_W2': _L1_ffn_in['W2'], 'L1_ffn_b2': _L1_ffn_in['b2'], 'L1_ffn_edge_index': _L1_ffn_in['edge_index']}

def reference(x, src, dst, L0_gnn_Wq, L0_gnn_bq, L0_gnn_Wk, L0_gnn_bk, L0_gnn_Wv, L0_gnn_bv, L0_ffn_W_fx, L0_ffn_b_fx, L0_ffn_W_x, L0_ffn_b_x, L0_ffn_W_slice, L0_ffn_b_slice, L0_ffn_W_q, L0_ffn_W_k, L0_ffn_W_v, L0_ffn_W_out, L0_ffn_b_out, L0_ffn_temperature, L1_gnn_Wq, L1_gnn_Wk, L1_gnn_Wv, L1_gnn_Wo, L1_gnn_ln_g, L1_gnn_ln_b, L1_gnn_w1, L1_gnn_b1, L1_gnn_w2, L1_gnn_b2, L1_ffn_W_gat, L1_ffn_att_src, L1_ffn_att_dst, L1_ffn_b_gat, L1_ffn_ln_gamma, L1_ffn_ln_beta, L1_ffn_W1, L1_ffn_b1, L1_ffn_W2, L1_ffn_b2, L1_ffn_edge_index):
    import jax
    import jax.numpy as jnp

    def _L0_gnn_ref(x, Wq, bq, Wk, bk, Wv, bv, src, dst):
        import jax, jax.numpy as jnp
        import numpy as np
        N_NODES = 50000
        N_EDGES = 25000
        DIM = 256
        HEADS = 8
        DIM_OUT = 32
        n = x.shape[0]
        q = (x @ Wq + bq).reshape(n, HEADS, DIM_OUT)
        k = (x @ Wk + bk).reshape(n, HEADS, DIM_OUT)
        v = (x @ Wv + bv).reshape(n, HEADS, DIM_OUT)
        scores = jnp.einsum('ehd,ehd->eh', q[src], k[dst]) / jnp.sqrt(jnp.asarray(DIM_OUT, dtype=x.dtype))
        m = jax.ops.segment_max(scores, dst, num_segments=n)
        m = jnp.where(jnp.isfinite(m), m, 0.0)
        e = jnp.exp(scores - m[dst])
        z = jax.ops.segment_sum(e, dst, num_segments=n)
        p = e / jnp.maximum(z[dst], 1e-16)
        out = jax.ops.segment_sum(v[src] * p[:, :, None], dst, num_segments=n)
        return out.reshape(n, HEADS * DIM_OUT)

    def _L0_ffn_ref(x, W_fx, b_fx, W_x, b_x, W_slice, b_slice, W_q, W_k, W_v, W_out, b_out, temperature):
        import jax, jax.numpy as jnp
        import numpy as np
        DIM = 256
        H = 8
        D = 64
        G = 64
        INNER = H * D
        SCALE = D ** (-0.5)
        B, N, _ = x.shape
        fx_mid = (x @ W_fx + b_fx).reshape(B, N, H, D).transpose(0, 2, 1, 3)
        x_mid = (x @ W_x + b_x).reshape(B, N, H, D).transpose(0, 2, 1, 3)
        temp = jnp.clip(temperature, 0.1, 5.0)
        slice_weights = jax.nn.softmax((x_mid @ W_slice + b_slice) / temp, axis=-1)
        slice_norm = slice_weights.sum(axis=2)
        slice_token = jnp.einsum('bhnc,bhng->bhgc', fx_mid, slice_weights)
        slice_token = slice_token / (slice_norm[..., None] + 1e-05)
        q = slice_token @ W_q
        k = slice_token @ W_k
        v = slice_token @ W_v
        attn = jax.nn.softmax(jnp.einsum('bhgc,bhkc->bhgk', q, k) * SCALE, axis=-1)
        out_slice = jnp.einsum('bhgk,bhkc->bhgc', attn, v)
        out_x = jnp.einsum('bhgc,bhng->bhnc', out_slice, slice_weights)
        out_x = out_x.transpose(0, 2, 1, 3).reshape(B, N, INNER)
        return out_x @ W_out + b_out

    def _L1_gnn_ref(h, src, dst, Wq, Wk, Wv, Wo, ln_g, ln_b, w1, b1, w2, b2):
        import jax, jax.numpy as jnp
        import numpy as np
        N, E, D, H, DK, DV, L, HUS = (625, 10000, 256, 8, 32, 32, 2, 1024)

        def _layer_norm(x, g, b, eps=1e-05):
            mu = jnp.mean(x, axis=-1, keepdims=True)
            var = jnp.mean((x - mu) ** 2, axis=-1, keepdims=True)
            return (x - mu) * jax.lax.rsqrt(var + eps) * g + b

        def _ga_layer(h, src, dst, Wq, Wk, Wv, Wo, g, b):
            n = h.shape[0]
            q = (h @ Wq).reshape(n, H, DK)
            k = (h @ Wk).reshape(n, H, DK)
            v = (h @ Wv).reshape(n, H, DV)
            e = jnp.sum(q[dst] * k[src], axis=-1) / np.sqrt(DK).astype(np.float32)
            m = jax.ops.segment_max(e, dst, num_segments=n)
            a = jnp.exp(e - m[dst])
            z = jax.ops.segment_sum(a, dst, num_segments=n)
            alpha = a / (z[dst] + 1e-09)
            msg = v[src] * alpha[:, :, None]
            agg = jax.ops.segment_sum(msg, dst, num_segments=n).reshape(n, H * DV)
            out = agg @ Wo
            return _layer_norm(out + h, g, b)
        for l in range(Wq.shape[0]):
            h = _ga_layer(h, src, dst, Wq[l], Wk[l], Wv[l], Wo[l], ln_g[l], ln_b[l])
        return jax.nn.relu(h @ w1 + b1) @ w2 + b2

    def _L1_ffn_ref(x, W_gat, att_src, att_dst, b_gat, ln_gamma, ln_beta, W1, b1, W2, b2, edge_index):
        import jax, jax.numpy as jnp
        import numpy as np
        B, N, D = (16, 128, 256)
        NUM_EXPERTS, TOP_K, HEADS = (4, 2, 4)
        N_EDGES = 32768
        LN_EPS = 1e-05

        def _layernorm(x, g, b):
            mu = x.mean(-1, keepdims=True)
            var = ((x - mu) ** 2).mean(-1, keepdims=True)
            return (x - mu) * jax.lax.rsqrt(var + LN_EPS) * g + b

        def _forward(x, edge_index, W_gat, att_src, att_dst, b_gat, ln_gamma, ln_beta, W1, b1, W2, b2):
            Bc, Nc, Dc = x.shape
            M = Bc * Nc
            x_flat = x.reshape(M, Dc)
            h = (x_flat @ W_gat).reshape(M, HEADS, NUM_EXPERTS)
            loops = jnp.arange(M, dtype=edge_index.dtype)
            src = jnp.concatenate([edge_index[0], loops])
            dst = jnp.concatenate([edge_index[1], loops])
            a_src = (h * att_src).sum(-1)
            a_dst = (h * att_dst).sum(-1)
            e = jax.nn.leaky_relu(a_src[src] + a_dst[dst], negative_slope=0.2)
            e_max = jax.ops.segment_max(e, dst, num_segments=M)
            ee = jnp.exp(e - e_max[dst])
            denom = jax.ops.segment_sum(ee, dst, num_segments=M)
            alpha = ee / (denom[dst] + 1e-16)
            msg = h[src] * alpha[:, :, None]
            agg = jax.ops.segment_sum(msg, dst, num_segments=M).reshape(M, HEADS * NUM_EXPERTS) + b_gat
            scores = _layernorm(agg, ln_gamma, ln_beta).reshape(M, HEADS, NUM_EXPERTS).mean(1)
            scores = scores.reshape(Bc, Nc, NUM_EXPERTS)
            topk_s, topk_i = jax.lax.top_k(scores, TOP_K)
            w = jax.nn.softmax(topk_s, axis=-1)
            out = jnp.zeros_like(x)
            for ei in range(NUM_EXPERTS):
                g = jnp.where(topk_i == ei, w, 0.0).sum(-1)
                hh = jax.nn.gelu(x @ W1[ei] + b1[ei], approximate=False)
                out = out + g[..., None] * (hh @ W2[ei] + b2[ei])
            return out
        return _forward(x, edge_index, W_gat, att_src, att_dst, b_gat, ln_gamma, ln_beta, W1, b1, W2, b2)
    x = x + _L0_gnn_ref(_layernorm(x, axis=-1), L0_gnn_Wq, L0_gnn_bq, L0_gnn_Wk, L0_gnn_bk, L0_gnn_Wv, L0_gnn_bv, src, dst)
    x = x + _L0_ffn_ref(_layernorm(x, axis=-1)[None], L0_ffn_W_fx, L0_ffn_b_fx, L0_ffn_W_x, L0_ffn_b_x, L0_ffn_W_slice, L0_ffn_b_slice, L0_ffn_W_q, L0_ffn_W_k, L0_ffn_W_v, L0_ffn_W_out, L0_ffn_b_out, L0_ffn_temperature)[0]
    x = x + _L1_gnn_ref(_layernorm(x, axis=-1), src, dst, L1_gnn_Wq, L1_gnn_Wk, L1_gnn_Wv, L1_gnn_Wo, L1_gnn_ln_g, L1_gnn_ln_b, L1_gnn_w1, L1_gnn_b1, L1_gnn_w2, L1_gnn_b2)
    x = x + _L1_ffn_ref(_layernorm(x, axis=-1)[None], L1_ffn_W_gat, L1_ffn_att_src, L1_ffn_att_dst, L1_ffn_b_gat, L1_ffn_ln_gamma, L1_ffn_ln_beta, L1_ffn_W1, L1_ffn_b1, L1_ffn_W2, L1_ffn_b2, L1_ffn_edge_index)[0]
    return x

_drawn_inputs = setup_inputs


def setup_inputs(seed=0):
    import zlib

    import numpy as np

    out = dict(_drawn_inputs(seed))
    spreads = {'L0_ffn_b_fx': (0.0, 0.1),
     'L0_ffn_b_x': (0.0, 0.429),
     'L0_ffn_b_slice': (0.0, 0.351),
     'L0_ffn_b_out': (0.0, 0.1),
     'L0_ffn_temperature': (0.5, 0.6),
     'L1_gnn_ln_g': (1.0, 0.2),
     'L1_gnn_ln_b': (0.0, 0.1),
     'L1_gnn_b1': (0.0, 0.1),
     'L1_gnn_b2': (0.0, 0.1),
     'L1_ffn_b_gat': (0.0, 0.1),
     'L1_ffn_ln_gamma': (1.0, 0.2),
     'L1_ffn_ln_beta': (0.0, 0.1),
     'L1_ffn_b1': (0.0, 0.1),
     'L1_ffn_b2': (0.0, 0.1)}
    factors = {'L0_gnn_bq': 8.0,
     'L0_gnn_bk': 5.461,
     'L0_ffn_W_x': 2.966,
     'L0_ffn_W_q': 8.0,
     'L0_ffn_W_k': 8.0,
     'L1_gnn_Wq': 8.0,
     'L1_gnn_Wk': 8.0,
     'L1_gnn_Wo': 2.897}
    for name, (base, spread) in spreads.items():
        noise = np.random.default_rng([zlib.crc32(name.encode()), seed]).standard_normal(out[name].shape)
        drawn = base * np.exp(spread * noise) if base else spread * noise
        out[name] = jnp.asarray(drawn.astype(out[name].dtype))
    for name, factor in factors.items():
        out[name] = (out[name] * factor).astype(out[name].dtype)
    return out
```

```python
from contextlib import ExitStack

import numpy as np

import concourse.bass as bass
from concourse import mybir

F32 = mybir.dt.float32
F16 = mybir.dt.float16
I32 = mybir.dt.int32
ALU = mybir.AluOpType
ACT = mybir.ActivationFunctionType
AX = mybir.AxisListType

N = 3125
P = 125
T = N // P
D = 256
KD = D // 128
G = 5
GT = T // G
GN = GT * P
SPLIT = ((0, 3 * P), (3 * P, GN))
NN = N * N
CELLS = 128 * N * T
LOWER = 1024.0
FAR = 1e30
EMPTY = 1e20
LN_EPS = 1e-5

GROUPS = tuple(tuple(range(4 * j, min(4 * j + 4, T))) for j in range(7))
GROUP_COLS = tuple((4 * P * j, min(4 * P * (j + 1), N)) for j in range(7))
LAST = len(GROUPS) - 1
BIAS_COLS = ((0, 1000), (1000, 2000), (2000, 3000), (3000, N))
EXP_COLS = ((0, 1000), (1000, 2000), (2000, N))
EXP_NEED = {0: 0, 2: 1, 4: 2}
EXP_AT = (0, 2, 4)
ON_ACT = (0, 2, 4, 5, 6)
ON_DVE = (1, 3)


def run_block(nc, c, *phases):
    with nc.Block() as block:
        @block.sync
        def _(sp):
            for ph in phases:
                if "sync" in ph:
                    ph["sync"](sp)

        @block.scalar
        def _(act):
            for ph in phases:
                if "scalar" in ph:
                    ph["scalar"](act)

        @block.vector
        def _(dve):
            for ph in phases:
                if "vector" in ph:
                    ph["vector"](dve)

        @block.tensor
        def _(pe):
            for ph in phases:
                if "tensor" in ph:
                    ph["tensor"](pe)

        @block.gpsimd
        def _(pool):
            for ph in phases:
                if "gpsimd" in ph:
                    ph["gpsimd"](pool)
    c.clear()


def wait_from(eng, sem, value):
    if not (isinstance(value, int) and value <= 0):
        eng.wait_ge(sem, value)


def peeled(eng, n, body):
    body(0)
    with eng.Fori(1, n) as i:
        body(i)


def wait_apart(eng, sem, value, passed):
    eng.wait_ge(sem, value)
    eng.sem_inc(passed, 1)


class Chip:

    def __init__(self, nc, ctx):
        self.nc, self.ctx, self.sems = nc, ctx, []

    def sem(self, name):
        self.sems.append(self.nc.alloc_semaphore(name))
        return self.sems[-1]

    def clear(self):
        self.nc.clear_and_free_semaphores(self.sems)
        self.nc.all_engine_barrier()
        self.sems = []


def sb(nc, ctx, name, shape, dt=F32):
    return ctx.enter_context(nc.sbuf_tensor(name, shape, dt))


def ps(nc, ctx, name, shape):
    return ctx.enter_context(nc.psum_tensor(name, shape, F32))


def rows(ap, n):
    return ap.rearrange("(o n) -> o n", o=1).to_broadcast([n, ap.shape[0]])


def setup_phase(c, ident, ones, fold):
    zeroed, made = c.sem("zeroed"), c.sem("made")

    def gpsimd(pool):
        pool.memset(ident[:, :], 0.0).then_inc(zeroed, 1)
        pool.memset(fold[:, :], 0.0).then_inc(zeroed, 1)
        pool.memset(ones[:, :], 1.0).then_inc(zeroed, 1)
        pool.wait_ge(zeroed, 3)
        pool.affine_select(out=ident[:, :], in_=ident[:, :], compare_op=ALU.not_equal, fill=1.0, base=0,
                           pattern=[[-1, 128]], channel_multiplier=1).then_inc(made, 1)
        for q in range(4):
            pool.wait_ge(made, q + 1)
            pool.affine_select(out=fold[:, :], in_=fold[:, :], compare_op=ALU.not_equal, fill=1.0,
                               base=-32 * q, pattern=[[-1, 32]], channel_multiplier=1).then_inc(made, 1)

    return dict(gpsimd=gpsimd)


COLS = 6


def clear_phase(c, mats, zero, ident, diag_of):
    zset, looped = c.sem("zset"), c.sem("looped")
    cleared = [c.sem(f"cleared{i}") for i in range(len(mats))]

    def vector(dve):
        dve.memset(zero[:, :], 0.0).then_inc(zset, 1)

    def sync(sp):
        sp.wait_ge(zset, 1)
        for i, m in enumerate(mats):
            v = m.rearrange("(t p n) o -> t p (n o)", p=128, n=N)
            with sp.Fori(0, T) as t:
                sp.dma_start(v[t], zero[:, :]).then_inc(cleared[i], 16)
            if m is diag_of:
                sp.wait_ge(cleared[i], 16 * T)
                w = m[0:NN, :].rearrange("(r n) o -> r (n o)", n=N)
                for t in range(T):
                    sp.dma_start(w[t * P:(t + 1) * P, t * P:(t + 1) * P], ident[0:P, 0:P]).then_inc(looped, 16)
        sp.wait_ge(looped, 16 * T)

    return dict(vector=vector, sync=sync), cleared


def edges_phase(nc, c, ctx, tag, src, dst, lanes, cols, idx_all, val_all, ident, ones, psk):
    turns = -(-cols // COLS)
    wide = turns * COLS
    raw = sb(nc, ctx, f"raw{tag}", [lanes, 2, cols], I32)
    num = sb(nc, ctx, f"num{tag}", [lanes, 2, cols])
    key = sb(nc, ctx, f"key{tag}", [lanes, wide])
    weight = sb(nc, ctx, f"weight{tag}", [lanes, lanes])
    spare = sb(nc, ctx, f"spare{tag}", [lanes, 1])
    diag = sb(nc, ctx, f"diag{tag}", [lanes, COLS, lanes])
    junk = sb(nc, ctx, f"junk{tag}", [lanes, lanes])
    same = sb(nc, ctx, f"same{tag}", [lanes, COLS])
    lost = sb(nc, ctx, f"lost{tag}", [lanes, COLS])
    loaded, spared, weighed = c.sem(f"loaded{tag}"), c.sem(f"spared{tag}"), c.sem(f"weighed{tag}")
    keyed, diags, spread = c.sem(f"keyed{tag}"), c.sem(f"diags{tag}"), c.sem(f"spread{tag}")
    counted, chosen = c.sem(f"counted{tag}"), c.sem(f"chosen{tag}")
    half = COLS // 2

    def sync(sp):
        sp.dma_start(raw[:, 0, :], src.rearrange("(p c) -> p c", p=lanes)).then_inc(loaded, 16)
        sp.dma_start(raw[:, 1, :], dst.rearrange("(p c) -> p c", p=lanes)).then_inc(loaded, 16)

    def gpsimd(pool):
        pool.iota(spare[:, :], pattern=[[0, 1]], base=NN, channel_multiplier=1,
                  allow_small_or_imprecise_dtypes=True).then_inc(spared, 1)
        pool.memset(weight[:, :], 1.0).then_inc(spared, 1)
        pool.wait_ge(spared, 2)
        pool.affine_select(out=weight[:, :], in_=weight[:, :], compare_op=ALU.is_ge, fill=1.0 + LOWER, base=0,
                           pattern=[[1, lanes]], channel_multiplier=-1).then_inc(weighed, 1)

    def vector(dve):
        dve.wait_ge(loaded, 32)
        dve.wait_ge(weighed, 1)
        dve.tensor_copy(num[:, :, :], raw[:, :, :]).then_inc(keyed, 1)
        dve.wait_ge(keyed, 1)
        dve.scalar_tensor_tensor(out=key[:, 0:cols], in0=num[:, 1, :], scalar=float(N), in1=num[:, 0, :],
                                 op0=ALU.mult, op1=ALU.add).then_inc(keyed, 1)
        if wide > cols:
            dve.tensor_scalar(key[:, cols:wide], spare[:, 0:1].to_broadcast([lanes, wide - cols]), 0.0, None,
                              ALU.add).then_inc(keyed, 1)
        dve.wait_ge(keyed, 2 + (wide > cols))
        def turn(i):
            for u in range(COLS):
                if u % half == 0:
                    wait_from(dve, spread, 2 * i)
                dve.tensor_scalar(diag[:, u, :], ident[0:lanes, 0:lanes], key[:, bass.ds(i * COLS + u, 1)], None,
                                  ALU.mult).then_inc(diags, 1)
            for u in range(COLS):
                if u % half == 0:
                    dve.wait_ge(spread, 2 * i + u // half + 1)
                dve.scalar_tensor_tensor(out=junk[:, :], in0=psk[u // half][0:lanes, (u % half) * lanes:(u % half + 1) * lanes],
                                         scalar=key[:, bass.ds(i * COLS + u, 1)], in1=weight[:, :],
                                         op0=ALU.is_equal, op1=ALU.mult, accum_out=same[:, u:u + 1]).then_inc(counted, 1)
                dve.wait_ge(counted, COLS * i + u + 1)
            dve.tensor_scalar(lost[:, :], same[:, :], LOWER, spare[:, 0:1], ALU.is_ge, ALU.mult).then_inc(chosen, 1)
            dve.tensor_copy(val_all[0:lanes, bass.ds(i * COLS, COLS)], same[:, :]).then_inc(chosen, 1)
            dve.wait_ge(chosen, 3 * i + 2)
            dve.tensor_tensor(idx_all[0:lanes, bass.ds(i * COLS, COLS)], lost[:, :],
                              key[:, bass.ds(i * COLS, COLS)], ALU.max).then_inc(chosen, 1)
            dve.wait_ge(chosen, 3 * i + 3)

        peeled(dve, turns, turn)
    def tensor(pe):
        def turn(i):
            for b in range(2):
                pe.wait_ge(diags, COLS * i + (b + 1) * half)
                if b == 0:
                    wait_from(pe, counted, COLS * i)
                pe.matmul(psk[b][0:lanes, 0:half * lanes], ones[0:lanes, 0:lanes],
                          diag[:, b * half:(b + 1) * half, :].rearrange("p u n -> p (u n)"),
                          start=True, stop=True).then_inc(spread, 1)

        peeled(pe, turns, turn)
    return dict(sync=sync, gpsimd=gpsimd, vector=vector, tensor=tensor), chosen


def scatter_phase(nc, c, ctx, tag, mats, lanes, cols, idx_all, val_all, cleared, chosen):
    turns = -(-cols // COLS)
    slot_idx = sb(nc, ctx, f"slot_idx{tag}", [lanes, COLS], I32)
    slot_val = sb(nc, ctx, f"slot_val{tag}", [lanes, COLS])
    staged, passed = c.sem(f"staged{tag}"), c.sem(f"passed{tag}")
    landed = [c.sem(f"landed{tag}{m}") for m in range(len(mats))]
    M = len(mats)

    def gpsimd(pool):
        for clear in cleared:
            pool.wait_ge(clear, 16 * T)
        def turn(i):
            for u in range(COLS):
                if chosen is not None and u == 0:
                    pool.wait_ge(chosen, 3 * i + 3)
                pool.tensor_copy(slot_idx[:, u:u + 1], idx_all[0:lanes, bass.ds(i * COLS + u, 1)]).then_inc(staged, 1)
                pool.tensor_copy(slot_val[:, u:u + 1], val_all[0:lanes, bass.ds(i * COLS + u, 1)]).then_inc(staged, 1)
                wait_from(pool, landed[u % M], 16 * (COLS // M * i + u // M))
                wait_apart(pool, staged, 2 * COLS * i + 2 * (u + 1), passed)
                pool.indirect_dma_start(mats[u % M], bass.IndirectOffsetOnAxis(ap=slot_idx[:, u:u + 1], axis=0),
                                        slot_val[:, u:u + 1], None, compute_op=ALU.add).then_inc(landed[u % M], 16)

        peeled(pool, turns, turn)
        for m in range(M):
            pool.wait_ge(landed[m], 16 * turns * COLS // M)

    return dict(gpsimd=gpsimd)


def bias_phase(nc, c, ctx, tag, mats, out):
    M = len(mats)
    cnt = sb(nc, ctx, f"cnt{tag}", [P, 2, M, N])
    none = sb(nc, ctx, f"none{tag}", [P, 2, N])
    loaded = [c.sem(f"cnt_in{tag}{b}") for b in range(2)]
    summed, fixed, logged, biased = (c.sem(f"{x}{tag}") for x in ("summed", "fixed", "logged", "biased"))
    stored = [c.sem(f"stored{tag}{b}") for b in range(2)]
    view = [m[0:NN, :].rearrange("(t p n) o -> t p (n o)", p=P, n=N) for m in mats]
    outv = out[0:NN, :].rearrange("(t p n) o -> t p (n o)", p=P, n=N)

    def sync(sp):
        for t in range(T):
            if t >= 2:
                sp.wait_ge(stored[t % 2], 16 * (t // 2))
            for m in range(M):
                sp.dma_start(cnt[:, t % 2, m, :], view[m][t]).then_inc(loaded[t % 2], 16)
            if t >= 1:
                sp.wait_ge(biased, t)
                sp.dma_start(outv[t - 1], none[:, (t - 1) % 2, :]).then_inc(stored[(t - 1) % 2], 16)
        sp.wait_ge(biased, T)
        sp.dma_start(outv[T - 1], none[:, (T - 1) % 2, :]).then_inc(stored[(T - 1) % 2], 16)
        for b in range(2):
            sp.wait_ge(stored[b], 16 * ((T - b + 1) // 2))

    def gpsimd(pool):
        if M == 2:
            for t in range(T):
                b = t % 2
                pool.wait_ge(loaded[b], 32 * (t // 2 + 1))
                pool.tensor_tensor(cnt[:, b, 0, :], cnt[:, b, 0, :], cnt[:, b, 1, :], ALU.add).then_inc(summed, 1)

    def vector(dve):
        def flags(t):
            b = t % 2
            if M == 2:
                dve.wait_ge(summed, t + 1)
            else:
                dve.wait_ge(loaded[b], 16 * (t // 2 + 1))
            if t >= 2:
                dve.wait_ge(stored[t % 2], 16 * (t // 2))
            dve.tensor_scalar(none[:, b, :], cnt[:, b, 0, :], 0.5, FAR, ALU.is_lt, ALU.mult).then_inc(fixed, 1)
            dve.tensor_scalar(cnt[:, b, 0, :], cnt[:, b, 0, :], 1.0, None, ALU.max).then_inc(fixed, 1)

        flags(0)
        for t in range(T):
            if t + 1 < T:
                flags(t + 1)
            dve.wait_ge(logged, t + 1)
            dve.tensor_tensor(none[:, t % 2, :], none[:, t % 2, :], cnt[:, t % 2, 0, :], ALU.subtract).then_inc(biased, 1)

    def scalar(act):
        for t in range(T):
            act.wait_ge(fixed, 2 * (t + 1))
            act.activation(cnt[:, t % 2, 0, :], cnt[:, t % 2, 0, :], ACT.Ln).then_inc(logged, 1)

    return dict(sync=sync, gpsimd=gpsimd, vector=vector, scalar=scalar)


def norm_phase(nc, c, ctx, tag, x, h, scratch, gamma=None, beta=None):
    st = sb(nc, ctx, f"stats{tag}", [P, 3, T])
    gb = sb(nc, ctx, f"gb{tag}", [P, 2, D]) if gamma is not None else None
    done, sq, root, gin = (c.sem(f"{v}{tag}") for v in ("ln", "ln_sq", "ln_root", "ln_gb"))

    def wide(ap):
        return ap.unsqueeze(2).to_broadcast([P, T, D])

    def sync(sp):
        if gamma is not None:
            sp.dma_start(gb[:, 0, :], rows(gamma, P)).then_inc(gin, 16)
            sp.dma_start(gb[:, 1, :], rows(beta, P)).then_inc(gin, 16)

    def vector(dve):
        dve.tensor_reduce(st[:, 0, :], x[:, :, :], AX.X, ALU.add).then_inc(done, 1)
        dve.wait_ge(done, 1)
        dve.tensor_scalar(st[:, 1, :], st[:, 0, :], 1.0 / D, None, ALU.mult).then_inc(done, 1)
        dve.wait_ge(done, 2)
        dve.tensor_tensor(h[:, :, :], x[:, :, :], wide(st[:, 1, :]), ALU.subtract).then_inc(done, 1)
        dve.wait_ge(sq, 1)
        dve.tensor_reduce(st[:, 0, :], scratch[:, :, :], AX.X, ALU.add).then_inc(done, 1)
        dve.wait_ge(done, 4)
        dve.tensor_scalar(st[:, 2, :], st[:, 0, :], 1.0 / D, LN_EPS, ALU.mult, ALU.add).then_inc(done, 1)
        dve.wait_ge(root, 1)
        dve.reciprocal(st[:, 2, :], st[:, 0, :]).then_inc(done, 1)
        dve.wait_ge(done, 6)
        dve.tensor_tensor(h[:, :, :], h[:, :, :], wide(st[:, 2, :]), ALU.mult).then_inc(done, 1)
        if gamma is not None:
            dve.wait_ge(gin, 32)
            for k, op in ((0, ALU.mult), (1, ALU.add)):
                dve.wait_ge(done, 7 + k)
                dve.tensor_tensor(h[:, :, :], h[:, :, :], gb[:, k, :].unsqueeze(1).to_broadcast([P, T, D]),
                                  op).then_inc(done, 1)
            dve.wait_ge(done, 9)
        else:
            dve.wait_ge(done, 7)

    def scalar(act):
        act.wait_ge(done, 3)
        act.activation(scratch[:, :, :], h[:, :, :], ACT.Square).then_inc(sq, 1)
        act.wait_ge(done, 5)
        act.activation(st[:, 0, :], st[:, 2, :], ACT.Sqrt).then_inc(root, 1)

    return dict(sync=sync, vector=vector, scalar=scalar)


def transpose_group(pe, hs, bank, ident, ready, free, turned):
    for k in range(KD):
        for s, (lo, hi) in enumerate(SPLIT):
            for j in range(lo // P, hi // P):
                mm = pe.transpose(bank[2 * k + s][:, j * P - lo:(j + 1) * P - lo], hs[0:P, j, k * 128:(k + 1) * 128],
                                  ident[0:P, 0:P])
            mm.then_inc(turned, 1)


def project_phase(nc, c, ctx, tag, h, w_dst, w_src, w_val, biases, scale, feat, v, ident, bank):
    w = sb(nc, ctx, f"w{tag}", [128, 3, KD, D])
    bcol = sb(nc, ctx, f"bcol{tag}", [128, 2, KD])
    brow = sb(nc, ctx, f"brow{tag}", [P, D])
    hs = sb(nc, ctx, f"hs{tag}", [P, GT, D])
    ht = sb(nc, ctx, f"ht{tag}", [128, KD, GN])
    full = sb(nc, ctx, f"full{tag}", [128, 2, GN])
    part = sb(nc, ctx, f"part{tag}", [128, 4, 2, GN], F16)
    (win, staged, turned, ht_ok, q_mm, v_mm, q_full, q_high, q_low, v_out, kept, bcol_ok) = (
        c.sem(f"{x}{tag}") for x in ("p_w", "p_stage", "p_turn", "p_ht", "p_q", "p_v", "p_full", "p_high", "p_low",
                                     "p_vout", "p_kept", "p_bcol"))
    nw = 3 + (3 if biases else 0)
    vbank = (0, 1, 2, 3, 0)

    def sync(sp):
        for i, wt in enumerate((w_dst, w_src, w_val)):
            sp.dma_start(w[:, i, :, :], wt.rearrange("(k p) n -> p k n", p=128)).then_inc(win, 16)
        if biases:
            for i in range(2):
                with nc.allow_non_contiguous_dma(reason="256 bias values, once"):
                    sp.dma_start(bcol[:, i, :], biases[i].rearrange("(k p) -> p k", p=128)).then_inc(win, 16)
            sp.dma_start(brow[:, :], rows(biases[2], P)).then_inc(win, 16)
        def group(g):
            for q in range(4):
                sp.wait_ge(q_low, 4 * g + q + 1)
                sp.wait_ge(q_high, 4 * g + q + 1)
                for hl in range(2):
                    sp.dma_start(feat[q // 2][hl][(q % 2) * 128:(q % 2 + 1) * 128, bass.ds(g * GN, GN)],
                                 part[:, q, hl, :]).then_inc(kept, 16)

        peeled(sp, G, group)
        sp.wait_ge(kept, 16 * 8 * G)

    def gpsimd(pool):
        def group(g):
            wait_from(pool, turned, 4 * g)
            for j in range(GT):
                pool.tensor_copy(hs[:, j, :], h[:, bass.ds(g * GT + j, 1), :].rearrange("p o n -> p (o n)")).then_inc(staged, 1)

        peeled(pool, G, group)
    def tensor(pe):
        pe.wait_ge(win, 16 * nw)
        def group(g):
            pe.wait_ge(staged, GT * (g + 1))
            wait_from(pe, v_out, GT * g)
            transpose_group(pe, hs, bank, ident, None, None, turned)
            pe.wait_ge(ht_ok, 4 * (g + 1))
            for q in range(4):
                for s, (lo, hi) in enumerate(SPLIT):
                    b = 4 + 2 * (q % 2) + s
                    if q >= 2:
                        wait_from(pe, q_full, 8 * g + 2 * (q - 2) + s + 1)
                    elif s == 0:
                        wait_from(pe, q_full, 8 * g)
                    for k in range(KD):
                        mm = pe.matmul(bank[b][:, 0:hi - lo], w[:, q // 2, k, (q % 2) * 128:(q % 2 + 1) * 128],
                                       ht[:, k, lo:hi], start=(k == 0), stop=(k == KD - 1))
                    mm.then_inc(q_mm, 1)
            for j in range(GT):
                if j == 4:
                    pe.wait_ge(v_out, GT * g + 1)
                for k in range(KD):
                    mm = pe.matmul(bank[vbank[j]][0:P, 0:D], ht[:, k, j * P:(j + 1) * P], w[:, 2, k, :],
                                   start=(k == 0), stop=(k == KD - 1))
                mm.then_inc(v_mm, 1)

        peeled(pe, G, group)
    def scalar(act):
        if biases:
            act.wait_ge(win, 16 * nw)
            act.mul(bcol[:, 0, :], bcol[:, 0, :], scale).then_inc(bcol_ok, 1)
            act.wait_ge(bcol_ok, 1)
        def group(g):
            wait_from(act, v_mm, GT * g)
            for k in range(KD):
                for s, (lo, hi) in enumerate(SPLIT):
                    act.wait_ge(turned, 4 * g + 2 * k + s + 1)
                    act.copy(ht[:, k, lo:hi], bank[2 * k + s][:, 0:hi - lo]).then_inc(ht_ok, 1)
            for q in range(4):
                for s, (lo, hi) in enumerate(SPLIT):
                    act.wait_ge(q_mm, 8 * g + 2 * q + s + 1)
                    if s == 0:
                        wait_from(act, q_low, (4 * g + q - 1) if q >= 1 else 4 * g)
                    src = bank[4 + 2 * (q % 2) + s][:, 0:hi - lo]
                    sc = scale if q < 2 else 1.0
                    act.activation(full[:, q % 2, lo:hi], src, ACT.Identity, scale=sc,
                                   bias=bcol[:, q // 2, q % 2:q % 2 + 1] if biases else 0.0).then_inc(q_full, 1)

        peeled(act, G, group)
    def vector(dve):
        if biases:
            dve.wait_ge(win, 16 * nw)
        def group(g):
            for q in range(4):
                dve.wait_ge(q_full, 8 * g + 2 * q + 2)
                if q == 0:
                    wait_from(dve, kept, 128 * g)
                dve.tensor_copy(part[:, q, 0, :], full[:, q % 2, :]).then_inc(q_high, 1)
                dve.wait_ge(q_high, 4 * g + q + 1)
                dve.tensor_tensor(part[:, q, 1, :], full[:, q % 2, :], part[:, q, 0, :], ALU.subtract).then_inc(q_low, 1)
            for j in range(GT):
                dve.wait_ge(v_mm, GT * g + j + 1)
                out = v[0:P, bass.ds(g * GT + j, 1), :].rearrange("p o n -> p (o n)")
                if biases:
                    dve.tensor_tensor(out, bank[vbank[j]][0:P, 0:D], brow[:, :], ALU.add).then_inc(v_out, 1)
                else:
                    dve.tensor_copy(out, bank[vbank[j]][0:P, 0:D]).then_inc(v_out, 1)

        peeled(dve, G, group)
    return dict(sync=sync, gpsimd=gpsimd, tensor=tensor, scalar=scalar, vector=vector)


def attention_phase(nc, c, ctx, tag, heads, width, feat, gat, bias, v, resid, w_out, add_eps, ident, fold, bank):
    H = heads
    dot = feat is not None
    pieces = GROUP_COLS if dot else EXP_COLS
    NC = len(pieces)
    NE = len(EXP_COLS)
    s_bank, t_bank, o_bank = bank[0:3], bank[3:6], bank[6:8]
    slots = 4
    S = sb(nc, ctx, f"S{tag}", [P, slots, N])
    B = sb(nc, ctx, f"B{tag}", [P, N])
    PT = sb(nc, ctx, f"PT{tag}", [P, 3, 4 * P])
    PTL = sb(nc, ctx, f"PTL{tag}", [P, 2, P])
    O4 = sb(nc, ctx, f"O4{tag}", [128, 2, P])
    low = sb(nc, ctx, f"low{tag}", [P, H, NC])
    least = sb(nc, ctx, f"least{tag}", [P, H])
    z = sb(nc, ctx, f"z{tag}", [P, H, NE])
    rz = sb(nc, ctx, f"rz{tag}", [P, 3, H])
    agg = sb(nc, ctx, f"agg{tag}", [P, H * width])
    names = ("a_in", "a_dA", "a_dB", "a_qk", "a_red", "a_least", "a_exp", "a_turn", "a_evA", "a_evD", "a_pv", "a_o",
             "a_fold", "a_small", "a_fin", "a_aggT", "a_aggC", "a_wo", "a_res", "a_fifth", "a_sum", "a_row", "a_passed", "a_passed2")
    (a_in, d_a, d_b, s_qk, s_red, s_least, s_exp, s_turn, s_evA, s_evD, s_pv, s_o,
     s_fold, s_small, s_fin, s_aggT, s_aggC, s_wo, s_res, s_fifth, s_sum, s_row, s_passed, s_went) = (
        c.sem(f"{x}{tag}") for x in names)
    b_in = [c.sem(f"a_b{i}{tag}") for i in range(len(BIAS_COLS))]
    biasv = bias[0:NN, :].rearrange("(t p n) o -> t p (n o)", p=P, n=N)
    HH = H // 2
    b_free = (2, 4, 6, 7) if dot else (1, 2, 3, 3)
    b_need = {0: (0,), 2: (1,), 4: (2,), 6: (3,)} if dot else {0: (0,), 1: (1,), 2: (2, 3)}
    if dot:
        A = sb(nc, ctx, f"A{tag}", [128, H, N], F16)
        Dt = sb(nc, ctx, f"Dt{tag}", [128, H, P], F16)
        fd = [f.rearrange("(h d) n -> d h n", d=32) for f in feat[0]]
        fs = [f.rearrange("(h d) n -> d h n", d=32) for f in feat[1]]
    else:
        nas, nad5, nad = gat
        T5 = sb(nc, ctx, f"T5{tag}", [P, 2, N])
        row5 = sb(nc, ctx, f"row5{tag}", [P, H])
    if w_out is not None:
        wo = sb(nc, ctx, f"wo{tag}", [128, KD, D])
        aggT = sb(nc, ctx, f"aggT{tag}", [128, KD, P])

    def before(t, h, n=1):
        return (t, h - n) if h >= n else (t - 1, h - n + H)

    def behind(t, h, n):
        return (t, h + n) if h + n < H else (t + 1, h + n - H)

    def dst_half(sp, t, half):
        for r in range(4):
            with nc.allow_non_contiguous_dma(reason="125 float16 of a row"):
                sp.dma_start(Dt[32 * r:32 * r + 32, half * HH:(half + 1) * HH, :],
                             fd[r // 2][:, half * HH:(half + 1) * HH, bass.ds(t * P, P)]).then_inc((d_a, d_b)[half], 16)

    def bias_part(sp, t, i):
        lo, hi = BIAS_COLS[i]
        sp.dma_start(B[:, lo:hi], biasv[t][:, lo:hi]).then_inc(b_in[i], 16)

    def sync(sp):
        if w_out is not None:
            sp.dma_start(wo[:, :, :], w_out.rearrange("(k p) n -> p k n", p=128)).then_inc(a_in, 16)
        if dot:
            for r in range(4):
                sp.dma_start(A[32 * r:32 * r + 32, :, :], fs[r % 2]).then_inc(a_in, 16)
            for half in range(2):
                dst_half(sp, 0, half)
        for i in range(len(BIAS_COLS)):
            bias_part(sp, 0, i)
        with sp.Fori(0, T - 1) as t:
            if dot:
                for half in range(2):
                    sp.wait_ge(s_qk, NC * (H * t + (half + 1) * HH))
                    dst_half(sp, t + 1, half)
            for i in range(len(BIAS_COLS)):
                sp.wait_ge(s_red, NC * (H * t + H - 1) + b_free[i])
                bias_part(sp, t + 1, i)

    def tensor(pe):
        if dot or w_out is not None:
            pe.wait_ge(a_in, 16 * ((4 if dot else 0) + (w_out is not None)))

        def scores(t, h, j, first=False):
            if not dot:
                return
            k = H * t + h
            if j == 0 and h == 0:
                pe.wait_ge(d_a, 64 * (t + 1))
            if j == 0 and h == HH:
                pe.wait_ge(d_b, 64 * (t + 1))
            if j >= 3:
                pe.wait_ge(s_red, NC * k + j - 2)
            elif not first:
                pe.wait_ge(s_red, NC * (k - 1) + (LAST, 4, 5)[j] + 1)
            lo, hi = GROUP_COLS[j]
            pe.matmul(s_bank[j % 3][0:P, 0:hi - lo], Dt[:, h, :], A[:, h, lo:hi], start=True,
                      stop=True).then_inc(s_qk, 1)

        def copied(t, h, j):
            k = H * t + h
            if j in ON_ACT:
                pe.wait_ge(s_evA, len(ON_ACT) * k + ON_ACT.index(j) + 1)
            else:
                pe.wait_ge(s_evD, len(ON_DVE) * k + ON_DVE.index(j) + 1)

        def turn(t, h, j, first):
            k = H * t + h
            if j in EXP_NEED:
                pe.wait_ge(s_exp, NE * k + EXP_NEED[j] + 1)
            if j >= 3:
                copied(t, h, j - 3)
            elif not first:
                copied(*before(t, h), (LAST, 4, 5)[j])
            for i, s in enumerate(GROUPS[j]):
                mm = pe.transpose(t_bank[j % 3][0:P, i * P:(i + 1) * P], S[0:P, h % slots, s * P:(s + 1) * P],
                                  ident[0:P, 0:P])
            mm.then_inc(s_turn, 1)

        def weigh(t, h, j, first):
            k = H * t + h
            if j == 0 and not (first and h < 2):
                pe.wait_ge(s_fin, k - 1)
            copied(t, h, j)
            for i, s in enumerate(GROUPS[j]):
                w = PT[0:P, j % 3, i * P:(i + 1) * P] if j < LAST else PTL[0:P, h % 2, :]
                mm = pe.matmul(o_bank[h % 2][32 * i:32 * i + 32, 0:P], v[0:P, s, 32 * h:32 * h + 32], w,
                               start=(j == 0), stop=(j == LAST if i == 0 else j == LAST - 1))
            mm.then_inc(s_pv, 1)

        def fold_head(t, h):
            k = H * t + h
            pe.wait_ge(s_o, k + 1)
            pe.matmul(o_bank[h % 2][0:P, 128:160], O4[:, h % 2, :], fold[:, :], start=True,
                      stop=True).then_inc(s_fold, 1)

        def turn_agg(t):
            pe.wait_ge(s_fin, H * (t + 1))
            for k in range(KD):
                mm = pe.transpose(t_bank[1][:, k * P:(k + 1) * P], agg[0:P, k * 128:(k + 1) * 128], ident[0:P, 0:P])
            mm.then_inc(s_aggT, 1)

        def out_project(t):
            pe.wait_ge(s_aggC, t + 1)
            for k in range(KD):
                mm = pe.matmul(t_bank[2][0:P, 0:D], aggT[:, k, :], wo[:, k, :], start=(k == 0), stop=(k == KD - 1))
            mm.then_inc(s_wo, 1)

        def tile(t, first=False, last=False):
            for h in range(H):
                for j in range(LAST + 1):
                    if w_out is not None and not first and h == 2 and j == 2:
                        pe.wait_ge(s_res, t)
                    turn(t, h, j, first and h == 0)
                    if not (last and h >= H - 2):
                        scores(*behind(t, h, 2), j)
                    if j >= 2:
                        weigh(t, h, j - 2, first)
                    elif not (first and h == 0):
                        weigh(*before(t, h), LAST - 1 + j, first)
                    if j == 3 and not (first and h == 0):
                        fold_head(*before(t, h))
                    if w_out is not None and not first:
                        if h == 1 and j == LAST:
                            copied(t, h, 4)
                            turn_agg(t - 1)
                        if h == 2 and j == 0:
                            copied(t, 1, 5)
                            out_project(t - 1)

        for h in range(2):
            for j in range(LAST + 1):
                scores(0, h, j, h == 0)
        tile(0, first=True)
        with pe.Fori(1, T - 1) as t:
            tile(t)
        tile(T - 1, last=True)
        for j in (LAST - 1, LAST):
            weigh(T - 1, H - 1, j, False)
        fold_head(T - 1, H - 1)
        if w_out is not None:
            turn_agg(T - 1)
            out_project(T - 1)

    def vector(dve):
        def reduce_piece(t, h, i):
            k = H * t + h
            lo, hi = pieces[i]
            if i == 0 and not (isinstance(t, int) and k < slots):
                dve.wait_ge(s_turn, 7 * (k - slots + 1))
            if h == 0:
                for b in b_need.get(i, ()):
                    dve.wait_ge(b_in[b], 16 * (t + 1))
            if dot:
                wait_apart(dve, s_qk, NC * k + i + 1, s_passed)
                src = s_bank[i % 3][0:P, 0:hi - lo]
            else:
                if i == 0:
                    dve.wait_ge(s_fifth, k + 1)
                src = T5[:, h % 2, lo:hi]
                dve.scalar_tensor_tensor(out=src, in0=nas[0:P, h, lo:hi], scalar=nad[0:P, bass.ds(t * H + h, 1)],
                                         in1=src, op0=ALU.add, op1=ALU.min).then_inc(s_row, 1)
                wait_apart(dve, s_row, NC * k + i + 1, s_passed)
            dve.tensor_tensor_reduce(S[:, h % slots, lo:hi], src, B[:, lo:hi], 1.0, EMPTY, ALU.add, ALU.min,
                                     low[:, h, i:i + 1]).then_inc(s_red, 1)

        def reduce_all(t, h):
            k = H * t + h
            dve.wait_ge(s_red, NC * (k + 1))
            dve.tensor_reduce(least[:, h:h + 1], low[:, h, :], AX.X, ALU.min).then_inc(s_least, 1)

        def copy_out(t, h, j):
            k = H * t + h
            dve.wait_ge(s_turn, 7 * k + j + 1)
            if j >= 3:
                dve.wait_ge(s_pv, 7 * k + j - 2)
            elif not (isinstance(t, int) and k == 0):
                dve.wait_ge(s_pv, 7 * (k - 1) + j + 4)
            n = len(GROUPS[j]) * P
            dve.tensor_copy(PT[:, j % 3, 0:n], t_bank[j % 3][0:P, 0:n]).then_inc(s_evD, 1)

        def row_sum(t, h, part):
            k = H * t + h
            if part == 0:
                dve.wait_ge(s_exp, NE * (k + 1))
                dve.tensor_reduce(rz[:, 0, h:h + 1], z[:, h, :], AX.X, ALU.add).then_inc(s_small, 1)
            elif part == 1:
                dve.wait_ge(s_small, 3 * k + 1)
                dve.tensor_scalar(rz[:, 1, h:h + 1], rz[:, 0, h:h + 1], add_eps if add_eps else 1e-16, None,
                                  ALU.add if add_eps else ALU.max).then_inc(s_small, 1)
            else:
                dve.wait_ge(s_small, 3 * k + 2)
                dve.reciprocal(rz[:, 2, h:h + 1], rz[:, 1, h:h + 1]).then_inc(s_small, 1)

        def finish(t, h):
            k = H * t + h
            dve.wait_ge(s_small, 3 * k + 3)
            dve.wait_ge(s_fold, k + 1)
            if h == 0 and w_out is not None and not (isinstance(t, int) and t == 0):
                dve.wait_ge(s_aggT, t)
            dve.tensor_scalar(agg[:, width * h:width * (h + 1)], o_bank[h % 2][0:P, 128:128 + width],
                              rz[:, 2, h:h + 1], None, ALU.mult).then_inc(s_fin, 1)

        def residual(t):
            row = resid[0:P, bass.ds(t, 1), 0:H * width].rearrange("p o n -> p (o n)")
            if w_out is not None:
                dve.wait_ge(s_wo, t + 1)
                dve.tensor_tensor(row, row, t_bank[2][0:P, 0:D], ALU.add).then_inc(s_res, 1)
                return
            dve.wait_ge(s_fin, H * (t + 1))
            if dot:
                dve.tensor_tensor(row, row, agg[:, :], ALU.add).then_inc(s_res, 1)
            else:
                dve.tensor_copy(row, agg[:, :]).then_inc(s_res, 1)

        def tile(t, first=False, last=False):
            for h in range(H):
                more = not (last and h >= H - 2)
                done = not (first and h == 0)
                if w_out is None and h == 1 and not first:
                    residual(t - 1)
                for j in range(LAST + 1):
                    if w_out is not None and h == 2 and j == 2 and not first:
                        residual(t - 1)
                    if more and dot:
                        reduce_piece(*behind(t, h, 2), j)
                    elif more and j in (0, 2, 4):
                        reduce_piece(*behind(t, h, 2), j // 2)
                    if j in ON_DVE:
                        copy_out(t, h, j)
                    if j in (0, 2, 4) and done:
                        row_sum(*before(t, h), j // 2)
                if more:
                    reduce_all(*behind(t, h, 2))
                if done:
                    finish(*before(t, h))

        for h in range(2):
            for i in range(NC):
                reduce_piece(0, h, i)
            reduce_all(0, h)
        tile(0, first=True)
        with dve.Fori(1, T - 1) as t:
            tile(t)
        tile(T - 1, last=True)
        for part in range(3):
            row_sum(T - 1, H - 1, part)
        finish(T - 1, H - 1)
        residual(T - 1)
        dve.wait_ge(s_res, T)

    def scalar(act):
        def weights(t, h, i):
            k = H * t + h
            lo, hi = EXP_COLS[i]
            if i == 0:
                act.wait_ge(s_least, k + 1)
            act.activation(S[:, h % slots, lo:hi], S[:, h % slots, lo:hi], ACT.Exp, bias=least[:, h:h + 1], scale=-1.0,
                           accum_out=z[:, h, i:i + 1]).then_inc(s_exp, 1)

        def copy_out(t, h, j):
            k = H * t + h
            act.wait_ge(s_turn, 7 * k + j + 1)
            if j == LAST:
                if not (isinstance(t, int) and k < 2):
                    act.wait_ge(s_pv, 7 * (k - 1))
                act.copy(PTL[:, h % 2, :], t_bank[j % 3][0:P, 0:P]).then_inc(s_evA, 1)
                return
            if j >= 3:
                act.wait_ge(s_pv, 7 * k + j - 2)
            elif not (isinstance(t, int) and k == 0):
                act.wait_ge(s_pv, 7 * (k - 1) + j + 4)
            n = len(GROUPS[j]) * P
            act.copy(PT[:, j % 3, 0:n], t_bank[j % 3][0:P, 0:n]).then_inc(s_evA, 1)

        def sums_out(t, h):
            k = H * t + h
            act.wait_ge(s_pv, 7 * (k + 1))
            if not (isinstance(t, int) and k < 2):
                act.wait_ge(s_fold, k - 1)
            act.copy(O4[:, h % 2, :], o_bank[h % 2][:, 0:P]).then_inc(s_o, 1)

        def agg_out(t):
            act.wait_ge(s_aggT, t + 1)
            act.copy(aggT[:, :, :], t_bank[1][:, 0:KD * P].rearrange("p (k n) -> p k n", k=KD)).then_inc(s_aggC, 1)

        def tile(t, first=False, last=False):
            for h in range(H):
                for j in range(LAST + 1):
                    if j in ON_ACT:
                        copy_out(t, h, j)
                    if w_out is not None and h == 2 and j == 0 and not first:
                        agg_out(t - 1)
                    if j in EXP_AT and not (last and h == H - 1):
                        weights(*behind(t, h, 1), EXP_AT.index(j))
                    if j == 2 and not (first and h == 0):
                        sums_out(*before(t, h))

        for i in range(NE):
            weights(0, 0, i)
        tile(0, first=True)
        with act.Fori(1, T - 1) as t:
            tile(t)
        tile(T - 1, last=True)
        sums_out(T - 1, H - 1)
        if w_out is not None:
            agg_out(T - 1)

    def gpsimd(pool):
        def fifth(t, h):
            k = H * t + h
            if h == 0:
                if not (isinstance(t, int) and t == 0):
                    pool.wait_ge(s_fifth, k)
                pool.tensor_copy(row5[:, :], nad5[0:P, bass.ds(t * H, H)]).then_inc(s_sum, 1)
                wait_apart(pool, s_sum, t + 1, s_went)
            if not (isinstance(t, int) and k < 2):
                wait_apart(pool, s_red, NC * (k - 1), s_went)
            pool.tensor_scalar(T5[:, h % 2, :], nas[0:P, h, :], 0.2, row5[:, h:h + 1], ALU.mult,
                               ALU.add).then_inc(s_fifth, 1)

        for h in range(H):
            fifth(0, h)
        with pool.Fori(1, T) as t:
            for h in range(H):
                fifth(t, h)

    phase = dict(sync=sync, tensor=tensor, vector=vector, scalar=scalar)
    if not dot:
        phase["gpsimd"] = gpsimd
    return phase


def stage_rows(pool, g, h, hs, turned, staged):
    wait_from(pool, turned, 4 * g)
    for j in range(GT):
        pool.tensor_copy(hs[:, j, :], h[:, bass.ds(g * GT + j, 1), :].rearrange("p o n -> p (o n)")).then_inc(staged, 1)


def turned_out(act, g, ht, bank, turned, ht_ok):
    for k in range(KD):
        for s, (lo, hi) in enumerate(SPLIT):
            act.wait_ge(turned, 4 * g + 2 * k + s + 1)
            act.copy(ht[:, k, lo:hi], bank[2 * k + s][:, 0:hi - lo]).then_inc(ht_ok, 1)


def ffn_phase(nc, c, ctx, tag, h, x, w1, b1, w2, b2, func, experts, hidden, gate, ident, bank):
    E, M = experts, hidden // 128
    w1s = sb(nc, ctx, f"w1{tag}", [128, KD, E, hidden])
    w2s = sb(nc, ctx, f"w2{tag}", [128, E, M, D])
    b1s = sb(nc, ctx, f"b1{tag}", [128, E, M])
    b2s = sb(nc, ctx, f"b2{tag}", [P, E, D])
    hs = sb(nc, ctx, f"hs{tag}", [P, GT, D])
    ht = sb(nc, ctx, f"ht{tag}", [128, KD, GN])
    mid = sb(nc, ctx, f"mid{tag}", [128, M, GN])
    plus = sb(nc, ctx, f"plus{tag}", [P, 2, D])
    (win, staged, turned, ht_ok, up_mm, up_out, down_mm, down_b, down_out) = (
        c.sem(f"{v}{tag}") for v in ("f_w", "f_stage", "f_turn", "f_ht", "f_up", "f_mid", "f_down", "f_plus", "f_x"))
    U = 2 * M

    def sync(sp):
        for e in range(E):
            sp.dma_start(w1s[:, :, e, :], w1[e].rearrange("(k p) n -> p k n", p=128)).then_inc(win, 16)
            sp.dma_start(w2s[:, e, :, :], w2[e].rearrange("(m p) n -> p m n", p=128)).then_inc(win, 16)
            with nc.allow_non_contiguous_dma(reason="a bias column, once"):
                sp.dma_start(b1s[:, e, :], b1[e].rearrange("(m p) -> p m", p=128)).then_inc(win, 16)
            sp.dma_start(b2s[:, e, :], rows(b2[e], P)).then_inc(win, 16)

    def gpsimd(pool):
        def group(g):
            stage_rows(pool, g, h, hs, turned, staged)

        peeled(pool, G, group)
    def tensor(pe):
        pe.wait_ge(win, 64 * E)
        def group(g):
            pe.wait_ge(staged, GT * (g + 1))
            wait_from(pe, up_out, U * E * g)
            transpose_group(pe, hs, bank, ident, None, None, turned)
            pe.wait_ge(ht_ok, 4 * (g + 1))
            for e in range(E):
                for m in range(M):
                    for s, (lo, hi) in enumerate(SPLIT):
                        n = 2 * m + s
                        if n >= 4:
                            wait_from(pe, up_out, U * (E * g + e) + n - 3)
                        elif e:
                            wait_from(pe, up_out, U * (E * g + e) - 4 + n + 1)
                        for k in range(KD):
                            mm = pe.matmul(bank[n % 4][:, 0:hi - lo], w1s[:, k, e, m * 128:(m + 1) * 128],
                                           ht[:, k, lo:hi], start=(k == 0), stop=(k == KD - 1))
                        mm.then_inc(up_mm, 1)
                pe.wait_ge(up_out, U * (E * g + e + 1))
                for j in range(GT):
                    i = e * GT + j
                    if i >= 4:
                        wait_from(pe, down_b, E * GT * g + i - 3)
                    else:
                        wait_from(pe, down_b, E * GT * g)
                    for m in range(M):
                        mm = pe.matmul(bank[4 + i % 4][0:P, 0:D], mid[:, m, j * P:(j + 1) * P], w2s[:, e, m, :],
                                       start=(m == 0), stop=(m == M - 1))
                    mm.then_inc(down_mm, 1)

        peeled(pe, G, group)
    def scalar(act):
        act.wait_ge(win, 64 * E)
        def group(g):
            wait_from(act, up_mm, U * E * g)
            turned_out(act, g, ht, bank, turned, ht_ok)
            for e in range(E):
                wait_from(act, down_mm, GT * (E * g + e))
                for m in range(M):
                    for s, (lo, hi) in enumerate(SPLIT):
                        act.wait_ge(up_mm, U * (E * g + e) + 2 * m + s + 1)
                        act.activation(mid[:, m, lo:hi], bank[(2 * m + s) % 4][:, 0:hi - lo], func,
                                       bias=b1s[:, e, m:m + 1]).then_inc(up_out, 1)

        peeled(act, G, group)
    def vector(dve):
        dve.wait_ge(win, 64 * E)
        def group(g):
            for e in range(E):
                for j in range(GT):
                    i = e * GT + j
                    n = E * GT * g + i
                    row = x[0:P, bass.ds(g * GT + j, 1), :].rearrange("p o n -> p (o n)")
                    dve.wait_ge(down_mm, n + 1)
                    dve.tensor_tensor(plus[:, i % 2, :], bank[4 + i % 4][0:P, 0:D], b2s[:, e, :], ALU.add).then_inc(down_b, 1)
                    dve.wait_ge(down_b, n + 1)
                    if gate is None:
                        dve.tensor_tensor(row, row, plus[:, i % 2, :], ALU.add).then_inc(down_out, 1)
                    else:
                        dve.scalar_tensor_tensor(out=row, in0=plus[:, i % 2, :],
                                                 scalar=gate[0:P, bass.ds((g * GT + j) * E + e, 1)], in1=row,
                                                 op0=ALU.mult, op1=ALU.add).then_inc(down_out, 1)
                    if j == GT - 1:
                        dve.wait_ge(down_out, n + 1)

        peeled(dve, G, group)
    return dict(sync=sync, gpsimd=gpsimd, tensor=tensor, scalar=scalar, vector=vector)


SH, SG = 8, 64
SI = SH * SG
SM = SI // 128


def slice_phase(nc, c, ctx, tag, h, a, swt, token, norm, ident, ones, bank):
    wfx = sb(nc, ctx, "wfx", [128, KD, SI])
    wx = sb(nc, ctx, "wx", [128, KD, SI])
    bx = sb(nc, ctx, "bx", [128, SM])
    bfx = sb(nc, ctx, "bfx", [P, SI])
    bsl = sb(nc, ctx, "bsl", [P, SI])
    tmp = sb(nc, ctx, "tmp", [P, SH])
    rtw = sb(nc, ctx, "rtw", [P, SI])
    wsl = sb(nc, ctx, "wsl", [128, 128])
    hs = sb(nc, ctx, "hs_s", [P, GT, D])
    ht = sb(nc, ctx, "ht_s", [128, KD, GN])
    xm = sb(nc, ctx, "xm", [128, SM, GN])
    fx = sb(nc, ctx, "fx", [P, 2, SI])
    lg = sb(nc, ctx, "lg", [P, 2, SI])
    top = sb(nc, ctx, "top", [P, 2, 3, SH])
    names = ("win", "wz", "prep", "staged", "turned", "ht_ok", "xm_mm", "xm_out", "fx_mm", "fx_out", "lg_mm", "lg_out",
             "soft", "exped", "sw_ok", "tok_mm", "tok_out", "swt_mm", "swt_out")
    (win, wz, prep, staged, turned, ht_ok, xm_mm, xm_out, fx_mm, fx_out, lg_mm, lg_out, soft, exped, sw_ok, tok_mm,
     tok_out, swt_mm, swt_out) = (c.sem(f"s_{v}") for v in names)

    def sync(sp):
        sp.dma_start(wfx[:, :, :], a["L0_ffn_W_fx"].rearrange("(k p) n -> p k n", p=128)).then_inc(win, 16)
        sp.dma_start(wx[:, :, :], a["L0_ffn_W_x"].rearrange("(k p) n -> p k n", p=128)).then_inc(win, 16)
        with nc.allow_non_contiguous_dma(reason="a bias column, once"):
            sp.dma_start(bx[:, :], a["L0_ffn_b_x"].rearrange("(m p) -> p m", p=128)).then_inc(win, 16)
        sp.dma_start(bfx[:, :], rows(a["L0_ffn_b_fx"], P)).then_inc(win, 16)
        for i in range(SH):
            sp.dma_start(bsl[:, i * SG:(i + 1) * SG], rows(a["L0_ffn_b_slice"], P)).then_inc(win, 16)
        sp.dma_start(tmp[:, :], rows(a["L0_ffn_temperature"].rearrange("a h b c -> (a h b c)"), P)).then_inc(win, 16)
        sp.wait_ge(wz, 1)
        for i in range(2):
            sp.dma_start(wsl[64 * i:64 * i + 64, 64 * i:64 * i + 64], a["L0_ffn_W_slice"]).then_inc(win, 16)

    def gpsimd(pool):
        pool.memset(wsl[:, :], 0.0).then_inc(wz, 1)
        def group(g):
            stage_rows(pool, g, h, hs, turned, staged)

        peeled(pool, G, group)
    def tensor(pe):
        pe.wait_ge(win, 16 * 15)
        def group(g):
            pe.wait_ge(staged, GT * (g + 1))
            wait_from(pe, xm_out, 8 * g)
            wait_from(pe, tok_out, 2 * g)
            transpose_group(pe, hs, bank, ident, None, None, turned)
            pe.wait_ge(ht_ok, 4 * (g + 1))
            for m in range(SM):
                for s, (lo, hi) in enumerate(SPLIT):
                    n = 2 * m + s
                    if n >= 4:
                        wait_from(pe, xm_out, 8 * g + n - 3)
                    for k in range(KD):
                        mm = pe.matmul(bank[n % 4][:, 0:hi - lo], wx[:, k, m * 128:(m + 1) * 128], ht[:, k, lo:hi],
                                       start=(k == 0), stop=(k == KD - 1))
                    mm.then_inc(xm_mm, 1)

            def logits(j):
                t = GT * g + j
                wait_from(pe, fx_out, t)
                for k in range(KD):
                    mm = pe.matmul(bank[4][0:P, :], ht[:, k, j * P:(j + 1) * P], wfx[:, k, :], start=(k == 0), stop=(k == KD - 1))
                mm.then_inc(fx_mm, 1)
                wait_from(pe, lg_out, t)
                if j == 0:
                    pe.wait_ge(xm_out, 8 * (g + 1))
                for m in range(SM):
                    mm = pe.matmul(bank[5][0:P, m * 128:(m + 1) * 128], xm[:, m, j * P:(j + 1) * P], wsl[:, :],
                                   start=True, stop=True)
                mm.then_inc(lg_mm, 1)

            def tokens(j):
                t = GT * g + j
                pe.wait_ge(sw_ok, t + 1)
                for m in range(SM):
                    pe.matmul(bank[7][:, m * 128:(m + 1) * 128], lg[:, j % 2, m * 128:(m + 1) * 128],
                              fx[:, j % 2, m * 128:(m + 1) * 128], start=(j == 0 and m == 0),
                              stop=(j == GT - 1 and m == SM - 1), skip_group_check=True)
                for m in range(SM):
                    mm = pe.matmul(bank[3][:, m:m + 1], lg[:, j % 2, m * 128:(m + 1) * 128], ones[0:P, 0:1],
                                   start=(j == 0 and m == 0), stop=(j == GT - 1 and m == SM - 1), skip_group_check=True)
                mm.then_inc(tok_mm, 1)
                wait_from(pe, swt_out, t)
                for m in range(SM):
                    mm = pe.transpose(bank[6][:, m * P:(m + 1) * P], lg[0:P, j % 2, m * 128:(m + 1) * 128], ident[0:P, 0:P])
                mm.then_inc(swt_mm, 1)

            logits(0)
            for j in range(GT):
                if j + 1 < GT:
                    logits(j + 1)
                tokens(j)

        peeled(pe, G, group)
    def scalar(act):
        act.wait_ge(win, 16 * 15)
        def group(g):
            wait_from(act, fx_mm, GT * g)
            turned_out(act, g, ht, bank, turned, ht_ok)
            wait_from(act, lg_mm, GT * g)
            for m in range(SM):
                for s, (lo, hi) in enumerate(SPLIT):
                    n = 2 * m + s
                    act.wait_ge(xm_mm, 8 * g + n + 1)
                    act.activation(xm[:, m, lo:hi], bank[n % 4][:, 0:hi - lo], ACT.Identity,
                                   bias=bx[:, m:m + 1]).then_inc(xm_out, 1)
            for j in range(GT):
                t = GT * g + j
                act.wait_ge(soft, 3 * t + 2)
                act.activation(lg[:, j % 2, :], lg[:, j % 2, :], ACT.Exp).then_inc(exped, 1)
                if j >= 1:
                    wait_from(act, swt_mm, t)
                    act.copy(swt[:, :, bass.ds((t - 1) * P, P)], bank[6][:, 0:SM * P].rearrange("p (m n) -> p m n", m=SM)).then_inc(swt_out, 1)
            act.wait_ge(swt_mm, GT * g + GT)
            act.copy(swt[:, :, bass.ds((GT * g + GT - 1) * P, P)],
                     bank[6][:, 0:SM * P].rearrange("p (m n) -> p m n", m=SM)).then_inc(swt_out, 1)

        peeled(act, G, group)
    def vector(dve):
        def heads(ap):
            return ap.rearrange("p (h g) -> p h g", h=SH)

        dve.wait_ge(win, 16 * 15)
        dve.memset(token[:, :], 0.0).then_inc(prep, 1)
        dve.memset(norm[:, :], 0.0).then_inc(prep, 1)
        dve.tensor_scalar(tmp[:, :], tmp[:, :], 0.1, 5.0, ALU.max, ALU.min).then_inc(prep, 1)
        dve.wait_ge(prep, 3)
        dve.reciprocal(tmp[:, :], tmp[:, :]).then_inc(prep, 1)
        dve.wait_ge(prep, 4)
        dve.tensor_copy(heads(rtw[:, :]), tmp[:, :].unsqueeze(2).to_broadcast([P, SH, SG])).then_inc(prep, 1)
        dve.wait_ge(prep, 5)
        def group(g):
            for j in range(GT):
                t = GT * g + j
                b = j % 2
                dve.wait_ge(fx_mm, t + 1)
                if j >= 2:
                    wait_from(dve, tok_mm, t - 1)
                    wait_from(dve, swt_mm, t - 1)
                else:
                    wait_from(dve, tok_mm, GT * g)
                    wait_from(dve, swt_mm, GT * g)
                dve.tensor_tensor(fx[:, b, :], bank[4][0:P, :], bfx[:, :], ALU.add).then_inc(fx_out, 1)
                dve.wait_ge(lg_mm, t + 1)
                dve.tensor_tensor(lg[:, b, :], bank[5][0:P, :], bsl[:, :], ALU.add).then_inc(lg_out, 1)
                dve.wait_ge(lg_out, t + 1)
                dve.tensor_tensor(lg[:, b, :], lg[:, b, :], rtw[:, :], ALU.mult).then_inc(soft, 1)
                dve.wait_ge(soft, 3 * t + 1)
                dve.tensor_reduce(top[:, b, 0, :], heads(lg[:, b, :]), AX.X, ALU.max).then_inc(prep, 1)
                dve.wait_ge(prep, 5 + 3 * t + 1)
                dve.tensor_tensor(heads(lg[:, b, :]), heads(lg[:, b, :]),
                                  top[:, b, 0, :].unsqueeze(2).to_broadcast([P, SH, SG]), ALU.subtract).then_inc(soft, 1)
                dve.wait_ge(exped, t + 1)
                dve.tensor_reduce(top[:, b, 1, :], heads(lg[:, b, :]), AX.X, ALU.add).then_inc(prep, 1)
                dve.wait_ge(prep, 5 + 3 * t + 2)
                dve.reciprocal(top[:, b, 2, :], top[:, b, 1, :]).then_inc(prep, 1)
                dve.wait_ge(prep, 5 + 3 * t + 3)
                dve.tensor_tensor(heads(lg[:, b, :]), heads(lg[:, b, :]),
                                  top[:, b, 2, :].unsqueeze(2).to_broadcast([P, SH, SG]), ALU.mult).then_inc(soft, 1)
                dve.wait_ge(soft, 3 * t + 3)
                dve.sem_inc(sw_ok, 1)
            dve.wait_ge(tok_mm, GT * (g + 1))
            dve.tensor_tensor(token[:, :], token[:, :], bank[7][:, :], ALU.add).then_inc(tok_out, 1)
            dve.tensor_tensor(norm[:, :], norm[:, :], bank[3][:, 0:SM], ALU.add).then_inc(tok_out, 1)
            dve.wait_ge(tok_out, 2 * (g + 1))

        peeled(dve, G, group)
    return dict(sync=sync, gpsimd=gpsimd, tensor=tensor, scalar=scalar, vector=vector)


def token_phase(nc, c, ctx, a, token, norm, mix, ident, bank):
    block = sb(nc, ctx, "block", [128, SM, 128])
    w3 = sb(nc, ctx, "w3", [128, 3, 128])
    wo = sb(nc, ctx, "wo_s", [128, SM, D])
    tt = sb(nc, ctx, "tt", [128, SM, 128])
    qkv = sb(nc, ctx, "qkv", [128, 3, SM, 128])
    att = sb(nc, ctx, "att_s", [128, SM, SG])
    attb = sb(nc, ctx, "attb", [128, SM, 128])
    attt = sb(nc, ctx, "attt", [128, SM, 128])
    outt = sb(nc, ctx, "outt", [128, SM, 128])
    rn = sb(nc, ctx, "rn", [128, SM])
    st = sb(nc, ctx, "st_s", [128, 3, SM])
    win, wz, step, mm_ok, act_ok = (c.sem(f"t_{v}") for v in ("win", "wz", "step", "mm", "act"))
    halves = ((0, 64), (64, 128))

    def sync(sp):
        sp.wait_ge(wz, 2)
        for i, w in enumerate(("L0_ffn_W_q", "L0_ffn_W_k", "L0_ffn_W_v")):
            for lo, hi in halves:
                sp.dma_start(w3[lo:hi, i, lo:hi], a[w]).then_inc(win, 16)
        sp.dma_start(wo[:, :, :], a["L0_ffn_W_out"].rearrange("(m p) n -> p m n", p=128)).then_inc(win, 16)

    def gpsimd(pool):
        pool.memset(w3[:, :, :], 0.0).then_inc(wz, 1)
        pool.memset(block[:, :, :], 0.0).then_inc(wz, 1)

    def flat(ap):
        return ap.rearrange("p m n -> p (m n)")

    def vector(dve):
        n = [0]

        def then(ins):
            n[0] += 1
            ins.then_inc(step, 1)
            dve.wait_ge(step, n[0])

        dve.wait_ge(wz, 2)
        for lo, hi in halves:
            then(dve.memset(block[lo:hi, :, lo:hi], 1.0))
        then(dve.tensor_scalar(rn[:, :], norm[:, :], 1e-5, None, ALU.add))
        then(dve.reciprocal(rn[:, :], rn[:, :]))
        t3 = token[:, :].rearrange("p (m n) -> p m n", m=SM)
        then(dve.tensor_tensor(t3, t3, rn[:, :].unsqueeze(2).to_broadcast([128, SM, 128]), ALU.mult))
        then(dve.tensor_tensor(t3, t3, block[:, :, :], ALU.mult))
        dve.wait_ge(mm_ok, 1)
        then(dve.tensor_copy(flat(tt[:, :, :]), bank[0][:, :]))
        for i in range(3):
            dve.wait_ge(mm_ok, 2 + i)
            then(dve.tensor_copy(flat(qkv[:, i, :, :]), bank[1 + i][:, :]))
        dve.wait_ge(mm_ok, 5)
        s3 = bank[4][:, :].rearrange("p (m n) -> p m n", m=SM)
        for lo, hi in halves:
            then(dve.tensor_copy(att[lo:hi, :, :], s3[lo:hi, :, lo:hi]))
        then(dve.tensor_reduce(st[:, 0, :], att[:, :, :], AX.X, ALU.max))
        then(dve.tensor_tensor(att[:, :, :], att[:, :, :], st[:, 0, :].unsqueeze(2).to_broadcast([128, SM, SG]),
                               ALU.subtract))
        dve.wait_ge(act_ok, 1)
        then(dve.tensor_reduce(st[:, 1, :], att[:, :, :], AX.X, ALU.add))
        then(dve.reciprocal(st[:, 2, :], st[:, 1, :]))
        then(dve.tensor_tensor(att[:, :, :], att[:, :, :], st[:, 2, :].unsqueeze(2).to_broadcast([128, SM, SG]), ALU.mult))
        then(dve.memset(attb[:, :, :], 0.0))
        for lo, hi in halves:
            then(dve.tensor_copy(attb[lo:hi, :, lo:hi], att[lo:hi, :, :]))
        dve.wait_ge(mm_ok, 6)
        then(dve.tensor_copy(flat(attt[:, :, :]), bank[5][:, :]))
        dve.wait_ge(mm_ok, 7)
        then(dve.tensor_copy(flat(outt[:, :, :]), bank[6][:, :]))
        for m in range(SM):
            dve.wait_ge(mm_ok, 8 + m)
            then(dve.tensor_copy(mix[:, m, :], bank[m][:, 0:D]))

    def scalar(act):
        act.wait_ge(step, 14)
        act.activation(att[:, :, :], att[:, :, :], ACT.Exp, scale=float(SG) ** -0.5).then_inc(act_ok, 1)

    def tensor(pe):
        def four(b, lhs, rhs):
            for m in range(SM):
                mm = pe.matmul(bank[b][:, m * 128:(m + 1) * 128], lhs(m), rhs(m), start=True, stop=True)
            mm.then_inc(mm_ok, 1)

        pe.wait_ge(win, 16 * 7)
        pe.wait_ge(step, 6)
        for m in range(SM):
            mm = pe.transpose(bank[0][:, m * 128:(m + 1) * 128], token[:, m * 128:(m + 1) * 128], ident[:, :])
        mm.then_inc(mm_ok, 1)
        pe.wait_ge(step, 7)
        four(1, lambda m: w3[:, 0, :], lambda m: tt[:, m, :])
        four(2, lambda m: w3[:, 1, :], lambda m: tt[:, m, :])
        four(3, lambda m: tt[:, m, :], lambda m: w3[:, 2, :])
        pe.wait_ge(step, 10)
        four(4, lambda m: qkv[:, 0, m, :], lambda m: qkv[:, 1, m, :])
        pe.wait_ge(step, 20)
        for m in range(SM):
            mm = pe.transpose(bank[5][:, m * 128:(m + 1) * 128], attb[:, m, :], ident[:, :])
        mm.then_inc(mm_ok, 1)
        pe.wait_ge(step, 21)
        four(6, lambda m: qkv[:, 2, m, :], lambda m: attt[:, m, :])
        pe.wait_ge(step, 22)
        for m in range(SM):
            pe.matmul(bank[m][:, 0:D], outt[:, m, :], wo[:, m, :], start=True, stop=True).then_inc(mm_ok, 1)

    return dict(sync=sync, gpsimd=gpsimd, tensor=tensor, scalar=scalar, vector=vector)


def spread_phase(nc, c, ctx, a, swt, mix, x, bank):
    part = sb(nc, ctx, "part_s", [128, SM, GN])
    bo = sb(nc, ctx, "bo", [P, D])
    plus = sb(nc, ctx, "plus_s", [P, 2, D])
    win, staged, mm_ok, added, out = (c.sem(f"o_{v}") for v in ("win", "stage", "mm", "add", "out"))

    def sync(sp):
        sp.dma_start(bo[:, :], rows(a["L0_ffn_b_out"], P)).then_inc(win, 16)

    def gpsimd(pool):
        def group(g):
            wait_from(pool, mm_ok, GT * g)
            for m in range(SM):
                pool.tensor_copy(part[:, m, :], swt[:, m, bass.ds(g * GN, GN)]).then_inc(staged, 1)

        peeled(pool, G, group)
    def tensor(pe):
        def group(g):
            pe.wait_ge(staged, SM * (g + 1))
            wait_from(pe, added, GT * g)
            for j in range(GT):
                for m in range(SM):
                    mm = pe.matmul(bank[j][0:P, 0:D], part[:, m, j * P:(j + 1) * P], mix[:, m, :], start=(m == 0), stop=(m == SM - 1))
                mm.then_inc(mm_ok, 1)

        peeled(pe, G, group)
    def vector(dve):
        dve.wait_ge(win, 16)
        def group(g):
            for j in range(GT):
                n = GT * g + j
                row = x[0:P, bass.ds(n, 1), :].rearrange("p o n -> p (o n)")
                dve.wait_ge(mm_ok, n + 1)
                dve.tensor_tensor(plus[:, j % 2, :], bank[j][0:P, 0:D], bo[:, :], ALU.add).then_inc(added, 1)
                dve.wait_ge(added, n + 1)
                dve.tensor_tensor(row, row, plus[:, j % 2, :], ALU.add).then_inc(out, 1)
                dve.wait_ge(out, n + 1)

        peeled(dve, G, group)
    return dict(sync=sync, gpsimd=gpsimd, tensor=tensor, vector=vector)


RH, RE = 4, 4
RF = RH * RE


def router_phase(nc, c, ctx, h, a, vpad, nas, nad, nad5, ident, bank):
    wg = sb(nc, ctx, "wg", [128, KD, RF])
    asrc = sb(nc, ctx, "asrc", [RF, 1])
    spread = sb(nc, ctx, "spread_r", [RF, RH, 128])
    adst = sb(nc, ctx, "adst", [P, RF])
    hs = sb(nc, ctx, "hs_r", [P, GT, D])
    ht = sb(nc, ctx, "ht_r", [128, KD, GN])
    hg = sb(nc, ctx, "hg", [RF, GN])
    prod = sb(nc, ctx, "prod_r", [P, T * RF])
    win, prep, masked, staged, turned, ht_ok, hg_mm, hg_out, row_mm, row_out, v_mm, v_out, fin = (
        c.sem(f"r_{v}") for v in ("win", "prep", "mask", "stage", "turn", "ht", "hgm", "hgo", "rowm", "rowo", "vm", "vo", "fin"))

    def sync(sp):
        sp.dma_start(wg[:, :, :], a["L1_ffn_W_gat"].rearrange("(k p) n -> p k n", p=128)).then_inc(win, 16)
        with nc.allow_non_contiguous_dma(reason="16 values, once"):
            sp.dma_start(asrc[:, :], a["L1_ffn_att_src"].rearrange("h (e o) -> (h e) o", o=1)).then_inc(win, 16)
        sp.dma_start(adst[:, :], rows(a["L1_ffn_att_dst"].rearrange("h e -> (h e)"), P)).then_inc(win, 16)

    def gpsimd(pool):
        pool.wait_ge(prep, 1)
        for hd in range(RH):
            pool.affine_select(out=spread[:, hd, :], in_=spread[:, hd, :], compare_op=ALU.is_ge, fill=0.0,
                               base=-RE * hd, pattern=[[0, 128]], channel_multiplier=1).then_inc(masked, 1)
            pool.wait_ge(masked, 2 * hd + 1)
            pool.affine_select(out=spread[:, hd, :], in_=spread[:, hd, :], compare_op=ALU.is_ge, fill=0.0,
                               base=RE * hd + RE - 1, pattern=[[0, 128]], channel_multiplier=-1).then_inc(masked, 1)
        def group(g):
            stage_rows(pool, g, h, hs, turned, staged)

        peeled(pool, G, group)
    def tensor(pe):
        pe.wait_ge(win, 48)
        pe.wait_ge(masked, 2 * RH)
        def group(g):
            pe.wait_ge(staged, GT * (g + 1))
            wait_from(pe, hg_out, 2 * g)
            wait_from(pe, row_out, 2 * RH * g)
            transpose_group(pe, hs, bank, ident, None, None, turned)
            pe.wait_ge(ht_ok, 4 * (g + 1))
            for s, (lo, hi) in enumerate(SPLIT):
                for k in range(KD):
                    mm = pe.matmul(bank[s][0:RF, 0:hi - lo], wg[:, k, :], ht[:, k, lo:hi], start=(k == 0), stop=(k == KD - 1))
                mm.then_inc(hg_mm, 1)
            for j in range(GT):
                wait_from(pe, v_out, GT * g + j - 3 if j >= 4 else GT * g)
                for k in range(KD):
                    mm = pe.matmul(bank[4 + j % 4][0:P, 0:RF], ht[:, k, j * P:(j + 1) * P], wg[:, k, :], start=(k == 0), stop=(k == KD - 1))
                mm.then_inc(v_mm, 1)
            pe.wait_ge(hg_out, 2 * (g + 1))
            for hd in range(RH):
                for s, (lo, hi) in enumerate(SPLIT):
                    n = 2 * hd + s
                    if n >= 4:
                        wait_from(pe, row_out, 2 * RH * g + n - 3)
                    pe.matmul(bank[n % 4][:, 0:hi - lo], spread[:, hd, :], hg[:, lo:hi], start=True, stop=True).then_inc(row_mm, 1)

        peeled(pe, G, group)
    def scalar(act):
        def group(g):
            wait_from(act, v_mm, GT * g)
            turned_out(act, g, ht, bank, turned, ht_ok)
            wait_from(act, row_mm, 2 * RH * g)
            for s, (lo, hi) in enumerate(SPLIT):
                act.wait_ge(hg_mm, 2 * g + s + 1)
                act.copy(hg[:, lo:hi], bank[s][0:RF, 0:hi - lo]).then_inc(hg_out, 1)
            for hd in range(RH):
                for s, (lo, hi) in enumerate(SPLIT):
                    n = 2 * hd + s
                    act.wait_ge(row_mm, 2 * RH * g + n + 1)
                    act.copy(nas[:, hd, bass.ds(g * GN + lo, hi - lo)], bank[n % 4][:, 0:hi - lo]).then_inc(row_out, 1)

        peeled(act, G, group)
    def vector(dve):
        dve.wait_ge(win, 48)
        dve.tensor_scalar(spread[:, :, :].rearrange("p h n -> p (h n)"), asrc[:, 0:1].to_broadcast([RF, RH * 128]), -1.0,
                          None, ALU.mult).then_inc(prep, 1)
        dve.memset(vpad[:, :, :, :], 0.0).then_inc(fin, 1)
        dve.wait_ge(fin, 1)
        def group(g):
            for j in range(GT):
                dve.wait_ge(v_mm, GT * g + j + 1)
                dve.tensor_copy(vpad[:, bass.ds(g * GT + j, 1), :, 0:RE].rearrange("p o h e -> p (o h) e"),
                                bank[4 + j % 4][0:P, 0:RF].rearrange("p (h e) -> p h e", h=RH)).then_inc(v_out, 1)

        peeled(dve, G, group)
        dve.wait_ge(v_out, T)
        p3 = prod[:, :].rearrange("p (t h e) -> p t h e", t=T, h=RH)
        for hd in range(RH):
            dve.tensor_tensor(p3[:, :, hd, :], vpad[:, :, hd, 0:RE],
                              adst[:, hd * RE:(hd + 1) * RE].unsqueeze(1).to_broadcast([P, T, RE]), ALU.mult).then_inc(fin, 1)
        dve.wait_ge(fin, 1 + RH)
        dve.tensor_reduce(nad[:, :], prod[:, :].rearrange("p (n e) -> p n e", e=RE), AX.X, ALU.add, negate=True).then_inc(fin, 1)
        dve.wait_ge(fin, 2 + RH)
        dve.tensor_scalar(nad5[:, :], nad[:, :], 0.2, None, ALU.mult).then_inc(fin, 1)

    return dict(sync=sync, gpsimd=gpsimd, tensor=tensor, scalar=scalar, vector=vector)


def gate_phase(nc, c, ctx, a, agg, gate):
    vec = sb(nc, ctx, "vec_g", [P, 3, RF])
    sq = sb(nc, ctx, "sq_g", [P, T, RF])
    st = sb(nc, ctx, "st_g", [P, 4, T])
    s = sb(nc, ctx, "s_g", [P, T, RE])
    ex = sb(nc, ctx, "ex_g", [P, T, RE])
    rank = sb(nc, ctx, "rank_g", [P, T, RE])
    more = sb(nc, ctx, "more_g", [P, T])
    win, step, act_ok = c.sem("g_win"), c.sem("g_step"), c.sem("g_act")

    def sync(sp):
        for i, v in enumerate(("L1_ffn_b_gat", "L1_ffn_ln_gamma", "L1_ffn_ln_beta")):
            sp.dma_start(vec[:, i, :], rows(a[v], P)).then_inc(win, 16)

    def vector(dve):
        n = [0]

        def then(ins):
            n[0] += 1
            ins.then_inc(step, 1)
            dve.wait_ge(step, n[0])

        def row(i):
            return vec[:, i, :].unsqueeze(1).to_broadcast([P, T, RF])

        def col(i, w):
            return st[:, i, :].unsqueeze(2).to_broadcast([P, T, w])

        dve.wait_ge(win, 48)
        x = agg[:, :, :]
        then(dve.tensor_tensor(x, x, row(0), ALU.add))
        then(dve.tensor_reduce(st[:, 0, :], x, AX.X, ALU.add))
        then(dve.tensor_scalar(st[:, 0, :], st[:, 0, :], 1.0 / RF, None, ALU.mult))
        then(dve.tensor_tensor(x, x, col(0, RF), ALU.subtract))
        then(dve.tensor_tensor(sq[:, :, :], x, x, ALU.mult))
        then(dve.tensor_reduce(st[:, 1, :], sq[:, :, :], AX.X, ALU.add))
        then(dve.tensor_scalar(st[:, 1, :], st[:, 1, :], 1.0 / RF, LN_EPS, ALU.mult, ALU.add))
        dve.wait_ge(act_ok, 1)
        then(dve.reciprocal(st[:, 2, :], st[:, 2, :]))
        then(dve.tensor_tensor(x, x, col(2, RF), ALU.mult))
        then(dve.tensor_tensor(x, x, row(1), ALU.mult))
        then(dve.tensor_tensor(x, x, row(2), ALU.add))
        then(dve.tensor_reduce(s[:, :, :], agg[:, :, :].rearrange("p t (h e) -> p t e h", h=RH), AX.X, ALU.add))
        then(dve.tensor_scalar(s[:, :, :], s[:, :, :], 1.0 / RH, None, ALU.mult))
        for e in range(RE):
            first = True
            for j in range(RE):
                if j == e:
                    continue
                op = ALU.is_ge if j < e else ALU.is_gt
                if first:
                    then(dve.tensor_tensor(rank[:, :, e], s[:, :, j], s[:, :, e], op))
                    first = False
                else:
                    then(dve.tensor_tensor(more[:, :], s[:, :, j], s[:, :, e], op))
                    then(dve.tensor_tensor(rank[:, :, e], rank[:, :, e], more[:, :], ALU.add))
        then(dve.tensor_scalar(rank[:, :, :], rank[:, :, :], 2.0, None, ALU.is_lt))
        then(dve.tensor_reduce(st[:, 3, :], s[:, :, :], AX.X, ALU.max))
        then(dve.tensor_tensor(s[:, :, :], s[:, :, :], col(3, RE), ALU.subtract))
        dve.wait_ge(act_ok, 2)
        then(dve.tensor_tensor(ex[:, :, :], ex[:, :, :], rank[:, :, :], ALU.mult))
        then(dve.tensor_reduce(st[:, 0, :], ex[:, :, :], AX.X, ALU.add))
        then(dve.reciprocal(st[:, 1, :], st[:, 0, :]))
        then(dve.tensor_tensor(gate[:, :].rearrange("p (t e) -> p t e", t=T), ex[:, :, :], col(1, RE), ALU.mult))

    def scalar(act):
        act.wait_ge(step, 7)
        act.activation(st[:, 2, :], st[:, 1, :], ACT.Sqrt).then_inc(act_ok, 1)
        act.wait_ge(step, 13 + RE * (1 + 2 * (RE - 2)) + 3)
        act.activation(ex[:, :, :], s[:, :, :], ACT.Exp).then_inc(act_ok, 1)

    return dict(sync=sync, vector=vector, scalar=scalar)


def program(nc, a, out, stop=99):
    ctx = ExitStack()
    with ctx:
        c = Chip(nc, ctx)
        bank = [ps(nc, ctx, f"bank{i}", [128, 512])[:, :] for i in range(8)]
        ident = sb(nc, ctx, "ident", [128, 128])
        ones = sb(nc, ctx, "ones", [128, 128])
        fold = sb(nc, ctx, "fold", [128, 32])
        X = sb(nc, ctx, "X", [P, T, D])
        col1, col2 = len_cols(a["src"], P), len_cols2(a["L1_ffn_edge_index"], 128)
        wide1, wide2 = -(-col1 // COLS) * COLS, -(-col2 // COLS) * COLS
        idx1 = sb(nc, ctx, "idx1", [P, wide1], I32)
        val1 = sb(nc, ctx, "val1", [P, wide1])
        idx2 = sb(nc, ctx, "idx2", [128, wide2], I32)
        val2 = sb(nc, ctx, "val2", [128, wide2])
        mats = [nc.dram_tensor(f"count{i}", [CELLS, 1], F32, kind="Internal").ap() for i in range(3)]
        feat = [[nc.dram_tensor(f"feat{s}{p}", [D, N], F16, kind="Internal").ap() for p in range(2)] for s in range(2)]
        x_in = c.sem("x_in")

        def load_x(sp):
            sp.dma_start(X[:, :, :], a["x"].rearrange("(t p) d -> p t d", p=P)).then_inc(x_in, 16)
            sp.wait_ge(x_in, 16)

        run_block(nc, c, setup_phase(c, ident, ones, fold), dict(sync=load_x))
        if stop <= 0:
            return store(nc, c, X, out)
        with ExitStack() as g:
            zero = sb(nc, g, "zero", [128, N])
            clear, cleared = clear_phase(c, mats, zero, ident, mats[2])
            with ExitStack() as e:
                e1, chosen1 = edges_phase(nc, c, e, "_m", a["src"], a["dst"], P, col1, idx1, val1, ident, ones, bank[4:6])
                e2, _ = edges_phase(nc, c, e, "_g", a["L1_ffn_edge_index"][0], a["L1_ffn_edge_index"][1], 128, col2,
                                    idx2, val2, ident, ones, bank[6:8])
                sc1 = scatter_phase(nc, c, e, "_m", mats[0:2], P, col1, idx1, val1, cleared[0:2], chosen1)
                run_block(nc, c, dict(sync=e1["sync"]), dict(sync=e2["sync"]), clear,
                          dict(gpsimd=e1["gpsimd"]), dict(gpsimd=e2["gpsimd"]),
                          dict(tensor=e1["tensor"], vector=e1["vector"]),
                          dict(tensor=e2["tensor"], vector=e2["vector"]), sc1)
        with ExitStack() as e:
            run_block(nc, c, bias_phase(nc, c, e, "_m", mats[0:2], mats[0]))

        def graph_layer(tag, H, w, biases, scale, resid, w_out, add_eps, side=None):
            with ExitStack() as g:
                V = sb(nc, g, f"values_{tag}", [P, T, D])
                with ExitStack() as e:
                    if H is None:
                        H = sb(nc, e, f"H{tag}", [P, T, D])
                        run_block(nc, c, norm_phase(nc, c, e, tag, resid, H, V))
                    run_block(nc, c, project_phase(nc, c, e, tag, H, *w, biases, scale, feat, V, ident, bank))
                with ExitStack() as e:
                    att = attention_phase(nc, c, e, tag, 8, 32, feat, None, mats[0], V, resid, w_out, add_eps,
                                          ident, fold, bank)
                    extra = side(e) if side else []
                    run_block(nc, c, att, *extra)

        graph_layer("0", None, (a["L0_gnn_Wk"], a["L0_gnn_Wq"], a["L0_gnn_Wv"]),
                    (a["L0_gnn_bk"], a["L0_gnn_bq"], a["L0_gnn_bv"]), -32 ** -0.5, X, None, None,
                    lambda e: [scatter_phase(nc, c, e, "_g", mats[2:3], 128, col2, idx2, val2, (), None)])
        if stop <= 3:
            return store(nc, c, X, out)

        with ExitStack() as g:
            swt = sb(nc, g, "swt", [128, SM, N])
            mix = sb(nc, g, "mix", [128, SM, D])
            with ExitStack() as e:
                token = sb(nc, e, "token", [128, SI])
                norm = sb(nc, e, "norm", [128, SM])
                with ExitStack() as f:
                    H = sb(nc, f, "Hs", [P, T, D])
                    with ExitStack() as f2:
                        run_block(nc, c, norm_phase(nc, c, f2, "s", X, H, sb(nc, f2, "scr_s", [P, T, D])))
                    run_block(nc, c, slice_phase(nc, c, f, "s", H, a, swt, token, norm, ident, ones, bank))
                with ExitStack() as f:
                    run_block(nc, c, token_phase(nc, c, f, a, token, norm, mix, ident, bank))
            with ExitStack() as e:
                run_block(nc, c, spread_phase(nc, c, e, a, swt, mix, X, bank))
        if stop <= 4:
            return store(nc, c, X, out)

        with ExitStack() as g:
            H = sb(nc, g, "H1", [P, T, D])
            with ExitStack() as e:
                run_block(nc, c, norm_phase(nc, c, e, "h", X, H, sb(nc, e, "scr_h", [P, T, D])))
            for l in range(2):
                graph_layer(f"{l + 1}", H, (a["L1_gnn_Wq"][l], a["L1_gnn_Wk"][l], a["L1_gnn_Wv"][l]), None,
                            -32 ** -0.5, H, a["L1_gnn_Wo"][l], 1e-9)
                with ExitStack() as e:
                    run_block(nc, c, norm_phase(nc, c, e, f"n{l}", H, H, sb(nc, e, f"scr_n{l}", [P, T, D]),
                                             a["L1_gnn_ln_g"][l], a["L1_gnn_ln_b"][l]))
            with ExitStack() as e:
                def one(v):
                    return v.rearrange("(o a) b -> o a b", o=1) if len(v.shape) == 2 else v.rearrange("(o a) -> o a", o=1)
                run_block(nc, c, ffn_phase(nc, c, e, "_d", H, X, one(a["L1_gnn_w1"]), one(a["L1_gnn_b1"]), one(a["L1_gnn_w2"]),
                                        one(a["L1_gnn_b2"]), ACT.Relu, 1, 1024, None, ident, bank))
        if stop <= 5:
            return store(nc, c, X, out)

        with ExitStack() as g:
            gate = sb(nc, g, "gate", [P, T * RE])
            agg = sb(nc, g, "agg_r", [P, T, RF])
            with ExitStack() as e:
                run_block(nc, c, bias_phase(nc, c, e, "_g", mats[2:3], mats[2]))
            with ExitStack() as e:
                vpad = sb(nc, e, "vpad", [P, T, RH, 32])
                nas = sb(nc, e, "nas", [128, RH, N])
                nad = sb(nc, e, "nad", [P, T * RH])
                nad5 = sb(nc, e, "nad5", [P, T * RH])
                with ExitStack() as f:
                    H = sb(nc, f, "H2", [P, T, D])
                    with ExitStack() as f2:
                        run_block(nc, c, norm_phase(nc, c, f2, "r", X, H, sb(nc, f2, "scr_r", [P, T, D])))
                    run_block(nc, c, router_phase(nc, c, f, H, a, vpad, nas, nad, nad5, ident, bank))
                with ExitStack() as f:
                    vv = vpad[:, :, :, :].rearrange("p t h e -> p t (h e)")
                    run_block(nc, c, attention_phase(nc, c, f, "r", RH, RE, None, (nas, nad5, nad), mats[2], vv, agg,
                                                  None, 1e-16, ident, fold, bank))
                with ExitStack() as f:
                    run_block(nc, c, gate_phase(nc, c, f, a, agg, gate))
            with ExitStack() as e:
                H = sb(nc, e, "H3", [P, T, D])
                with ExitStack() as f:
                    run_block(nc, c, norm_phase(nc, c, f, "x", X, H, sb(nc, f, "scr_x", [P, T, D])))
                run_block(nc, c, ffn_phase(nc, c, e, "_x", H, X, a["L1_ffn_W1"], a["L1_ffn_b1"], a["L1_ffn_W2"],
                                        a["L1_ffn_b2"], ACT.Gelu, RE, 512, gate, ident, bank))
        store(nc, c, X, out)


def len_cols(v, lanes):
    return v.shape[0] // lanes


def len_cols2(v, lanes):
    return v.shape[1] // lanes


def store(nc, c, X, out):
    done = c.sem("done")

    def sync(sp):
        sp.dma_start(out.rearrange("(t p) d -> p t d", p=P), X[:, :, :]).then_inc(done, 16)
        sp.wait_ge(done, 16)

    run_block(nc, c, dict(sync=sync))


def kernel(**inputs):
    import numpy as _np
    import concourse.bacc as _bacc
    from concourse import mybir as _mybir
    from concourse.bass_utils import run_bass_kernel_spmd as _run

    nc = _bacc.Bacc("TRN2", target_bir_lowering=False, num_devices=1)
    arrays, args = {}, {}
    for name, value in inputs.items():
        array = _np.ascontiguousarray(value)
        arrays[f"in_{name}"] = array
        args[name] = nc.dram_tensor(f"in_{name}", array.shape, _mybir.dt.from_np(array.dtype), kind="ExternalInput").ap()
    out = nc.dram_tensor("out_x", (N, D), F32, kind="ExternalOutput").ap()
    program(nc, args, out)
    r = _run(nc, [arrays], core_ids=[0])
    return r.results[0]["out_x"]
```

```python
from contextlib import ExitStack

import numpy as np

import concourse.bass as bass
from concourse import mybir

F32 = mybir.dt.float32
F16 = mybir.dt.float16
I32 = mybir.dt.int32
ALU = mybir.AluOpType
ACT = mybir.ActivationFunctionType
AX = mybir.AxisListType

N = 3125
P = 125
T = N // P
D = 256
KD = D // 128
G = 5
GT = T // G
GN = GT * P
SPLIT = ((0, 3 * P), (3 * P, GN))
NN = N * N
CELLS = 128 * N * T
LOWER = 1024.0
FAR = 1e30
EMPTY = 1e20
LN_EPS = 1e-5

GROUPS = tuple(tuple(range(4 * j, min(4 * j + 4, T))) for j in range(7))
GROUP_COLS = tuple((4 * P * j, min(4 * P * (j + 1), N)) for j in range(7))
LAST = len(GROUPS) - 1
BIAS_COLS = ((0, 1000), (1000, 2000), (2000, 3000), (3000, N))
EXP_COLS = ((0, 1000), (1000, 2000), (2000, N))
EXP_NEED = {0: 0, 2: 1, 4: 2}
EXP_AT = (1, 3, 6)
ON_ACT = (0, 2, 4, 5, 6)
ON_DVE = (1, 3)
ON_ACT_GAT, ON_DVE_GAT = tuple(range(7)), ()
DMA_ROWS = ((0, 112), (112, P))
FLAGS_AT = tuple((2, j) for j in range(6))
LOG_AT = (3, 1)


def run_block(nc, c, *phases):
    with nc.Block() as block:
        @block.sync
        def _(sp):
            for ph in phases:
                if "sync" in ph:
                    ph["sync"](sp)

        @block.scalar
        def _(act):
            for ph in phases:
                if "scalar" in ph:
                    ph["scalar"](act)

        @block.vector
        def _(dve):
            for ph in phases:
                if "vector" in ph:
                    ph["vector"](dve)

        @block.tensor
        def _(pe):
            for ph in phases:
                if "tensor" in ph:
                    ph["tensor"](pe)

        @block.gpsimd
        def _(pool):
            for ph in phases:
                if "gpsimd" in ph:
                    ph["gpsimd"](pool)
    c.clear()


def wait_from(eng, sem, value):
    if not (isinstance(value, int) and value <= 0):
        eng.wait_ge(sem, value)


def peeled(eng, n, body):
    body(0)
    with eng.Fori(1, n) as i:
        body(i)


def wait_apart(eng, sem, value, passed):
    if isinstance(value, int) and value <= 0:
        return
    eng.wait_ge(sem, value)
    eng.sem_inc(passed, 1)


class Chip:

    def __init__(self, nc, ctx):
        self.nc, self.ctx, self.sems = nc, ctx, []

    def sem(self, name):
        self.sems.append(self.nc.alloc_semaphore(name))
        return self.sems[-1]

    def clear(self):
        self.nc.clear_and_free_semaphores(self.sems)
        self.nc.all_engine_barrier()
        self.sems = []


def sb(nc, ctx, name, shape, dt=F32):
    return ctx.enter_context(nc.sbuf_tensor(name, shape, dt))


def ps(nc, ctx, name, shape):
    return ctx.enter_context(nc.psum_tensor(name, shape, F32))


def rows(ap, n):
    return ap.rearrange("(o n) -> o n", o=1).to_broadcast([n, ap.shape[0]])


def setup_phase(c, ident, ones, fold):
    zeroed, made = c.sem("zeroed"), c.sem("made")

    def gpsimd(pool):
        pool.memset(ident[:, :], 0.0).then_inc(zeroed, 1)
        pool.memset(fold[:, :], 0.0).then_inc(zeroed, 1)
        pool.memset(ones[:, :], 1.0).then_inc(zeroed, 1)
        pool.wait_ge(zeroed, 3)
        pool.affine_select(out=ident[:, :], in_=ident[:, :], compare_op=ALU.not_equal, fill=1.0, base=0,
                           pattern=[[-1, 128]], channel_multiplier=1).then_inc(made, 1)
        for q in range(4):
            pool.wait_ge(made, q + 1)
            pool.affine_select(out=fold[:, :], in_=fold[:, :], compare_op=ALU.not_equal, fill=1.0,
                               base=-32 * q, pattern=[[-1, 32]], channel_multiplier=1).then_inc(made, 1)

    return dict(gpsimd=gpsimd)


COLS = 6
TURNS = 2


def round_up(cols):
    return -(-cols // (COLS * TURNS)) * COLS * TURNS


def clear_phase(c, mats, zero, ident, diag_of):
    zset, looped = c.sem("zset"), c.sem("looped")
    cleared = [c.sem(f"cleared{i}") for i in range(len(mats))]

    def vector(dve):
        dve.memset(zero[:, :], 0.0).then_inc(zset, 1)

    def sync(sp):
        sp.wait_ge(zset, 1)
        for i, m in enumerate(mats):
            v = m.rearrange("(t p n) o -> t p (n o)", p=128, n=N)
            with sp.Fori(0, T) as t:
                sp.dma_start(v[t], zero[:, :]).then_inc(cleared[i], 16)
            if m is diag_of:
                sp.wait_ge(cleared[i], 16 * T)
                w = m[0:NN, :].rearrange("(r n) o -> r (n o)", n=N)
                for t in range(T):
                    sp.dma_start(w[t * P:(t + 1) * P, t * P:(t + 1) * P], ident[0:P, 0:P]).then_inc(looped, 16)
        sp.wait_ge(looped, 16 * T)

    return dict(vector=vector, sync=sync), cleared


def edges_phase(nc, c, ctx, tag, src, dst, lanes, cols, idx_all, val_all, ident, ones, psk):
    wide = round_up(cols)
    turns = wide // COLS
    raw = sb(nc, ctx, f"raw{tag}", [lanes, 2, cols], I32)
    num = sb(nc, ctx, f"num{tag}", [lanes, 2, cols])
    key = sb(nc, ctx, f"key{tag}", [lanes, wide])
    weight = sb(nc, ctx, f"weight{tag}", [lanes, lanes])
    spare = sb(nc, ctx, f"spare{tag}", [lanes, 1])
    diag = sb(nc, ctx, f"diag{tag}", [lanes, COLS, lanes])
    junk = sb(nc, ctx, f"junk{tag}", [lanes, lanes])
    same = sb(nc, ctx, f"same{tag}", [lanes, COLS])
    lost = sb(nc, ctx, f"lost{tag}", [lanes, COLS])
    loaded, spared, weighed = c.sem(f"loaded{tag}"), c.sem(f"spared{tag}"), c.sem(f"weighed{tag}")
    keyed, diags, spread = c.sem(f"keyed{tag}"), c.sem(f"diags{tag}"), c.sem(f"spread{tag}")
    counted, chosen = c.sem(f"counted{tag}"), c.sem(f"chosen{tag}")
    half = COLS // 2

    def sync(sp):
        sp.dma_start(raw[:, 0, :], src.rearrange("(p c) -> p c", p=lanes)).then_inc(loaded, 16)
        sp.dma_start(raw[:, 1, :], dst.rearrange("(p c) -> p c", p=lanes)).then_inc(loaded, 16)

    def gpsimd(pool):
        pool.iota(spare[:, :], pattern=[[0, 1]], base=NN, channel_multiplier=1,
                  allow_small_or_imprecise_dtypes=True).then_inc(spared, 1)
        pool.memset(weight[:, :], 1.0).then_inc(spared, 1)
        pool.wait_ge(spared, 2)
        pool.affine_select(out=weight[:, :], in_=weight[:, :], compare_op=ALU.is_ge, fill=1.0 + LOWER, base=0,
                           pattern=[[1, lanes]], channel_multiplier=-1).then_inc(weighed, 1)

    def vector(dve):
        dve.wait_ge(loaded, 32)
        dve.wait_ge(weighed, 1)
        dve.tensor_copy(num[:, :, :], raw[:, :, :]).then_inc(keyed, 1)
        dve.wait_ge(keyed, 1)
        dve.scalar_tensor_tensor(out=key[:, 0:cols], in0=num[:, 1, :], scalar=float(N), in1=num[:, 0, :],
                                 op0=ALU.mult, op1=ALU.add).then_inc(keyed, 1)
        if wide > cols:
            dve.tensor_scalar(key[:, cols:wide], spare[:, 0:1].to_broadcast([lanes, wide - cols]), 0.0, None,
                              ALU.add).then_inc(keyed, 1)
        dve.wait_ge(keyed, 2 + (wide > cols))
        def turn(i):
            for u in range(COLS):
                if u % half == 0:
                    wait_from(dve, spread, 2 * i)
                dve.tensor_scalar(diag[:, u, :], ident[0:lanes, 0:lanes], key[:, bass.ds(i * COLS + u, 1)], None,
                                  ALU.mult).then_inc(diags, 1)
            for u in range(COLS):
                if u % half == 0:
                    dve.wait_ge(spread, 2 * i + u // half + 1)
                dve.scalar_tensor_tensor(out=junk[:, :], in0=psk[u // half][0:lanes, (u % half) * lanes:(u % half + 1) * lanes],
                                         scalar=key[:, bass.ds(i * COLS + u, 1)], in1=weight[:, :],
                                         op0=ALU.is_equal, op1=ALU.mult, accum_out=same[:, u:u + 1]).then_inc(counted, 1)
                dve.wait_ge(counted, COLS * i + u + 1)
            dve.tensor_scalar(lost[:, :], same[:, :], LOWER, spare[:, 0:1], ALU.is_ge, ALU.mult).then_inc(chosen, 1)
            dve.tensor_copy(val_all[0:lanes, bass.ds(i * COLS, COLS)], same[:, :]).then_inc(chosen, 1)
            dve.wait_ge(chosen, 3 * i + 2)
            dve.tensor_tensor(idx_all[0:lanes, bass.ds(i * COLS, COLS)], lost[:, :],
                              key[:, bass.ds(i * COLS, COLS)], ALU.max).then_inc(chosen, 1)
            dve.wait_ge(chosen, 3 * i + 3)

        peeled(dve, turns, turn)

    def tensor(pe):
        def turn(i):
            for b in range(2):
                pe.wait_ge(diags, COLS * i + (b + 1) * half)
                if b == 0:
                    wait_from(pe, counted, COLS * i)
                pe.matmul(psk[b][0:lanes, 0:half * lanes], ones[0:lanes, 0:lanes],
                          diag[:, b * half:(b + 1) * half, :].rearrange("p u n -> p (u n)"),
                          start=True, stop=True).then_inc(spread, 1)

        peeled(pe, turns, turn)

    return dict(sync=sync, gpsimd=gpsimd, vector=vector, tensor=tensor), chosen


def scatter_phase(nc, c, ctx, tag, mats, lanes, cols, idx_all, val_all, cleared, chosen):
    turns = round_up(cols) // (COLS * TURNS)
    M = len(mats)
    slot_idx = sb(nc, ctx, f"slot_idx{tag}", [lanes, TURNS, COLS], I32)
    slot_val = sb(nc, ctx, f"slot_val{tag}", [lanes, TURNS, COLS])
    staged, passed = c.sem(f"staged{tag}"), c.sem(f"passed{tag}")
    landed = [c.sem(f"landed{tag}{m}") for m in range(M)]

    def stage(pool, i, r):
        at = bass.ds((i * TURNS + r) * COLS, COLS)
        if chosen is not None:
            pool.wait_ge(chosen, 3 * (TURNS * i + r) + 3)
        for m in range(M):
            wait_from(pool, landed[m], 16 * (COLS // M) * (TURNS * (i - 1) + r + 1))
        pool.tensor_copy(slot_idx[:, r, :], idx_all[0:lanes, at]).then_inc(staged, 1)
        pool.tensor_copy(slot_val[:, r, :], val_all[0:lanes, at]).then_inc(staged, 1)

    def gpsimd(pool):
        for clear in cleared:
            pool.wait_ge(clear, 16 * T)
        def turn(i):
            for r in range(TURNS):
                stage(pool, i, r)
                wait_apart(pool, staged, 2 * (TURNS * i + r + 1), passed)
                for u in range(COLS):
                    n = r * COLS + u
                    wait_apart(pool, landed[n % M], 16 * (COLS * TURNS // M * i + n // M), passed)
                    pool.indirect_dma_start(mats[n % M], bass.IndirectOffsetOnAxis(ap=slot_idx[:, r, u:u + 1], axis=0),
                                            slot_val[:, r, u:u + 1], None, compute_op=ALU.add).then_inc(landed[n % M], 16)

        peeled(pool, turns, turn)
        for m in range(M):
            pool.wait_ge(landed[m], 16 * turns * TURNS * COLS // M)

    return dict(gpsimd=gpsimd)


def bias_phase(nc, c, ctx, tag, counts):
    BUFS = 3
    cnt = sb(nc, ctx, f"cnt{tag}", [128, BUFS, N])
    none = sb(nc, ctx, f"none{tag}", [128, BUFS, N])
    loaded = [c.sem(f"cnt_in{tag}{b}") for b in range(BUFS)]
    fixed, logged, biased = (c.sem(f"{x}{tag}") for x in ("fixed", "logged", "biased"))
    stored = [c.sem(f"stored{tag}{b}") for b in range(BUFS)]
    view = counts.rearrange("(t p n) o -> t p (n o)", p=128, n=N)

    def sync(sp):
        for t in range(T):
            if t >= BUFS:
                sp.wait_ge(biased, t - BUFS + 1)
            sp.dma_start(cnt[:, t % BUFS, :], view[t]).then_inc(loaded[t % BUFS], 16)

    def vector(dve):
        def flags(t):
            b = t % BUFS
            dve.wait_ge(loaded[b], 16 * (t // BUFS + 1))
            if t >= BUFS:
                dve.wait_ge(stored[b], 16 * (t // BUFS))
            dve.tensor_scalar(none[:, b, :], cnt[:, b, :], 0.5, FAR, ALU.is_lt, ALU.mult).then_inc(fixed, 1)
            dve.tensor_scalar(cnt[:, b, :], cnt[:, b, :], 1.0, None, ALU.max).then_inc(fixed, 1)

        flags(0)
        for t in range(T):
            if t + 1 < T:
                flags(t + 1)
            dve.wait_ge(logged, t + 1)
            b = t % BUFS
            dve.tensor_tensor(none[:, b, :], none[:, b, :], cnt[:, b, :], ALU.subtract).then_inc(biased, 1)

    def scalar(act):
        def store(t):
            act.wait_ge(biased, t + 1)
            act.dma_start(view[t], none[:, t % BUFS, :]).then_inc(stored[t % BUFS], 16)

        for t in range(T):
            act.wait_ge(fixed, 2 * (t + 1))
            act.activation(cnt[:, t % BUFS, :], cnt[:, t % BUFS, :], ACT.Ln).then_inc(logged, 1)
            if t >= 1:
                store(t - 1)
        store(T - 1)
        for b in range(BUFS):
            act.wait_ge(stored[b], 16 * len(range(b, T, BUFS)))

    return dict(sync=sync, vector=vector, scalar=scalar)


def norm_phase(nc, c, ctx, tag, x, h, scratch, gamma=None, beta=None, shared=True):
    parts = ((0, 9), (9, 17), (17, T))
    own = parts[:2] if shared else parts
    st = sb(nc, ctx, f"stats{tag}", [P, 3, T])
    gb = sb(nc, ctx, f"gb{tag}", [P, 2, D]) if gamma is not None else None
    (total, centred, centred_pool, squared, summed, scaled, root, recip, out, out_pool, gin) = (
        c.sem(f"{v}{tag}") for v in ("ln_total", "ln_cent", "ln_centp", "ln_sq", "ln_sum", "ln_scale", "ln_root",
                                     "ln_recip", "ln_out", "ln_outp", "ln_gb"))
    steps = 1 if gamma is None else 3

    def wide(row, lo, hi):
        return st[:, row, lo:hi].unsqueeze(2).to_broadcast([P, hi - lo, D])

    def centre(eng, lo, hi, done):
        eng.tensor_tensor(h[:, lo:hi, :], x[:, lo:hi, :], wide(1, lo, hi), ALU.subtract).then_inc(done, 1)

    def finish(eng, lo, hi, done):
        eng.wait_ge(recip, 1)
        eng.tensor_tensor(h[:, lo:hi, :], h[:, lo:hi, :], wide(2, lo, hi), ALU.mult).then_inc(done, 1)
        if gamma is not None:
            eng.wait_ge(gin, 32)
            for k, op in ((0, ALU.mult), (1, ALU.add)):
                eng.wait_ge(done, k + 1)
                eng.tensor_tensor(h[:, lo:hi, :], h[:, lo:hi, :],
                                  gb[:, k, :].unsqueeze(1).to_broadcast([P, hi - lo, D]), op).then_inc(done, 1)

    def sync(sp):
        if gamma is not None:
            sp.dma_start(gb[:, 0, :], rows(gamma, P)).then_inc(gin, 16)
            sp.dma_start(gb[:, 1, :], rows(beta, P)).then_inc(gin, 16)

    def vector(dve):
        dve.tensor_reduce(st[:, 0, :], x[:, :, :], AX.X, ALU.add).then_inc(total, 1)
        dve.wait_ge(total, 1)
        dve.tensor_scalar(st[:, 1, :], st[:, 0, :], 1.0 / D, None, ALU.mult).then_inc(total, 1)
        dve.wait_ge(total, 2)
        for lo, hi in own:
            centre(dve, lo, hi, centred)
        for i, (lo, hi) in enumerate(parts):
            dve.wait_ge(squared, i + 1)
            dve.tensor_reduce(st[:, 0, lo:hi], scratch[:, lo:hi, :], AX.X, ALU.add).then_inc(summed, 1)
        dve.wait_ge(summed, 3)
        dve.tensor_scalar(st[:, 2, :], st[:, 0, :], 1.0 / D, LN_EPS, ALU.mult, ALU.add).then_inc(scaled, 1)
        dve.wait_ge(root, 1)
        dve.reciprocal(st[:, 2, :], st[:, 0, :]).then_inc(recip, 1)
        finish(dve, 0, own[-1][1], out)
        dve.wait_ge(out, steps)

    def gpsimd(pool):
        if shared:
            pool.wait_ge(total, 2)
            centre(pool, *parts[2], centred_pool)
            finish(pool, *parts[2], out_pool)
            pool.wait_ge(out_pool, steps)

    def scalar(act):
        for i, (lo, hi) in enumerate(parts):
            if i < len(own):
                act.wait_ge(centred, i + 1)
            else:
                act.wait_ge(centred_pool, 1)
            act.activation(scratch[:, lo:hi, :], h[:, lo:hi, :], ACT.Square).then_inc(squared, 1)
        act.wait_ge(scaled, 1)
        act.activation(st[:, 0, :], st[:, 2, :], ACT.Sqrt).then_inc(root, 1)

    return dict(sync=sync, vector=vector, scalar=scalar, gpsimd=gpsimd), (out, steps)


def transpose_group(pe, hs, bank, ident, turned):
    for k in range(KD):
        for s, (lo, hi) in enumerate(SPLIT):
            for j in range(lo // P, hi // P):
                mm = pe.transpose(bank[2 * k + s][:, j * P - lo:(j + 1) * P - lo], hs[0:P, j, k * 128:(k + 1) * 128],
                                  ident[0:P, 0:P])
            mm.then_inc(turned, 1)


def project_phase(nc, c, ctx, tag, h, w_dst, w_src, w_val, biases, scale, feat, v, ident, bank, ready=None,
                  stager="gpsimd"):
    w = sb(nc, ctx, f"w{tag}", [128, 3, KD, D])
    bcol = sb(nc, ctx, f"bcol{tag}", [128, 2, KD])
    brow = sb(nc, ctx, f"brow{tag}", [P, D])
    hs = sb(nc, ctx, f"hs{tag}", [P, GT, D])
    ht = sb(nc, ctx, f"ht{tag}", [128, KD, GN])
    full = sb(nc, ctx, f"full{tag}", [128, 2, GN])
    part = sb(nc, ctx, f"part{tag}", [128, 4, 2, GN], F16)
    (win, staged, turned, ht_ok, q_mm, v_mm, q_full, q_high, q_low, v_out, kept, bcol_ok) = (
        c.sem(f"{x}{tag}") for x in ("p_w", "p_stage", "p_turn", "p_ht", "p_q", "p_v", "p_full", "p_high", "p_low",
                                     "p_vout", "p_kept", "p_bcol"))
    nw = 3 + (3 if biases else 0)
    vbank = (0, 1, 2, 3, 0)

    def sync(sp):
        for i, wt in enumerate((w_dst, w_src, w_val)):
            sp.dma_start(w[:, i, :, :], wt.rearrange("(k p) n -> p k n", p=128)).then_inc(win, 16)
        if biases:
            for i in range(2):
                with nc.allow_non_contiguous_dma(reason="256 bias values, once"):
                    sp.dma_start(bcol[:, i, :], biases[i].rearrange("(k p) -> p k", p=128)).then_inc(win, 16)
            sp.dma_start(brow[:, :], rows(biases[2], P)).then_inc(win, 16)
        def group(g):
            for q in range(4):
                sp.wait_ge(q_low, 4 * g + q + 1)
                sp.wait_ge(q_high, 4 * g + q + 1)
                for hl in range(2):
                    sp.dma_start(feat[q // 2][hl][(q % 2) * 128:(q % 2 + 1) * 128, bass.ds(g * GN, GN)],
                                 part[:, q, hl, :]).then_inc(kept, 16)

        peeled(sp, G, group)
        sp.wait_ge(kept, 16 * 8 * G)

    def stage(eng, copy, g):
        wait_from(eng, turned, 4 * g)
        for j in range(GT):
            copy(hs[:, j, :], h[:, bass.ds(g * GT + j, 1), :].rearrange("p o n -> p (o n)")).then_inc(staged, 1)

    def gpsimd(pool):
        if stager == "gpsimd":
            if ready:
                pool.wait_ge(*ready)
            peeled(pool, G, lambda g: stage(pool, pool.tensor_copy, g))

    def tensor(pe):
        pe.wait_ge(win, 16 * nw)
        def group(g):
            pe.wait_ge(staged, GT * (g + 1))
            wait_from(pe, v_out, GT * g)
            transpose_group(pe, hs, bank, ident, turned)
            pe.wait_ge(ht_ok, 4 * (g + 1))
            for q in range(4):
                for s, (lo, hi) in enumerate(SPLIT):
                    b = 4 + 2 * (q % 2) + s
                    if q >= 2:
                        wait_from(pe, q_full, 8 * g + 2 * (q - 2) + s + 1)
                    elif s == 0:
                        wait_from(pe, q_full, 8 * g)
                    for k in range(KD):
                        mm = pe.matmul(bank[b][:, 0:hi - lo], w[:, q // 2, k, (q % 2) * 128:(q % 2 + 1) * 128],
                                       ht[:, k, lo:hi], start=(k == 0), stop=(k == KD - 1))
                    mm.then_inc(q_mm, 1)
            for j in range(GT):
                if j == 4:
                    pe.wait_ge(v_out, GT * g + 1)
                for k in range(KD):
                    mm = pe.matmul(bank[vbank[j]][0:P, 0:D], ht[:, k, j * P:(j + 1) * P], w[:, 2, k, :],
                                   start=(k == 0), stop=(k == KD - 1))
                mm.then_inc(v_mm, 1)

        peeled(pe, G, group)

    def scalar(act):
        if biases:
            act.wait_ge(win, 16 * nw)
            act.mul(bcol[:, 0, :], bcol[:, 0, :], scale).then_inc(bcol_ok, 1)
            act.wait_ge(bcol_ok, 1)
        if stager == "scalar" and ready:
            act.wait_ge(*ready)

        def group(g):
            if stager == "scalar":
                stage(act, act.copy, g)
            wait_from(act, v_mm, GT * g)
            for k in range(KD):
                for s, (lo, hi) in enumerate(SPLIT):
                    act.wait_ge(turned, 4 * g + 2 * k + s + 1)
                    act.copy(ht[:, k, lo:hi], bank[2 * k + s][:, 0:hi - lo]).then_inc(ht_ok, 1)
            for q in range(4):
                for s, (lo, hi) in enumerate(SPLIT):
                    act.wait_ge(q_mm, 8 * g + 2 * q + s + 1)
                    if s == 0:
                        wait_from(act, q_low, (4 * g + q - 1) if q >= 1 else 4 * g)
                    src = bank[4 + 2 * (q % 2) + s][:, 0:hi - lo]
                    sc = scale if q < 2 else 1.0
                    act.activation(full[:, q % 2, lo:hi], src, ACT.Identity, scale=sc,
                                   bias=bcol[:, q // 2, q % 2:q % 2 + 1] if biases else 0.0).then_inc(q_full, 1)

        peeled(act, G, group)

    def vector(dve):
        if biases:
            dve.wait_ge(win, 16 * nw)
        def group(g):
            for q in range(4):
                dve.wait_ge(q_full, 8 * g + 2 * q + 2)
                if q == 0:
                    wait_from(dve, kept, 128 * g)
                dve.tensor_copy(part[:, q, 0, :], full[:, q % 2, :]).then_inc(q_high, 1)
                dve.wait_ge(q_high, 4 * g + q + 1)
                dve.tensor_tensor(part[:, q, 1, :], full[:, q % 2, :], part[:, q, 0, :], ALU.subtract).then_inc(q_low, 1)
            for j in range(GT):
                dve.wait_ge(v_mm, GT * g + j + 1)
                out = v[0:P, bass.ds(g * GT + j, 1), :].rearrange("p o n -> p (o n)")
                if biases:
                    dve.tensor_tensor(out, bank[vbank[j]][0:P, 0:D], brow[:, :], ALU.add).then_inc(v_out, 1)
                else:
                    dve.tensor_copy(out, bank[vbank[j]][0:P, 0:D]).then_inc(v_out, 1)

        peeled(dve, G, group)

    return dict(sync=sync, gpsimd=gpsimd, tensor=tensor, scalar=scalar, vector=vector)


def attention_phase(nc, c, ctx, tag, heads, width, feat, gat, bias, v, resid, w_out, add_eps, ident, fold, bank,
                    counts=None):
    H = heads
    dot = feat is not None
    pieces = GROUP_COLS if dot else EXP_COLS
    NC = len(pieces)
    NE = len(EXP_COLS)
    on_act, on_dve = (ON_ACT, ON_DVE) if dot else (ON_ACT_GAT, ON_DVE_GAT)
    s_bank, t_bank, o_bank = bank[0:3], bank[3:6], bank[6:8]
    slots = 4
    S = sb(nc, ctx, f"S{tag}", [P, slots, N])
    B = sb(nc, ctx, f"B{tag}", [P, N])
    PT = sb(nc, ctx, f"PT{tag}", [P, 3, 4 * P])
    PTL = sb(nc, ctx, f"PTL{tag}", [P, 2, P])
    O4 = sb(nc, ctx, f"O4{tag}", [128, 2, P])
    low = sb(nc, ctx, f"low{tag}", [P, H, NC])
    least = sb(nc, ctx, f"least{tag}", [P, H])
    z = sb(nc, ctx, f"z{tag}", [P, H, NE])
    rz = sb(nc, ctx, f"rz{tag}", [P, 3, H])
    agg = sb(nc, ctx, f"agg{tag}", [P, H * width])
    names = ("a_in", "a_dA", "a_dB", "a_qk", "a_red", "a_least", "a_exp", "a_turn", "a_evA", "a_evD", "a_pv", "a_o",
             "a_fold", "a_small", "a_fin", "a_aggT", "a_aggC", "a_wo", "a_res", "a_fifth", "a_sum", "a_row", "a_passed",
             "a_went")
    (a_in, d_a, d_b, s_qk, s_red, s_least, s_exp, s_turn, s_evA, s_evD, s_pv, s_o,
     s_fold, s_small, s_fin, s_aggT, s_aggC, s_wo, s_res, s_fifth, s_sum, s_row, s_passed,
     s_went) = (
        c.sem(f"{x}{tag}") for x in names)
    b_in = [c.sem(f"a_b{i}{tag}") for i in range(len(BIAS_COLS))]
    biasv = bias[0:NN, :].rearrange("(t p n) o -> t p (n o)", p=P, n=N)
    HH = H // 2
    b_free = (2, 4, 6, 7) if dot else (1, 2, 3, 3)
    b_need = {0: (0,), 2: (1,), 4: (2,), 6: (3,)} if dot else {0: (0,), 1: (1,), 2: (2, 3)}
    if dot:
        A = sb(nc, ctx, f"A{tag}", [128, H, N], F16)
        Dt = sb(nc, ctx, f"Dt{tag}", [128, H, P], F16)
        fd = [f.rearrange("(h d) n -> d h n", d=32) for f in feat[0]]
        fs = [f.rearrange("(h d) n -> d h n", d=32) for f in feat[1]]
    else:
        nas, nad = gat
        T5 = sb(nc, ctx, f"T5{tag}", [P, 2, N])
        row = sb(nc, ctx, f"row{tag}", [P, H])
    if counts:
        C = sb(nc, ctx, f"C{tag}", [P, 2, N])
        c_in, c_sum, c_flag, c_log, c_bias, c_out, c_went = (
            c.sem(f"{x}{tag}") for x in ("c_in", "c_sum", "c_flag", "c_log", "c_bias", "c_out", "c_went"))
        countv = [m[0:NN, :].rearrange("(t p n) o -> t p (n o)", p=P, n=N) for m in counts]
    if w_out is not None:
        wo = sb(nc, ctx, f"wo{tag}", [128, KD, D])
        aggT = sb(nc, ctx, f"aggT{tag}", [128, KD, P])

    def before(t, h, n=1):
        return (t, h - n) if h >= n else (t - 1, h - n + H)

    def behind(t, h, n):
        return (t, h + n) if h + n < H else (t + 1, h + n - H)

    def dst_half(sp, t, half):
        for r in range(4):
            with nc.allow_non_contiguous_dma(reason="125 float16 of a row"):
                sp.dma_start(Dt[32 * r:32 * r + 32, half * HH:(half + 1) * HH, :],
                             fd[r // 2][:, half * HH:(half + 1) * HH, bass.ds(t * P, P)]).then_inc((d_a, d_b)[half], 16)

    def bias_part(sp, t, i):
        lo, hi = BIAS_COLS[i]
        for r0, r1 in DMA_ROWS:
            sp.dma_start(B[r0:r1, lo:hi], biasv[t][r0:r1, lo:hi]).then_inc(b_in[i], 16)

    def load_counts(sp, n):
        for m in range(2):
            for r0, r1 in DMA_ROWS:
                sp.dma_start(C[r0:r1, m, :], countv[m][n][r0:r1, :]).then_inc(c_in, 16)

    def store_bias(sp, n):
        for i, (lo, hi) in enumerate(EXP_COLS):
            sp.wait_ge(c_bias, 3 * n + i + 1)
            for r0, r1 in DMA_ROWS:
                sp.dma_start(biasv[n][r0:r1, lo:hi], C[r0:r1, 1, lo:hi]).then_inc(c_out, 16)
        sp.wait_ge(c_out, 96 * (n + 1))

    def sync(sp):
        if counts:
            load_counts(sp, 0)
        if w_out is not None:
            sp.dma_start(wo[:, :, :], w_out.rearrange("(k p) n -> p k n", p=128)).then_inc(a_in, 16)
        if dot:
            for r in range(4):
                sp.dma_start(A[32 * r:32 * r + 32, :, :], fs[r % 2]).then_inc(a_in, 16)
            for half in range(2):
                dst_half(sp, 0, half)
        if counts:
            store_bias(sp, 0)
        for i in range(len(BIAS_COLS)):
            bias_part(sp, 0, i)
        if counts:
            load_counts(sp, 1)
        def next_half(t, half):
            if dot:
                sp.wait_ge(s_qk, NC * (H * t + (half + 1) * HH))
                dst_half(sp, t + 1, half)

        def next_tile(t, last=False):
            next_half(t, 0)
            if counts:
                store_bias(sp, t + 1)
            for i in range(len(BIAS_COLS)):
                sp.wait_ge(s_red, NC * (H * t + H - 1) + b_free[i])
                bias_part(sp, t + 1, i)
            if counts and not last:
                load_counts(sp, t + 2)
            next_half(t, 1)

        with sp.Fori(0, T - 2) as t:
            next_tile(t)
        next_tile(T - 2, last=True)

    def tensor(pe):
        if dot or w_out is not None:
            pe.wait_ge(a_in, 16 * ((4 if dot else 0) + (w_out is not None)))

        def scores(t, h, j, first=False):
            if not dot:
                return
            k = H * t + h
            if j == 0 and h == 0:
                pe.wait_ge(d_a, 64 * (t + 1))
            if j == 0 and h == HH:
                pe.wait_ge(d_b, 64 * (t + 1))
            if j >= 3:
                pe.wait_ge(s_red, NC * k + j - 2)
            elif not first:
                pe.wait_ge(s_red, NC * (k - 1) + (LAST, 4, 5)[j] + 1)
            lo, hi = GROUP_COLS[j]
            pe.matmul(s_bank[j % 3][0:P, 0:hi - lo], Dt[:, h, :], A[:, h, lo:hi], start=True,
                      stop=True).then_inc(s_qk, 1)

        def copied(t, h, j):
            k = H * t + h
            if j in on_act:
                pe.wait_ge(s_evA, len(on_act) * k + on_act.index(j) + 1)
            else:
                pe.wait_ge(s_evD, len(on_dve) * k + on_dve.index(j) + 1)

        def turn(t, h, j, first):
            k = H * t + h
            if j in EXP_NEED:
                pe.wait_ge(s_exp, NE * k + EXP_NEED[j] + 1)
            if j >= 3:
                copied(t, h, j - 3)
            elif not first:
                copied(*before(t, h), (LAST, 4, 5)[j])
            for i, s in enumerate(GROUPS[j]):
                mm = pe.transpose(t_bank[j % 3][0:P, i * P:(i + 1) * P], S[0:P, h % slots, s * P:(s + 1) * P],
                                  ident[0:P, 0:P])
            mm.then_inc(s_turn, 1)

        def weigh(t, h, j, first):
            k = H * t + h
            if j == 0 and not (first and h < 2):
                pe.wait_ge(s_fin, k - 1)
            copied(t, h, j)
            for i, s in enumerate(GROUPS[j]):
                w = PT[0:P, j % 3, i * P:(i + 1) * P] if j < LAST else PTL[0:P, h % 2, :]
                mm = pe.matmul(o_bank[h % 2][32 * i:32 * i + 32, 0:P], v[0:P, s, 32 * h:32 * h + 32], w,
                               start=(j == 0), stop=(j == LAST if i == 0 else j == LAST - 1))
            mm.then_inc(s_pv, 1)

        def fold_head(t, h):
            k = H * t + h
            pe.wait_ge(s_o, k + 1)
            pe.matmul(o_bank[h % 2][0:P, 128:160], O4[:, h % 2, :], fold[:, :], start=True,
                      stop=True).then_inc(s_fold, 1)

        def turn_agg(t):
            pe.wait_ge(s_fin, H * (t + 1))
            for k in range(KD):
                mm = pe.transpose(t_bank[1][:, k * P:(k + 1) * P], agg[0:P, k * 128:(k + 1) * 128], ident[0:P, 0:P])
            mm.then_inc(s_aggT, 1)

        def out_project(t):
            pe.wait_ge(s_aggC, t + 1)
            for k in range(KD):
                mm = pe.matmul(t_bank[2][0:P, 0:D], aggT[:, k, :], wo[:, k, :], start=(k == 0), stop=(k == KD - 1))
            mm.then_inc(s_wo, 1)

        def tile(t, first=False, last=False):
            for h in range(H):
                for j in range(LAST + 1):
                    if w_out is not None and not first and h == 2 and j == 2:
                        pe.wait_ge(s_res, t)
                    turn(t, h, j, first and h == 0)
                    if not (last and h >= H - 2):
                        scores(*behind(t, h, 2), j)
                    if j >= 2:
                        weigh(t, h, j - 2, first)
                    elif not (first and h == 0):
                        weigh(*before(t, h), LAST - 1 + j, first)
                    if j == 3 and not (first and h == 0):
                        fold_head(*before(t, h))
                    if w_out is not None and not first:
                        if h == 1 and j == LAST:
                            copied(t, h, 4)
                            turn_agg(t - 1)
                        if h == 2 and j == 0:
                            copied(t, 1, 5)
                            out_project(t - 1)

        for h in range(2):
            for j in range(LAST + 1):
                scores(0, h, j, h == 0)
        tile(0, first=True)
        with pe.Fori(1, T - 1) as t:
            tile(t)
        tile(T - 1, last=True)
        for j in (LAST - 1, LAST):
            weigh(T - 1, H - 1, j, False)
        fold_head(T - 1, H - 1)
        if w_out is not None:
            turn_agg(T - 1)
            out_project(T - 1)

    def vector(dve):
        def flag(n, i):
            lo, hi = EXP_COLS[i // 2]
            if i % 2 == 0:
                dve.wait_ge(c_sum, 3 * n + i // 2 + 1)
                dve.tensor_scalar(C[:, 1, lo:hi], C[:, 0, lo:hi], 0.5, FAR, ALU.is_lt, ALU.mult).then_inc(c_flag, 1)
            else:
                dve.tensor_scalar(C[:, 0, lo:hi], C[:, 0, lo:hi], 1.0, None, ALU.max).then_inc(c_flag, 1)

        def reduce_piece(t, h, i):
            k = H * t + h
            lo, hi = pieces[i]
            if i == 0 and not (isinstance(t, int) and k < slots):
                dve.wait_ge(s_turn, 7 * (k - slots + 1))
            if h == 0:
                for b in b_need.get(i, ()):
                    dve.wait_ge(b_in[b], 32 * (t + 1))
            if dot:
                wait_apart(dve, s_qk, NC * k + i + 1, s_passed)
                src = s_bank[i % 3][0:P, 0:hi - lo]
            else:
                if i == 0:
                    dve.wait_ge(s_fifth, k + 1)
                src = T5[:, h % 2, lo:hi]
                dve.scalar_tensor_tensor(out=src, in0=nas[0:P, h, lo:hi], scalar=nad[0:P, bass.ds(t * H + h, 1)],
                                         in1=src, op0=ALU.add, op1=ALU.min).then_inc(s_row, 1)
                wait_apart(dve, s_row, NC * k + i + 1, s_passed)
            dve.tensor_tensor_reduce(S[:, h % slots, lo:hi], src, B[:, lo:hi], 1.0, EMPTY, ALU.add, ALU.min,
                                     low[:, h, i:i + 1]).then_inc(s_red, 1)

        def reduce_all(t, h):
            k = H * t + h
            dve.wait_ge(s_red, NC * (k + 1))
            dve.tensor_reduce(least[:, h:h + 1], low[:, h, :], AX.X, ALU.min).then_inc(s_least, 1)

        def copy_out(t, h, j):
            k = H * t + h
            dve.wait_ge(s_turn, 7 * k + j + 1)
            if j >= 3:
                dve.wait_ge(s_pv, 7 * k + j - 2)
            elif not (isinstance(t, int) and k == 0):
                dve.wait_ge(s_pv, 7 * (k - 1) + j + 4)
            n = len(GROUPS[j]) * P
            dve.tensor_copy(PT[:, j % 3, 0:n], t_bank[j % 3][0:P, 0:n]).then_inc(s_evD, 1)

        def row_sum(t, h, part):
            k = H * t + h
            if part == 0:
                dve.wait_ge(s_exp, NE * (k + 1))
                dve.tensor_reduce(rz[:, 0, h:h + 1], z[:, h, :], AX.X, ALU.add).then_inc(s_small, 1)
            elif part == 1:
                dve.wait_ge(s_small, 3 * k + 1)
                dve.tensor_scalar(rz[:, 1, h:h + 1], rz[:, 0, h:h + 1], add_eps if add_eps else 1e-16, None,
                                  ALU.add if add_eps else ALU.max).then_inc(s_small, 1)
            else:
                dve.wait_ge(s_small, 3 * k + 2)
                dve.reciprocal(rz[:, 2, h:h + 1], rz[:, 1, h:h + 1]).then_inc(s_small, 1)

        def finish(t, h):
            k = H * t + h
            dve.wait_ge(s_small, 3 * k + 3)
            dve.wait_ge(s_fold, k + 1)
            if h == 0 and w_out is not None and not (isinstance(t, int) and t == 0):
                dve.wait_ge(s_aggT, t)
            dve.tensor_scalar(agg[:, width * h:width * (h + 1)], o_bank[h % 2][0:P, 128:128 + width],
                              rz[:, 2, h:h + 1], None, ALU.mult).then_inc(s_fin, 1)

        def residual(t):
            row = resid[0:P, bass.ds(t, 1), 0:H * width].rearrange("p o n -> p (o n)")
            if w_out is not None:
                dve.wait_ge(s_wo, t + 1)
                dve.tensor_tensor(row, row, t_bank[2][0:P, 0:D], ALU.add).then_inc(s_res, 1)
                return
            dve.wait_ge(s_fin, H * (t + 1))
            if dot:
                dve.tensor_tensor(row, row, agg[:, :], ALU.add).then_inc(s_res, 1)
            else:
                dve.tensor_copy(row, agg[:, :]).then_inc(s_res, 1)

        def tile(t, first=False, last=False):
            for h in range(H):
                more = not (last and h >= H - 2)
                done = not (first and h == 0)
                if w_out is None and h == 1 and not first:
                    residual(t - 1)
                for j in range(LAST + 1):
                    if w_out is not None and h == 2 and j == 1 and not first:
                        residual(t - 1)
                    if more and dot:
                        reduce_piece(*behind(t, h, 2), j)
                    elif more and j in (0, 2, 4):
                        reduce_piece(*behind(t, h, 2), j // 2)
                    if counts and not last and (h, j) in FLAGS_AT:
                        flag(t + 1, FLAGS_AT.index((h, j)))
                    if j in on_dve:
                        copy_out(t, h, j)
                    if j in (0, 2, 4) and done:
                        row_sum(*before(t, h), j // 2)
                if more:
                    reduce_all(*behind(t, h, 2))
                if done:
                    finish(*before(t, h))

        if counts:
            for i in range(6):
                flag(0, i)
        for h in range(2):
            for i in range(NC):
                reduce_piece(0, h, i)
            reduce_all(0, h)
        tile(0, first=True)
        with dve.Fori(1, T - 1) as t:
            tile(t)
        tile(T - 1, last=True)
        for part in range(3):
            row_sum(T - 1, H - 1, part)
        finish(T - 1, H - 1)
        residual(T - 1)
        dve.wait_ge(s_res, T)

    def scalar(act):
        def logs(n):
            act.wait_ge(c_flag, 6 * (n + 1))
            act.activation(C[:, 0, :], C[:, 0, :], ACT.Ln).then_inc(c_log, 1)

        def weights(t, h, i):
            k = H * t + h
            lo, hi = EXP_COLS[i]
            if i == 0:
                act.wait_ge(s_least, k + 1)
            act.activation(S[:, h % slots, lo:hi], S[:, h % slots, lo:hi], ACT.Exp, bias=least[:, h:h + 1], scale=-1.0,
                           accum_out=z[:, h, i:i + 1]).then_inc(s_exp, 1)

        def copy_out(t, h, j):
            k = H * t + h
            act.wait_ge(s_turn, 7 * k + j + 1)
            if j == LAST:
                if not (isinstance(t, int) and k < 2):
                    act.wait_ge(s_pv, 7 * (k - 1))
                act.copy(PTL[:, h % 2, :], t_bank[j % 3][0:P, 0:P]).then_inc(s_evA, 1)
                return
            if j >= 3:
                act.wait_ge(s_pv, 7 * k + j - 2)
            elif not (isinstance(t, int) and k == 0):
                act.wait_ge(s_pv, 7 * (k - 1) + j + 4)
            n = len(GROUPS[j]) * P
            act.copy(PT[:, j % 3, 0:n], t_bank[j % 3][0:P, 0:n]).then_inc(s_evA, 1)

        def sums_out(t, h):
            k = H * t + h
            act.wait_ge(s_pv, 7 * (k + 1))
            if not (isinstance(t, int) and k < 2):
                act.wait_ge(s_fold, k - 1)
            act.copy(O4[:, h % 2, :], o_bank[h % 2][:, 0:P]).then_inc(s_o, 1)

        def agg_out(t):
            act.wait_ge(s_aggT, t + 1)
            act.copy(aggT[:, :, :], t_bank[1][:, 0:KD * P].rearrange("p (k n) -> p k n", k=KD)).then_inc(s_aggC, 1)

        def tile(t, first=False, last=False):
            for h in range(H):
                for j in range(LAST + 1):
                    if j in on_act:
                        copy_out(t, h, j)
                    if w_out is not None and h == 1 and j == LAST and not first:
                        agg_out(t - 1)
                    if j in EXP_AT and not (last and h == H - 1):
                        weights(*behind(t, h, 1), EXP_AT.index(j))
                    if j == 2 and not (first and h == 0):
                        sums_out(*before(t, h))
                    if counts and not last and (h, j) == LOG_AT:
                        logs(t + 1)

        if counts:
            logs(0)
        for i in range(NE):
            weights(0, 0, i)
        tile(0, first=True)
        with act.Fori(1, T - 1) as t:
            tile(t)
        tile(T - 1, last=True)
        sums_out(T - 1, H - 1)
        if w_out is not None:
            agg_out(T - 1)

    def make_bias(pool):
        def tile(n):
            wait_apart(pool, c_in, 64 * (n + 1), c_went)
            for lo, hi in EXP_COLS:
                pool.tensor_tensor(C[:, 0, lo:hi], C[:, 0, lo:hi], C[:, 1, lo:hi], ALU.add).then_inc(c_sum, 1)
            wait_apart(pool, c_log, n + 1, c_went)
            for lo, hi in EXP_COLS:
                pool.tensor_tensor(C[:, 1, lo:hi], C[:, 1, lo:hi], C[:, 0, lo:hi], ALU.subtract).then_inc(c_bias, 1)

        peeled(pool, T, tile)

    def router_scores(pool):
        def fifth(t, h):
            k = H * t + h
            if h == 0:
                if not (isinstance(t, int) and t == 0):
                    pool.wait_ge(s_fifth, k)
                pool.tensor_copy(row[:, :], nad[0:P, bass.ds(t * H, H)]).then_inc(s_sum, 1)
                wait_apart(pool, s_sum, t + 1, s_went)
            if not (isinstance(t, int) and k < 2):
                wait_apart(pool, s_red, NC * (k - 1), s_went)
            pool.tensor_scalar(T5[:, h % 2, :], nas[0:P, h, :], row[:, h:h + 1], 0.2, ALU.add,
                               ALU.mult).then_inc(s_fifth, 1)

        for h in range(H):
            fifth(0, h)
        with pool.Fori(1, T) as t:
            for h in range(H):
                fifth(t, h)

    phase = dict(sync=sync, tensor=tensor, vector=vector, scalar=scalar)
    if counts:
        phase["gpsimd"] = make_bias
    if not dot:
        phase["gpsimd"] = router_scores
    return phase


def stage_rows(pool, g, h, hs, turned, staged):
    wait_from(pool, turned, 4 * g)
    for j in range(GT):
        pool.tensor_copy(hs[:, j, :], h[:, bass.ds(g * GT + j, 1), :].rearrange("p o n -> p (o n)")).then_inc(staged, 1)


def turned_out(act, g, ht, bank, turned, ht_ok):
    for k in range(KD):
        for s, (lo, hi) in enumerate(SPLIT):
            act.wait_ge(turned, 4 * g + 2 * k + s + 1)
            act.copy(ht[:, k, lo:hi], bank[2 * k + s][:, 0:hi - lo]).then_inc(ht_ok, 1)


def ffn_phase(nc, c, ctx, tag, h, x, w1, b1, w2, b2, func, experts, hidden, gate, ident, bank):
    E, M = experts, hidden // 128
    w1s = sb(nc, ctx, f"w1{tag}", [128, KD, E, hidden])
    w2s = sb(nc, ctx, f"w2{tag}", [128, E, M, D])
    b1s = sb(nc, ctx, f"b1{tag}", [128, E, M])
    b2s = sb(nc, ctx, f"b2{tag}", [P, E, D])
    hs = sb(nc, ctx, f"hs{tag}", [P, GT, D])
    ht = sb(nc, ctx, f"ht{tag}", [128, KD, GN])
    mid = sb(nc, ctx, f"mid{tag}", [128, M, GN])
    plus = sb(nc, ctx, f"plus{tag}", [P, 2, D])
    (win, staged, turned, ht_ok, up_mm, up_out, down_mm, down_b, down_out) = (
        c.sem(f"{v}{tag}") for v in ("f_w", "f_stage", "f_turn", "f_ht", "f_up", "f_mid", "f_down", "f_plus", "f_x"))
    U = 2 * M

    def sync(sp):
        for e in range(E):
            sp.dma_start(w1s[:, :, e, :], w1[e].rearrange("(k p) n -> p k n", p=128)).then_inc(win, 16)
            sp.dma_start(w2s[:, e, :, :], w2[e].rearrange("(m p) n -> p m n", p=128)).then_inc(win, 16)
            with nc.allow_non_contiguous_dma(reason="a bias column, once"):
                sp.dma_start(b1s[:, e, :], b1[e].rearrange("(m p) -> p m", p=128)).then_inc(win, 16)
            sp.dma_start(b2s[:, e, :], rows(b2[e], P)).then_inc(win, 16)

    def gpsimd(pool):
        def group(g):
            stage_rows(pool, g, h, hs, turned, staged)

        peeled(pool, G, group)

    def tensor(pe):
        pe.wait_ge(win, 64 * E)
        def group(g):
            pe.wait_ge(staged, GT * (g + 1))
            wait_from(pe, up_out, U * E * g)
            transpose_group(pe, hs, bank, ident, turned)
            pe.wait_ge(ht_ok, 4 * (g + 1))
            for e in range(E):
                for m in range(M):
                    for s, (lo, hi) in enumerate(SPLIT):
                        n = 2 * m + s
                        if n >= 4:
                            wait_from(pe, up_out, U * (E * g + e) + n - 3)
                        elif e:
                            wait_from(pe, up_out, U * (E * g + e) - 4 + n + 1)
                        for k in range(KD):
                            mm = pe.matmul(bank[n % 4][:, 0:hi - lo], w1s[:, k, e, m * 128:(m + 1) * 128],
                                           ht[:, k, lo:hi], start=(k == 0), stop=(k == KD - 1))
                        mm.then_inc(up_mm, 1)
                pe.wait_ge(up_out, U * (E * g + e + 1))
                for j in range(GT):
                    i = e * GT + j
                    if i >= 4:
                        wait_from(pe, down_b, E * GT * g + i - 3)
                    else:
                        wait_from(pe, down_b, E * GT * g)
                    for m in range(M):
                        mm = pe.matmul(bank[4 + i % 4][0:P, 0:D], mid[:, m, j * P:(j + 1) * P], w2s[:, e, m, :],
                                       start=(m == 0), stop=(m == M - 1))
                    mm.then_inc(down_mm, 1)

        peeled(pe, G, group)

    def scalar(act):
        act.wait_ge(win, 64 * E)
        def group(g):
            wait_from(act, up_mm, U * E * g)
            turned_out(act, g, ht, bank, turned, ht_ok)
            for e in range(E):
                wait_from(act, down_mm, GT * (E * g + e))
                for m in range(M):
                    for s, (lo, hi) in enumerate(SPLIT):
                        act.wait_ge(up_mm, U * (E * g + e) + 2 * m + s + 1)
                        act.activation(mid[:, m, lo:hi], bank[(2 * m + s) % 4][:, 0:hi - lo], func,
                                       bias=b1s[:, e, m:m + 1]).then_inc(up_out, 1)

        peeled(act, G, group)

    def vector(dve):
        dve.wait_ge(win, 64 * E)
        def group(g):
            for e in range(E):
                for j in range(GT):
                    i = e * GT + j
                    n = E * GT * g + i
                    row = x[0:P, bass.ds(g * GT + j, 1), :].rearrange("p o n -> p (o n)")
                    dve.wait_ge(down_mm, n + 1)
                    dve.tensor_tensor(plus[:, i % 2, :], bank[4 + i % 4][0:P, 0:D], b2s[:, e, :], ALU.add).then_inc(down_b, 1)
                    dve.wait_ge(down_b, n + 1)
                    if gate is None:
                        dve.tensor_tensor(row, row, plus[:, i % 2, :], ALU.add).then_inc(down_out, 1)
                    else:
                        dve.scalar_tensor_tensor(out=row, in0=plus[:, i % 2, :],
                                                 scalar=gate[0:P, bass.ds((g * GT + j) * E + e, 1)], in1=row,
                                                 op0=ALU.mult, op1=ALU.add).then_inc(down_out, 1)
                    if j == GT - 1:
                        dve.wait_ge(down_out, n + 1)

        peeled(dve, G, group)

    return dict(sync=sync, gpsimd=gpsimd, tensor=tensor, scalar=scalar, vector=vector)


SH, SG = 8, 64
SI = SH * SG
SM = SI // 128


def slice_phase(nc, c, ctx, tag, h, a, swt, token, norm, ident, ones, bank):
    wfx = sb(nc, ctx, "wfx", [128, KD, SI])
    wx = sb(nc, ctx, "wx", [128, KD, SI])
    bx = sb(nc, ctx, "bx", [128, SM])
    bfx = sb(nc, ctx, "bfx", [P, SI])
    bsl = sb(nc, ctx, "bsl", [P, SI])
    tmp = sb(nc, ctx, "tmp", [P, SH])
    rtw = sb(nc, ctx, "rtw", [P, SI])
    wsl = sb(nc, ctx, "wsl", [128, 128])
    hs = sb(nc, ctx, "hs_s", [P, GT, D])
    ht = sb(nc, ctx, "ht_s", [128, KD, GN])
    xm = sb(nc, ctx, "xm", [128, SM, GN])
    fx = sb(nc, ctx, "fx", [P, 2, SI])
    lg = sb(nc, ctx, "lg", [P, 2, SI])
    top = sb(nc, ctx, "top", [P, 2, 3, SH])
    names = ("win", "wz", "prep", "staged", "turned", "ht_ok", "xm_mm", "xm_out", "fx_mm", "fx_out", "lg_mm", "lg_out",
             "soft", "exped", "sw_ok", "tok_mm", "tok_out", "swt_mm", "swt_out")
    (win, wz, prep, staged, turned, ht_ok, xm_mm, xm_out, fx_mm, fx_out, lg_mm, lg_out, soft, exped, sw_ok, tok_mm,
     tok_out, swt_mm, swt_out) = (c.sem(f"s_{v}") for v in names)

    def sync(sp):
        sp.dma_start(wfx[:, :, :], a["L0_ffn_W_fx"].rearrange("(k p) n -> p k n", p=128)).then_inc(win, 16)
        sp.dma_start(wx[:, :, :], a["L0_ffn_W_x"].rearrange("(k p) n -> p k n", p=128)).then_inc(win, 16)
        with nc.allow_non_contiguous_dma(reason="a bias column, once"):
            sp.dma_start(bx[:, :], a["L0_ffn_b_x"].rearrange("(m p) -> p m", p=128)).then_inc(win, 16)
        sp.dma_start(bfx[:, :], rows(a["L0_ffn_b_fx"], P)).then_inc(win, 16)
        for i in range(SH):
            sp.dma_start(bsl[:, i * SG:(i + 1) * SG], rows(a["L0_ffn_b_slice"], P)).then_inc(win, 16)
        sp.dma_start(tmp[:, :], rows(a["L0_ffn_temperature"].rearrange("a h b c -> (a h b c)"), P)).then_inc(win, 16)
        sp.wait_ge(wz, 1)
        for i in range(2):
            sp.dma_start(wsl[64 * i:64 * i + 64, 64 * i:64 * i + 64], a["L0_ffn_W_slice"]).then_inc(win, 16)

    def gpsimd(pool):
        pool.memset(wsl[:, :], 0.0).then_inc(wz, 1)
        def group(g):
            stage_rows(pool, g, h, hs, turned, staged)

        peeled(pool, G, group)

    def tensor(pe):
        pe.wait_ge(win, 16 * 15)
        def group(g):
            pe.wait_ge(staged, GT * (g + 1))
            wait_from(pe, xm_out, 8 * g)
            wait_from(pe, tok_out, 2 * g)
            transpose_group(pe, hs, bank, ident, turned)
            pe.wait_ge(ht_ok, 4 * (g + 1))
            for m in range(SM):
                for s, (lo, hi) in enumerate(SPLIT):
                    n = 2 * m + s
                    if n >= 4:
                        wait_from(pe, xm_out, 8 * g + n - 3)
                    for k in range(KD):
                        mm = pe.matmul(bank[n % 4][:, 0:hi - lo], wx[:, k, m * 128:(m + 1) * 128], ht[:, k, lo:hi],
                                       start=(k == 0), stop=(k == KD - 1))
                    mm.then_inc(xm_mm, 1)

            def logits(j):
                t = GT * g + j
                wait_from(pe, fx_out, t)
                for k in range(KD):
                    mm = pe.matmul(bank[4][0:P, :], ht[:, k, j * P:(j + 1) * P], wfx[:, k, :], start=(k == 0), stop=(k == KD - 1))
                mm.then_inc(fx_mm, 1)
                wait_from(pe, lg_out, t)
                if j == 0:
                    pe.wait_ge(xm_out, 8 * (g + 1))
                for m in range(SM):
                    mm = pe.matmul(bank[5][0:P, m * 128:(m + 1) * 128], xm[:, m, j * P:(j + 1) * P], wsl[:, :],
                                   start=True, stop=True)
                mm.then_inc(lg_mm, 1)

            def tokens(j):
                t = GT * g + j
                pe.wait_ge(sw_ok, t + 1)
                for m in range(SM):
                    pe.matmul(bank[7][:, m * 128:(m + 1) * 128], lg[:, j % 2, m * 128:(m + 1) * 128],
                              fx[:, j % 2, m * 128:(m + 1) * 128], start=(j == 0 and m == 0),
                              stop=(j == GT - 1 and m == SM - 1), skip_group_check=True)
                for m in range(SM):
                    mm = pe.matmul(bank[3][:, m:m + 1], lg[:, j % 2, m * 128:(m + 1) * 128], ones[0:P, 0:1],
                                   start=(j == 0 and m == 0), stop=(j == GT - 1 and m == SM - 1), skip_group_check=True)
                mm.then_inc(tok_mm, 1)
                wait_from(pe, swt_out, t)
                for m in range(SM):
                    mm = pe.transpose(bank[6][:, m * P:(m + 1) * P], lg[0:P, j % 2, m * 128:(m + 1) * 128], ident[0:P, 0:P])
                mm.then_inc(swt_mm, 1)

            logits(0)
            for j in range(GT):
                if j + 1 < GT:
                    logits(j + 1)
                tokens(j)

        peeled(pe, G, group)

    def scalar(act):
        act.wait_ge(win, 16 * 15)
        def group(g):
            wait_from(act, fx_mm, GT * g)
            turned_out(act, g, ht, bank, turned, ht_ok)
            wait_from(act, lg_mm, GT * g)
            for m in range(SM):
                for s, (lo, hi) in enumerate(SPLIT):
                    n = 2 * m + s
                    act.wait_ge(xm_mm, 8 * g + n + 1)
                    act.activation(xm[:, m, lo:hi], bank[n % 4][:, 0:hi - lo], ACT.Identity,
                                   bias=bx[:, m:m + 1]).then_inc(xm_out, 1)
            for j in range(GT):
                t = GT * g + j
                act.wait_ge(soft, 3 * t + 2)
                act.activation(lg[:, j % 2, :], lg[:, j % 2, :], ACT.Exp).then_inc(exped, 1)
                if j >= 1:
                    wait_from(act, swt_mm, t)
                    act.copy(swt[:, :, bass.ds((t - 1) * P, P)], bank[6][:, 0:SM * P].rearrange("p (m n) -> p m n", m=SM)).then_inc(swt_out, 1)
            act.wait_ge(swt_mm, GT * g + GT)
            act.copy(swt[:, :, bass.ds((GT * g + GT - 1) * P, P)],
                     bank[6][:, 0:SM * P].rearrange("p (m n) -> p m n", m=SM)).then_inc(swt_out, 1)

        peeled(act, G, group)

    def vector(dve):
        def heads(ap):
            return ap.rearrange("p (h g) -> p h g", h=SH)

        dve.wait_ge(win, 16 * 15)
        dve.memset(token[:, :], 0.0).then_inc(prep, 1)
        dve.memset(norm[:, :], 0.0).then_inc(prep, 1)
        dve.tensor_scalar(tmp[:, :], tmp[:, :], 0.1, 5.0, ALU.max, ALU.min).then_inc(prep, 1)
        dve.wait_ge(prep, 3)
        dve.reciprocal(tmp[:, :], tmp[:, :]).then_inc(prep, 1)
        dve.wait_ge(prep, 4)
        dve.tensor_copy(heads(rtw[:, :]), tmp[:, :].unsqueeze(2).to_broadcast([P, SH, SG])).then_inc(prep, 1)
        dve.wait_ge(prep, 5)
        def group(g):
            for j in range(GT):
                t = GT * g + j
                b = j % 2
                dve.wait_ge(fx_mm, t + 1)
                if j >= 2:
                    wait_from(dve, tok_mm, t - 1)
                    wait_from(dve, swt_mm, t - 1)
                else:
                    wait_from(dve, tok_mm, GT * g)
                    wait_from(dve, swt_mm, GT * g)
                dve.tensor_tensor(fx[:, b, :], bank[4][0:P, :], bfx[:, :], ALU.add).then_inc(fx_out, 1)
                dve.wait_ge(lg_mm, t + 1)
                dve.tensor_tensor(lg[:, b, :], bank[5][0:P, :], bsl[:, :], ALU.add).then_inc(lg_out, 1)
                dve.wait_ge(lg_out, t + 1)
                dve.tensor_tensor(lg[:, b, :], lg[:, b, :], rtw[:, :], ALU.mult).then_inc(soft, 1)
                dve.wait_ge(soft, 3 * t + 1)
                dve.tensor_reduce(top[:, b, 0, :], heads(lg[:, b, :]), AX.X, ALU.max).then_inc(prep, 1)
                dve.wait_ge(prep, 5 + 3 * t + 1)
                dve.tensor_tensor(heads(lg[:, b, :]), heads(lg[:, b, :]),
                                  top[:, b, 0, :].unsqueeze(2).to_broadcast([P, SH, SG]), ALU.subtract).then_inc(soft, 1)
                dve.wait_ge(exped, t + 1)
                dve.tensor_reduce(top[:, b, 1, :], heads(lg[:, b, :]), AX.X, ALU.add).then_inc(prep, 1)
                dve.wait_ge(prep, 5 + 3 * t + 2)
                dve.reciprocal(top[:, b, 2, :], top[:, b, 1, :]).then_inc(prep, 1)
                dve.wait_ge(prep, 5 + 3 * t + 3)
                dve.tensor_tensor(heads(lg[:, b, :]), heads(lg[:, b, :]),
                                  top[:, b, 2, :].unsqueeze(2).to_broadcast([P, SH, SG]), ALU.mult).then_inc(soft, 1)
                dve.wait_ge(soft, 3 * t + 3)
                dve.sem_inc(sw_ok, 1)
            dve.wait_ge(tok_mm, GT * (g + 1))
            dve.tensor_tensor(token[:, :], token[:, :], bank[7][:, :], ALU.add).then_inc(tok_out, 1)
            dve.tensor_tensor(norm[:, :], norm[:, :], bank[3][:, 0:SM], ALU.add).then_inc(tok_out, 1)
            dve.wait_ge(tok_out, 2 * (g + 1))

        peeled(dve, G, group)

    return dict(sync=sync, gpsimd=gpsimd, tensor=tensor, scalar=scalar, vector=vector)


def token_phase(nc, c, ctx, a, token, norm, mix, ident, bank):
    block = sb(nc, ctx, "block", [128, SM, 128])
    w3 = sb(nc, ctx, "w3", [128, 3, 128])
    wo = sb(nc, ctx, "wo_s", [128, SM, D])
    tt = sb(nc, ctx, "tt", [128, SM, 128])
    qkv = sb(nc, ctx, "qkv", [128, 3, SM, 128])
    att = sb(nc, ctx, "att_s", [128, SM, SG])
    attb = sb(nc, ctx, "attb", [128, SM, 128])
    attt = sb(nc, ctx, "attt", [128, SM, 128])
    outt = sb(nc, ctx, "outt", [128, SM, 128])
    rn = sb(nc, ctx, "rn", [128, SM])
    st = sb(nc, ctx, "st_s", [128, 3, SM])
    win, wz, step, mm_ok, act_ok = (c.sem(f"t_{v}") for v in ("win", "wz", "step", "mm", "act"))
    halves = ((0, 64), (64, 128))

    def sync(sp):
        sp.wait_ge(wz, 2)
        for i, w in enumerate(("L0_ffn_W_q", "L0_ffn_W_k", "L0_ffn_W_v")):
            for lo, hi in halves:
                sp.dma_start(w3[lo:hi, i, lo:hi], a[w]).then_inc(win, 16)
        sp.dma_start(wo[:, :, :], a["L0_ffn_W_out"].rearrange("(m p) n -> p m n", p=128)).then_inc(win, 16)

    def gpsimd(pool):
        pool.memset(w3[:, :, :], 0.0).then_inc(wz, 1)
        pool.memset(block[:, :, :], 0.0).then_inc(wz, 1)

    def flat(ap):
        return ap.rearrange("p m n -> p (m n)")

    def vector(dve):
        n = [0]

        def then(ins):
            n[0] += 1
            ins.then_inc(step, 1)
            dve.wait_ge(step, n[0])

        dve.wait_ge(wz, 2)
        for lo, hi in halves:
            then(dve.memset(block[lo:hi, :, lo:hi], 1.0))
        then(dve.tensor_scalar(rn[:, :], norm[:, :], 1e-5, None, ALU.add))
        then(dve.reciprocal(rn[:, :], rn[:, :]))
        t3 = token[:, :].rearrange("p (m n) -> p m n", m=SM)
        then(dve.tensor_tensor(t3, t3, rn[:, :].unsqueeze(2).to_broadcast([128, SM, 128]), ALU.mult))
        then(dve.tensor_tensor(t3, t3, block[:, :, :], ALU.mult))
        dve.wait_ge(mm_ok, 1)
        then(dve.tensor_copy(flat(tt[:, :, :]), bank[0][:, :]))
        for i in range(3):
            dve.wait_ge(mm_ok, 2 + i)
            then(dve.tensor_copy(flat(qkv[:, i, :, :]), bank[1 + i][:, :]))
        dve.wait_ge(mm_ok, 5)
        s3 = bank[4][:, :].rearrange("p (m n) -> p m n", m=SM)
        for lo, hi in halves:
            then(dve.tensor_copy(att[lo:hi, :, :], s3[lo:hi, :, lo:hi]))
        then(dve.tensor_reduce(st[:, 0, :], att[:, :, :], AX.X, ALU.max))
        then(dve.tensor_tensor(att[:, :, :], att[:, :, :], st[:, 0, :].unsqueeze(2).to_broadcast([128, SM, SG]),
                               ALU.subtract))
        dve.wait_ge(act_ok, 1)
        then(dve.tensor_reduce(st[:, 1, :], att[:, :, :], AX.X, ALU.add))
        then(dve.reciprocal(st[:, 2, :], st[:, 1, :]))
        then(dve.tensor_tensor(att[:, :, :], att[:, :, :], st[:, 2, :].unsqueeze(2).to_broadcast([128, SM, SG]), ALU.mult))
        then(dve.memset(attb[:, :, :], 0.0))
        for lo, hi in halves:
            then(dve.tensor_copy(attb[lo:hi, :, lo:hi], att[lo:hi, :, :]))
        dve.wait_ge(mm_ok, 6)
        then(dve.tensor_copy(flat(attt[:, :, :]), bank[5][:, :]))
        dve.wait_ge(mm_ok, 7)
        then(dve.tensor_copy(flat(outt[:, :, :]), bank[6][:, :]))
        for m in range(SM):
            dve.wait_ge(mm_ok, 8 + m)
            then(dve.tensor_copy(mix[:, m, :], bank[m][:, 0:D]))

    def scalar(act):
        act.wait_ge(step, 14)
        act.activation(att[:, :, :], att[:, :, :], ACT.Exp, scale=float(SG) ** -0.5).then_inc(act_ok, 1)

    def tensor(pe):
        def four(b, lhs, rhs):
            for m in range(SM):
                mm = pe.matmul(bank[b][:, m * 128:(m + 1) * 128], lhs(m), rhs(m), start=True, stop=True)
            mm.then_inc(mm_ok, 1)

        pe.wait_ge(win, 16 * 7)
        pe.wait_ge(step, 6)
        for m in range(SM):
            mm = pe.transpose(bank[0][:, m * 128:(m + 1) * 128], token[:, m * 128:(m + 1) * 128], ident[:, :])
        mm.then_inc(mm_ok, 1)
        pe.wait_ge(step, 7)
        four(1, lambda m: w3[:, 0, :], lambda m: tt[:, m, :])
        four(2, lambda m: w3[:, 1, :], lambda m: tt[:, m, :])
        four(3, lambda m: tt[:, m, :], lambda m: w3[:, 2, :])
        pe.wait_ge(step, 10)
        four(4, lambda m: qkv[:, 0, m, :], lambda m: qkv[:, 1, m, :])
        pe.wait_ge(step, 20)
        for m in range(SM):
            mm = pe.transpose(bank[5][:, m * 128:(m + 1) * 128], attb[:, m, :], ident[:, :])
        mm.then_inc(mm_ok, 1)
        pe.wait_ge(step, 21)
        four(6, lambda m: qkv[:, 2, m, :], lambda m: attt[:, m, :])
        pe.wait_ge(step, 22)
        for m in range(SM):
            pe.matmul(bank[m][:, 0:D], outt[:, m, :], wo[:, m, :], start=True, stop=True).then_inc(mm_ok, 1)

    return dict(sync=sync, gpsimd=gpsimd, tensor=tensor, scalar=scalar, vector=vector)


def spread_phase(nc, c, ctx, a, swt, mix, x, bank):
    part = sb(nc, ctx, "part_s", [128, SM, GN])
    bo = sb(nc, ctx, "bo", [P, D])
    plus = sb(nc, ctx, "plus_s", [P, 2, D])
    win, staged, mm_ok, added, out = (c.sem(f"o_{v}") for v in ("win", "stage", "mm", "add", "out"))

    def sync(sp):
        sp.dma_start(bo[:, :], rows(a["L0_ffn_b_out"], P)).then_inc(win, 16)

    def gpsimd(pool):
        def group(g):
            for j in range(GT):
                wait_from(pool, mm_ok, (GT * (g - 1) + j + 1))
                pool.tensor_copy(part[:, :, j * P:(j + 1) * P], swt[:, :, bass.ds(g * GN + j * P, P)]).then_inc(staged, 1)

        peeled(pool, G, group)

    def tensor(pe):
        def group(g):
            for j in range(GT):
                pe.wait_ge(staged, GT * g + j + 1)
                wait_from(pe, added, GT * (g - 1) + j + 1)
                for m in range(SM):
                    mm = pe.matmul(bank[j][0:P, 0:D], part[:, m, j * P:(j + 1) * P], mix[:, m, :], start=(m == 0), stop=(m == SM - 1))
                mm.then_inc(mm_ok, 1)

        peeled(pe, G, group)

    def vector(dve):
        dve.wait_ge(win, 16)
        def group(g):
            for j in range(GT):
                n = GT * g + j
                row = x[0:P, bass.ds(n, 1), :].rearrange("p o n -> p (o n)")
                dve.wait_ge(mm_ok, n + 1)
                dve.tensor_tensor(plus[:, j % 2, :], bank[j][0:P, 0:D], bo[:, :], ALU.add).then_inc(added, 1)
                dve.wait_ge(added, n + 1)
                dve.tensor_tensor(row, row, plus[:, j % 2, :], ALU.add).then_inc(out, 1)
                dve.wait_ge(out, n + 1)

        peeled(dve, G, group)

    return dict(sync=sync, gpsimd=gpsimd, tensor=tensor, vector=vector)


RH, RE = 4, 4
RF = RH * RE


def router_phase(nc, c, ctx, h, a, vpad, nas, nad, ident, bank):
    wg = sb(nc, ctx, "wg", [128, KD, RF])
    asrc = sb(nc, ctx, "asrc", [RF, 1])
    spread = sb(nc, ctx, "spread_r", [RF, RH, 128])
    adst = sb(nc, ctx, "adst", [P, RF])
    hs = sb(nc, ctx, "hs_r", [P, GT, D])
    ht = sb(nc, ctx, "ht_r", [128, KD, GN])
    hg = sb(nc, ctx, "hg", [RF, GN])
    prod = sb(nc, ctx, "prod_r", [P, T * RF])
    win, prep, masked, staged, turned, ht_ok, hg_mm, hg_out, row_mm, row_out, v_mm, v_out, fin = (
        c.sem(f"r_{v}") for v in ("win", "prep", "mask", "stage", "turn", "ht", "hgm", "hgo", "rowm", "rowo", "vm", "vo", "fin"))

    def sync(sp):
        sp.dma_start(wg[:, :, :], a["L1_ffn_W_gat"].rearrange("(k p) n -> p k n", p=128)).then_inc(win, 16)
        with nc.allow_non_contiguous_dma(reason="16 values, once"):
            sp.dma_start(asrc[:, :], a["L1_ffn_att_src"].rearrange("h (e o) -> (h e) o", o=1)).then_inc(win, 16)
        sp.dma_start(adst[:, :], rows(a["L1_ffn_att_dst"].rearrange("h e -> (h e)"), P)).then_inc(win, 16)

    def gpsimd(pool):
        pool.wait_ge(prep, 1)
        for hd in range(RH):
            pool.affine_select(out=spread[:, hd, :], in_=spread[:, hd, :], compare_op=ALU.is_ge, fill=0.0,
                               base=-RE * hd, pattern=[[0, 128]], channel_multiplier=1).then_inc(masked, 1)
            pool.wait_ge(masked, 2 * hd + 1)
            pool.affine_select(out=spread[:, hd, :], in_=spread[:, hd, :], compare_op=ALU.is_ge, fill=0.0,
                               base=RE * hd + RE - 1, pattern=[[0, 128]], channel_multiplier=-1).then_inc(masked, 1)
        def group(g):
            stage_rows(pool, g, h, hs, turned, staged)

        peeled(pool, G, group)

    def tensor(pe):
        pe.wait_ge(win, 48)
        pe.wait_ge(masked, 2 * RH)
        def group(g):
            pe.wait_ge(staged, GT * (g + 1))
            wait_from(pe, hg_out, 2 * g)
            wait_from(pe, row_out, 2 * RH * g)
            transpose_group(pe, hs, bank, ident, turned)
            pe.wait_ge(ht_ok, 4 * (g + 1))
            for s, (lo, hi) in enumerate(SPLIT):
                for k in range(KD):
                    mm = pe.matmul(bank[s][0:RF, 0:hi - lo], wg[:, k, :], ht[:, k, lo:hi], start=(k == 0), stop=(k == KD - 1))
                mm.then_inc(hg_mm, 1)
            for j in range(GT):
                wait_from(pe, v_out, GT * g + j - 3 if j >= 4 else GT * g)
                for k in range(KD):
                    mm = pe.matmul(bank[4 + j % 4][0:P, 0:RF], ht[:, k, j * P:(j + 1) * P], wg[:, k, :], start=(k == 0), stop=(k == KD - 1))
                mm.then_inc(v_mm, 1)
            pe.wait_ge(hg_out, 2 * (g + 1))
            for hd in range(RH):
                for s, (lo, hi) in enumerate(SPLIT):
                    n = 2 * hd + s
                    if n >= 4:
                        wait_from(pe, row_out, 2 * RH * g + n - 3)
                    pe.matmul(bank[n % 4][:, 0:hi - lo], spread[:, hd, :], hg[:, lo:hi], start=True, stop=True).then_inc(row_mm, 1)

        peeled(pe, G, group)

    def scalar(act):
        def group(g):
            wait_from(act, v_mm, GT * g)
            turned_out(act, g, ht, bank, turned, ht_ok)
            wait_from(act, row_mm, 2 * RH * g)
            for s, (lo, hi) in enumerate(SPLIT):
                act.wait_ge(hg_mm, 2 * g + s + 1)
                act.copy(hg[:, lo:hi], bank[s][0:RF, 0:hi - lo]).then_inc(hg_out, 1)
            for hd in range(RH):
                for s, (lo, hi) in enumerate(SPLIT):
                    n = 2 * hd + s
                    act.wait_ge(row_mm, 2 * RH * g + n + 1)
                    act.copy(nas[:, hd, bass.ds(g * GN + lo, hi - lo)], bank[n % 4][:, 0:hi - lo]).then_inc(row_out, 1)

        peeled(act, G, group)

    def vector(dve):
        dve.wait_ge(win, 48)
        dve.tensor_scalar(spread[:, :, :].rearrange("p h n -> p (h n)"), asrc[:, 0:1].to_broadcast([RF, RH * 128]), -1.0,
                          None, ALU.mult).then_inc(prep, 1)
        dve.memset(vpad[:, :, :, :], 0.0).then_inc(fin, 1)
        dve.wait_ge(fin, 1)
        def group(g):
            for j in range(GT):
                dve.wait_ge(v_mm, GT * g + j + 1)
                dve.tensor_copy(vpad[:, bass.ds(g * GT + j, 1), :, 0:RE].rearrange("p o h e -> p (o h) e"),
                                bank[4 + j % 4][0:P, 0:RF].rearrange("p (h e) -> p h e", h=RH)).then_inc(v_out, 1)

        peeled(dve, G, group)
        dve.wait_ge(v_out, T)
        p3 = prod[:, :].rearrange("p (t h e) -> p t h e", t=T, h=RH)
        for hd in range(RH):
            dve.tensor_tensor(p3[:, :, hd, :], vpad[:, :, hd, 0:RE],
                              adst[:, hd * RE:(hd + 1) * RE].unsqueeze(1).to_broadcast([P, T, RE]), ALU.mult).then_inc(fin, 1)
        dve.wait_ge(fin, 1 + RH)
        dve.tensor_reduce(nad[:, :], prod[:, :].rearrange("p (n e) -> p n e", e=RE), AX.X, ALU.add, negate=True).then_inc(fin, 1)
        dve.wait_ge(fin, 2 + RH)

    return dict(sync=sync, gpsimd=gpsimd, tensor=tensor, scalar=scalar, vector=vector)


def gate_phase(nc, c, ctx, a, agg, gate):
    vec = sb(nc, ctx, "vec_g", [P, 3, RF])
    sq = sb(nc, ctx, "sq_g", [P, T, RF])
    st = sb(nc, ctx, "st_g", [P, 4, T])
    s = sb(nc, ctx, "s_g", [P, T, RE])
    ex = sb(nc, ctx, "ex_g", [P, T, RE])
    rank = sb(nc, ctx, "rank_g", [P, T, RE])
    more = sb(nc, ctx, "more_g", [P, T])
    win, step, act_ok = c.sem("g_win"), c.sem("g_step"), c.sem("g_act")

    def sync(sp):
        for i, v in enumerate(("L1_ffn_b_gat", "L1_ffn_ln_gamma", "L1_ffn_ln_beta")):
            sp.dma_start(vec[:, i, :], rows(a[v], P)).then_inc(win, 16)

    def vector(dve):
        n = [0]

        def then(ins):
            n[0] += 1
            ins.then_inc(step, 1)
            dve.wait_ge(step, n[0])

        def row(i):
            return vec[:, i, :].unsqueeze(1).to_broadcast([P, T, RF])

        def col(i, w):
            return st[:, i, :].unsqueeze(2).to_broadcast([P, T, w])

        dve.wait_ge(win, 48)
        x = agg[:, :, :]
        then(dve.tensor_tensor(x, x, row(0), ALU.add))
        then(dve.tensor_reduce(st[:, 0, :], x, AX.X, ALU.add))
        then(dve.tensor_scalar(st[:, 0, :], st[:, 0, :], 1.0 / RF, None, ALU.mult))
        then(dve.tensor_tensor(x, x, col(0, RF), ALU.subtract))
        then(dve.tensor_tensor(sq[:, :, :], x, x, ALU.mult))
        then(dve.tensor_reduce(st[:, 1, :], sq[:, :, :], AX.X, ALU.add))
        then(dve.tensor_scalar(st[:, 1, :], st[:, 1, :], 1.0 / RF, LN_EPS, ALU.mult, ALU.add))
        dve.wait_ge(act_ok, 1)
        then(dve.reciprocal(st[:, 2, :], st[:, 2, :]))
        then(dve.tensor_tensor(x, x, col(2, RF), ALU.mult))
        then(dve.tensor_tensor(x, x, row(1), ALU.mult))
        then(dve.tensor_tensor(x, x, row(2), ALU.add))
        then(dve.tensor_reduce(s[:, :, :], agg[:, :, :].rearrange("p t (h e) -> p t e h", h=RH), AX.X, ALU.add))
        then(dve.tensor_scalar(s[:, :, :], s[:, :, :], 1.0 / RH, None, ALU.mult))
        for e in range(RE):
            first = True
            for j in range(RE):
                if j == e:
                    continue
                op = ALU.is_ge if j < e else ALU.is_gt
                if first:
                    then(dve.tensor_tensor(rank[:, :, e], s[:, :, j], s[:, :, e], op))
                    first = False
                else:
                    then(dve.tensor_tensor(more[:, :], s[:, :, j], s[:, :, e], op))
                    then(dve.tensor_tensor(rank[:, :, e], rank[:, :, e], more[:, :], ALU.add))
        then(dve.tensor_scalar(rank[:, :, :], rank[:, :, :], 2.0, None, ALU.is_lt))
        then(dve.tensor_reduce(st[:, 3, :], s[:, :, :], AX.X, ALU.max))
        then(dve.tensor_tensor(s[:, :, :], s[:, :, :], col(3, RE), ALU.subtract))
        dve.wait_ge(act_ok, 2)
        then(dve.tensor_tensor(ex[:, :, :], ex[:, :, :], rank[:, :, :], ALU.mult))
        then(dve.tensor_reduce(st[:, 0, :], ex[:, :, :], AX.X, ALU.add))
        then(dve.reciprocal(st[:, 1, :], st[:, 0, :]))
        then(dve.tensor_tensor(gate[:, :].rearrange("p (t e) -> p t e", t=T), ex[:, :, :], col(1, RE), ALU.mult))

    def scalar(act):
        act.wait_ge(step, 7)
        act.activation(st[:, 2, :], st[:, 1, :], ACT.Sqrt).then_inc(act_ok, 1)
        act.wait_ge(step, 13 + RE * (1 + 2 * (RE - 2)) + 3)
        act.activation(ex[:, :, :], s[:, :, :], ACT.Exp).then_inc(act_ok, 1)

    return dict(sync=sync, vector=vector, scalar=scalar)


def program(nc, a, out):
    ctx = ExitStack()
    with ctx:
        c = Chip(nc, ctx)
        bank = [ps(nc, ctx, f"bank{i}", [128, 512])[:, :] for i in range(8)]
        ident = sb(nc, ctx, "ident", [128, 128])
        fold = sb(nc, ctx, "fold", [128, 32])
        X = sb(nc, ctx, "X", [P, T, D])
        early = ctx.enter_context(ExitStack())
        ones = sb(nc, early, "ones", [128, 128])
        col1, col2 = len_cols(a["src"], P), len_cols2(a["L1_ffn_edge_index"], 128)
        wide1, wide2 = round_up(col1), round_up(col2)
        idx1 = sb(nc, early, "idx1", [P, wide1], I32)
        val1 = sb(nc, early, "val1", [P, wide1])
        idx2 = sb(nc, early, "idx2", [128, wide2], I32)
        val2 = sb(nc, early, "val2", [128, wide2])
        mats = [nc.dram_tensor(f"count{i}", [CELLS, 1], F32, kind="Internal").ap() for i in range(3)]
        feat = [[nc.dram_tensor(f"feat{s}{p}", [D, N], F16, kind="Internal").ap() for p in range(2)] for s in range(2)]
        x_in = c.sem("x_in")

        def load_x(sp):
            for r0, r1 in DMA_ROWS:
                sp.dma_start(X[r0:r1, :, :], a["x"].rearrange("(t p) d -> p t d", p=P)[r0:r1]).then_inc(x_in, 16)
            sp.wait_ge(x_in, 32)

        run_block(nc, c, setup_phase(c, ident, ones, fold), dict(sync=load_x))

        def attend(tag, V, resid, w_out, add_eps, counts=None, side=None):
            with ExitStack() as e:
                att = attention_phase(nc, c, e, tag, 8, 32, feat, None, mats[0], V, resid, w_out, add_eps,
                                      ident, fold, bank, counts)
                run_block(nc, c, att, *(side(e) if side else []))

        with ExitStack() as g:
            V = sb(nc, g, "values0", [P, T, D])
            with ExitStack() as e:
                H = sb(nc, e, "H0", [P, T, D])
                zero = sb(nc, e, "zero", [128, N])
                clear, cleared = clear_phase(c, mats, zero, ident, mats[2])
                e1, chosen1 = edges_phase(nc, c, e, "_m", a["src"], a["dst"], P, col1, idx1, val1, ident, ones, bank[4:6])
                e2, _ = edges_phase(nc, c, e, "_g", a["L1_ffn_edge_index"][0], a["L1_ffn_edge_index"][1], 128, col2,
                                    idx2, val2, ident, ones, bank[6:8])
                sc1 = scatter_phase(nc, c, e, "_m", mats[0:2], P, col1, idx1, val1, cleared[0:2], chosen1)
                nrm, ready = norm_phase(nc, c, e, "0", X, H, V, shared=False)
                prj = project_phase(nc, c, e, "0", H, a["L0_gnn_Wk"], a["L0_gnn_Wq"], a["L0_gnn_Wv"],
                                    (a["L0_gnn_bk"], a["L0_gnn_bq"], a["L0_gnn_bv"]), -32 ** -0.5, feat, V, ident, bank,
                                    ready=ready, stager="scalar")
                run_block(nc, c, dict(sync=e1["sync"]), dict(sync=e2["sync"]), clear,
                          dict(gpsimd=e1["gpsimd"]), dict(gpsimd=e2["gpsimd"]),
                          dict(tensor=e1["tensor"], vector=e1["vector"]),
                          dict(tensor=e2["tensor"], vector=e2["vector"]), sc1, nrm, prj)
            attend("0", V, X, None, None, counts=mats[0:2])

        with ExitStack() as g:
            swt = sb(nc, g, "swt", [128, SM, N])
            mix = sb(nc, g, "mix", [128, SM, D])
            with ExitStack() as e:
                token = sb(nc, e, "token", [128, SI])
                norm = sb(nc, e, "norm", [128, SM])
                with ExitStack() as f:
                    H = sb(nc, f, "Hs", [P, T, D])
                    with ExitStack() as f2:
                        run_block(nc, c, norm_phase(nc, c, f2, "s", X, H, sb(nc, f2, "scr_s", [P, T, D]))[0])
                    run_block(nc, c, slice_phase(nc, c, f, "s", H, a, swt, token, norm, ident, ones, bank))
                with ExitStack() as f:
                    run_block(nc, c, token_phase(nc, c, f, a, token, norm, mix, ident, bank))
            with ExitStack() as e:
                run_block(nc, c, spread_phase(nc, c, e, a, swt, mix, X, bank))

        with ExitStack() as g:
            H = sb(nc, g, "H1", [P, T, D])
            with ExitStack() as e:
                run_block(nc, c, norm_phase(nc, c, e, "h", X, H, sb(nc, e, "scr_h", [P, T, D]))[0])

            def scatter_router(e):
                return [scatter_phase(nc, c, e, "_g", mats[2:3], 128, col2, idx2, val2, (), None)]

            for l in range(2):
                with ExitStack() as e:
                    V = sb(nc, e, f"values{l + 1}", [P, T, D])
                    with ExitStack() as f:
                        run_block(nc, c, project_phase(nc, c, f, f"{l + 1}", H, a["L1_gnn_Wq"][l], a["L1_gnn_Wk"][l],
                                                       a["L1_gnn_Wv"][l], None, -32 ** -0.5, feat, V, ident, bank))
                    attend(f"{l + 1}", V, H, a["L1_gnn_Wo"][l], 1e-9,
                           side=scatter_router if l == 0 else None)
                with ExitStack() as e:
                    run_block(nc, c, norm_phase(nc, c, e, f"n{l}", H, H, sb(nc, e, f"scr_n{l}", [P, T, D]),
                                                a["L1_gnn_ln_g"][l], a["L1_gnn_ln_b"][l])[0])
            with ExitStack() as e:
                def one(v):
                    return v.rearrange("(o a) b -> o a b", o=1) if len(v.shape) == 2 else v.rearrange("(o a) -> o a", o=1)
                run_block(nc, c, ffn_phase(nc, c, e, "_d", H, X, one(a["L1_gnn_w1"]), one(a["L1_gnn_b1"]), one(a["L1_gnn_w2"]),
                                        one(a["L1_gnn_b2"]), ACT.Relu, 1, 1024, None, ident, bank))

        early.close()

        with ExitStack() as g:
            gate = sb(nc, g, "gate", [P, T * RE])
            agg = sb(nc, g, "agg_r", [P, T, RF])
            with ExitStack() as e:
                run_block(nc, c, bias_phase(nc, c, e, "_g", mats[2]))
            with ExitStack() as e:
                vpad = sb(nc, e, "vpad", [P, T, RH, 32])
                nas = sb(nc, e, "nas", [128, RH, N])
                nad = sb(nc, e, "nad", [P, T * RH])
                with ExitStack() as f:
                    H = sb(nc, f, "H2", [P, T, D])
                    with ExitStack() as f2:
                        run_block(nc, c, norm_phase(nc, c, f2, "r", X, H, sb(nc, f2, "scr_r", [P, T, D]))[0])
                    run_block(nc, c, router_phase(nc, c, f, H, a, vpad, nas, nad, ident, bank))
                with ExitStack() as f:
                    vv = vpad[:, :, :, :].rearrange("p t h e -> p t (h e)")
                    run_block(nc, c, attention_phase(nc, c, f, "r", RH, RE, None, (nas, nad), mats[2], vv, agg,
                                                  None, 1e-16, ident, fold, bank))
                with ExitStack() as f:
                    run_block(nc, c, gate_phase(nc, c, f, a, agg, gate))
            with ExitStack() as e:
                H = sb(nc, e, "H3", [P, T, D])
                with ExitStack() as f:
                    run_block(nc, c, norm_phase(nc, c, f, "x", X, H, sb(nc, f, "scr_x", [P, T, D]))[0])
                run_block(nc, c, ffn_phase(nc, c, e, "_x", H, X, a["L1_ffn_W1"], a["L1_ffn_b1"], a["L1_ffn_W2"],
                                        a["L1_ffn_b2"], ACT.Gelu, RE, 512, gate, ident, bank))
        store(nc, c, X, out)


def len_cols(v, lanes):
    return v.shape[0] // lanes


def len_cols2(v, lanes):
    return v.shape[1] // lanes


def store(nc, c, X, out):
    done = c.sem("done")

    def sync(sp):
        for r0, r1 in DMA_ROWS:
            sp.dma_start(out.rearrange("(t p) d -> p t d", p=P)[r0:r1], X[r0:r1, :, :]).then_inc(done, 16)
        sp.wait_ge(done, 32)

    run_block(nc, c, dict(sync=sync))


def kernel(**inputs):
    import numpy as _np
    import concourse.bacc as _bacc
    from concourse import mybir as _mybir
    from concourse.bass_utils import run_bass_kernel_spmd as _run

    nc = _bacc.Bacc("TRN2", target_bir_lowering=False, num_devices=1)
    arrays, args = {}, {}
    for name, value in inputs.items():
        array = _np.ascontiguousarray(value)
        arrays[f"in_{name}"] = array
        args[name] = nc.dram_tensor(f"in_{name}", array.shape, _mybir.dt.from_np(array.dtype), kind="ExternalInput").ap()
    out = nc.dram_tensor("out_x", (N, D), F32, kind="ExternalOutput").ap()
    program(nc, args, out)
    r = _run(nc, [arrays], core_ids=[0])
    return r.results[0]["out_x"]
```
